# Optimizing a Trainium2 kernel written in Bass

```python
import numpy as np
import jax
import jax.numpy as jnp

def _softmax(x, axis=-1):
    return jax.nn.softmax(x, axis=axis)

def _gelu(x):
    return jax.nn.gelu(x, approximate=True)

def _silu(x):
    return jax.nn.silu(x)

def _sigmoid(x):
    return jax.nn.sigmoid(x)

def _layernorm(x, axis=-1, eps=1e-05):
    m = jnp.mean(x, axis=axis, keepdims=True)
    v = jnp.var(x, axis=axis, keepdims=True)
    return (x - m) / jnp.sqrt(v + eps)

def _scatter_add(tgt, idx, src, axis=0):
    return tgt.at[idx].add(src)

def _segment_sum(src, seg, n):
    return jax.ops.segment_sum(src, seg, n)
kernel_name = 'mk_xattn_ffn_d1_seqx_r4_2231c6'

def setup_inputs(seed: int=0):
    np.random.seed(seed)
    _w = jnp.asarray

    def _rec_inputs():
        import jax
        import jax.numpy as jnp
        _rk = jax.random.key(seed)
        x = -0.000917 + 0.9994 * jax.random.normal(jax.random.fold_in(_rk, 1), (16, 128, 256), jnp.float32)
        _lenS = 128 - jax.random.randint(jax.random.fold_in(_rk, 7), (16,), 0, max(1, 128 // 4) + 1, jnp.int32)
        _lenS2 = 128 - jax.random.randint(jax.random.fold_in(_rk, 8), (16,), 0, max(1, 128 // 4) + 1, jnp.int32)
        _ctx_1024P = jax.random.normal(jax.random.fold_in(_rk, 11), (16, 16, 256), jnp.float32)
        _ctx_1024c = jax.random.dirichlet(jax.random.fold_in(_rk, 511), 0.3 * jnp.ones((16,), jnp.float32), (16, 128))
        _ctx_1024t = jnp.einsum('bsk,bkd->bsd', _ctx_1024c, _ctx_1024P)
        _ctx_1024t = _ctx_1024t * jax.lax.rsqrt(jnp.mean(jnp.square(_ctx_1024t)) + 1e-12) * 0.953939
        ctx_1024 = 0.000579855 + 1.00008 * (_ctx_1024t + 0.3 * jax.random.normal(jax.random.fold_in(_rk, 611), (16, 128, 256), jnp.float32))
        _validS = jnp.arange(128)[None, :] < _lenS[:, None]
        _validS2 = jnp.arange(128)[None, :] < _lenS2[:, None]
        _causal = jnp.tril(jnp.ones((128, 128), dtype=bool))
        mask_BxSxS2_ik1 = jnp.where(jnp.broadcast_to(_validS2[:, None, :], (16, 128, 128)), 1, 0).astype(jnp.int32)
        return (x, ctx_1024, mask_BxSxS2_ik1)
    x, ctx_1024, mask_BxSxS2_ik1 = _rec_inputs()

    def _L0_xattn_setup():
        import jax, jax.numpy as jnp
        import numpy as np
        B, L, C = (2, 512, 256)
        DK, H = (64, 16)
        key = jax.random.key(seed)
        ks = jax.random.split(key, 12)

        def lin(kw, kb, out_dim, in_dim):
            w = jax.random.normal(kw, (out_dim, in_dim), jnp.float32) * (1.0 / np.sqrt(in_dim))
            b = jnp.zeros((out_dim,), jnp.float32)
            return (w, b)
        WQ_w, WQ_b = lin(ks[0], ks[1], DK * H, C)
        WK_w, WK_b = lin(ks[2], ks[3], DK * H, C)
        WV_w, WV_b = lin(ks[4], ks[5], DK * H, C)
        WO_w, WO_b = lin(ks[6], ks[7], C, DK * H)
        qx = jax.random.normal(ks[8], (B, L, C), jnp.float32)
        kx = jax.random.normal(ks[9], (B, L, C), jnp.float32)
        vx = jax.random.normal(ks[10], (B, L, C), jnp.float32)
        maskPAD = jax.random.randint(ks[11], (B, L, L), 0, 2, jnp.int32)
        return {'qx': qx, 'kx': kx, 'vx': vx, 'maskPAD': maskPAD, 'WQ_w': WQ_w, 'WQ_b': WQ_b, 'WK_w': WK_w, 'WK_b': WK_b, 'WV_w': WV_w, 'WV_b': WV_b, 'WO_w': WO_w, 'WO_b': WO_b}
    _L0_xattn_all = _L0_xattn_setup()
    _L0_xattn_in = {k: v for k, v in _L0_xattn_all.items() if k in ('WQ_w', 'WQ_b', 'WK_w', 'WK_b', 'WV_w', 'WV_b', 'WO_w', 'WO_b')}
    del _L0_xattn_all

    def _L0_ffn_setup():
        import jax, jax.numpy as jnp
        import numpy as np
        B, S, D = (2, 1024, 256)
        H = 1024
        E = 8
        K = 4
        key = jax.random.key(seed)
        kx, kr, ku, kd = jax.random.split(key, 4)
        x = jax.random.normal(kx, (B, S, D), dtype=jnp.float32)
        router_w = jax.random.normal(kr, (D, E), dtype=jnp.float32) / np.sqrt(D)
        up_w = jax.random.normal(ku, (E, D, H), dtype=jnp.float32) / np.sqrt(D)
        down_w = jax.random.normal(kd, (E, H, D), dtype=jnp.float32) / np.sqrt(H)
        return {'x': x, 'router_w': router_w, 'up_w': up_w, 'down_w': down_w}
    _L0_ffn_all = _L0_ffn_setup()
    _L0_ffn_in = {k: v for k, v in _L0_ffn_all.items() if k in ('router_w', 'up_w', 'down_w')}
    del _L0_ffn_all
    return {'x': x, 'ctx_1024': ctx_1024, 'mask_BxSxS2_ik1': mask_BxSxS2_ik1, 'L0_xattn_WQ_w': _L0_xattn_in['WQ_w'], 'L0_xattn_WQ_b': _L0_xattn_in['WQ_b'], 'L0_xattn_WK_w': _L0_xattn_in['WK_w'], 'L0_xattn_WK_b': _L0_xattn_in['WK_b'], 'L0_xattn_WV_w': _L0_xattn_in['WV_w'], 'L0_xattn_WV_b': _L0_xattn_in['WV_b'], 'L0_xattn_WO_w': _L0_xattn_in['WO_w'], 'L0_xattn_WO_b': _L0_xattn_in['WO_b'], 'L0_ffn_router_w': _L0_ffn_in['router_w'], 'L0_ffn_up_w': _L0_ffn_in['up_w'], 'L0_ffn_down_w': _L0_ffn_in['down_w']}

def reference(x, ctx_1024, mask_BxSxS2_ik1, L0_xattn_WQ_w, L0_xattn_WQ_b, L0_xattn_WK_w, L0_xattn_WK_b, L0_xattn_WV_w, L0_xattn_WV_b, L0_xattn_WO_w, L0_xattn_WO_b, L0_ffn_router_w, L0_ffn_up_w, L0_ffn_down_w):
    import jax
    import jax.numpy as jnp

    def _L0_xattn_ref(qx, kx, vx, maskPAD, WQ_w, WQ_b, WK_w, WK_b, WV_w, WV_b, WO_w, WO_b):
        import jax, jax.numpy as jnp
        import numpy as np
        B, L, C = (2, 512, 256)
        DK, H = (64, 16)
        Bq, qL, _ = qx.shape
        kvL = kx.shape[1]
        q = (qx @ WQ_w.T + WQ_b).reshape(Bq, qL, H, DK).transpose(0, 2, 1, 3)
        k = (kx @ WK_w.T + WK_b).reshape(Bq, kvL, H, DK).transpose(0, 2, 1, 3)
        v = (vx @ WV_w.T + WV_b).reshape(Bq, kvL, H, DK).transpose(0, 2, 1, 3)
        scores = jnp.einsum('bhqd,bhkd->bhqk', q, k) / np.sqrt(DK).astype(np.float32)
        scores = jnp.where((maskPAD == 0)[:, None, :, :], jnp.float32(-2 ** 15 + 1), scores)
        alpha = jax.nn.softmax(scores, axis=3)
        z = jnp.einsum('bhqk,bhkd->bhqd', alpha, v)
        z = z.transpose(0, 2, 1, 3).reshape(Bq, qL, H * DK)
        return z @ WO_w.T + WO_b

    def _L0_ffn_ref(x, router_w, up_w, down_w):
        import jax, jax.numpy as jnp
        import numpy as np
        B, S, D = (2, 1024, 256)
        H = 1024
        E = 8
        K = 4
        router_logits = jnp.einsum('bsd,de->bse', x, router_w)
        routing_weights = jax.nn.softmax(router_logits, axis=-1)
        topk_weights, topk_indices = jax.lax.top_k(routing_weights, K)
        topk_weights = topk_weights / jnp.sum(topk_weights, axis=-1, keepdims=True)
        h = jnp.einsum('bsd,edh->bseh', x, up_w)
        h = jax.nn.gelu(h)
        expert_outputs = jnp.einsum('bseh,ehd->bsed', h, down_w)
        gathered = jnp.take_along_axis(expert_outputs, topk_indices[:, :, :, None], axis=2)
        output = jnp.sum(topk_weights[:, :, :, None] * gathered, axis=2)
        return output
    x = x + _L0_xattn_ref(_layernorm(x, axis=-1), ctx_1024, ctx_1024, mask_BxSxS2_ik1, L0_xattn_WQ_w, L0_xattn_WQ_b, L0_xattn_WK_w, L0_xattn_WK_b, L0_xattn_WV_w, L0_xattn_WV_b, L0_xattn_WO_w, L0_xattn_WO_b)
    x = x + _L0_ffn_ref(_layernorm(x, axis=-1), L0_ffn_router_w, L0_ffn_up_w, L0_ffn_down_w)
    return x

_drawn_inputs = setup_inputs


def setup_inputs(seed=0):
    import zlib

    import numpy as np

    out = dict(_drawn_inputs(seed))
    spreads = {'L0_xattn_WQ_b': (0.0, 0.285),
     'L0_xattn_WK_b': (0.0, 0.8),
     'L0_xattn_WV_b': (0.0, 0.1),
     'L0_xattn_WO_b': (0.0, 0.1)}
    factors = {}
    for name, (base, spread) in spreads.items():
        noise = np.random.default_rng([zlib.crc32(name.encode()), seed]).standard_normal(out[name].shape)
        drawn = base * np.exp(spread * noise) if base else spread * noise
        out[name] = jnp.asarray(drawn.astype(out[name].dtype))
    for name, factor in factors.items():
        out[name] = (out[name] * factor).astype(out[name].dtype)
    return out
```

```python
from contextlib import ExitStack

import concourse.bass as bass
from concourse import mybir

P = 128
F32, F16, I32 = mybir.dt.float32, mybir.dt.float16, mybir.dt.int32
ALU = mybir.AluOpType
ACT = mybir.ActivationFunctionType
AX_X = mybir.AxisListType.X

BATCH, SEQ, D = 16, 128, 256
HEADS, DK = 16, 64
HD = HEADS * DK
EXPERTS, TOPK, HIDDEN = 8, 4, 1024
DC = D // P
CHUNKS = HD // P
HC = HIDDEN // P
PAIRS = BATCH // 2
HG = 4
GH = HEADS // HG
STEPS = PAIRS * HG
TOK = 2 * SEQ
TILES = EXPERTS * PAIRS
MAT = 2048
SLOTS = 4
W_SCALE = 32.0
Q_SCALE = -1.0 / (W_SCALE * DK ** 0.5)
MASKED = 1.0e30
EPS = 1e-5


def real(i, offset):
    return not isinstance(i, int) or 0 <= HG * i + offset < STEPS


def transposes(i, group):
    uses = []
    if real(i, group - 2):
        uses.append("z")
    if real(i, group - 1):
        uses += ["p0", "p1"]
    if group == 0 and real(i + 1 if isinstance(i, int) else i, 0):
        uses.append("xn")
    if group == 2 and real(i - 1 if isinstance(i, int) else i, 0):
        uses.append("x2")
    return uses


PER_TRIP = sum(len(transposes(1, g)) for g in range(HG))


def t_use(i, group, kind):
    if isinstance(i, int):
        before = 1
        for s in range(HG * i + group):
            before += len(transposes(s // HG, s % HG))
        return before + transposes(i, group).index(kind)
    return i * PER_TRIP + (t_use(1, group, kind) - PER_TRIP)


def t_bank(group, kind):
    first = 1 if kind in transposes(1, group) else 0
    return t_use(first, group, kind) % 2


def xattn_ffn(nc, x, ctx_t, mask, wq_t, wk_t, wv_t, wo_t, bq_t, bk_t, bv, bo, router, up, down, out):
    assert PER_TRIP % 2 == 0
    x_rows = x.rearrange("b s d -> s b d")
    out_rows = out.rearrange("b s d -> s b d")
    mask_rows = mask.rearrange("b q k -> q b k")
    ctx_rows = ctx_t.rearrange("(c p) t -> p c t", p=P)
    attn_mats = [w.rearrange("(c p) n -> p c n", p=P) for w in (wq_t, wk_t, wv_t, wo_t)]

    ctx = ExitStack()
    with ctx:
        def sb(name, shape, dt):
            return ctx.enter_context(nc.sbuf_tensor(name, shape, dt))

        def sem(name):
            return ctx.enter_context(nc.semaphore(name))

        rows = sb("rows", [P, BATCH, D], F32)
        x2t_hi = sb("x2t_hi", [P, DC, BATCH * SEQ], F16)
        x2t_lo = sb("x2t_lo", [P, DC, BATCH * SEQ], F16)
        ident = sb("ident", [P, P], F32)
        stage = sb("stage", [P, SLOTS, MAT], F32)
        w_hi = sb("w_hi", [P, 4, MAT], F16)
        w_lo = sb("w_lo", [P, 4, MAT], F16)
        qt_hi = sb("qt_hi", [P, CHUNKS, TOK], F16)
        qt_lo = sb("qt_lo", [P, CHUNKS, TOK], F16)
        kt_hi = sb("kt_hi", [P, CHUNKS, TOK], F16)
        kt_lo = sb("kt_lo", [P, CHUNKS, TOK], F16)
        v_hi = sb("v_hi", [P, 2, HD], F16)
        v_lo = sb("v_lo", [P, 2, HD], F16)
        xnt_hi = sb("xnt_hi", [P, DC, TOK], F16)
        xnt_lo = sb("xnt_lo", [P, DC, TOK], F16)
        ctxt = sb("ctxt", [P, DC, TOK], F32)
        ctxt_hi = sb("ctxt_hi", [P, DC, TOK], F16)
        ctxt_lo = sb("ctxt_lo", [P, DC, TOK], F16)
        proj_f = sb("proj_f", [P, 3, 512], F32)
        mask_in = sb("mask_in", [P, 2, SEQ], I32)
        penalty = sb("penalty", [P, 2, SEQ], F32)
        x_in = sb("x_in", [P, 2, D], F32)
        x2 = sb("x2", [P, 2, D], F32)
        probs = sb("probs", [P, 2, 2, GH, SEQ], F32)
        pt_hi = sb("pt_hi", [P, 2, GH, SEQ], F16)
        pt_lo = sb("pt_lo", [P, 2, GH, SEQ], F16)
        z = sb("z", [P, 2, GH, DK], F32)
        zt_hi = sb("zt_hi", [P, 2, 2, SEQ], F16)
        zt_lo = sb("zt_lo", [P, 2, 2, SEQ], F16)
        xn = sb("xn", [P, 2, D], F32)
        x2n = sb("x2n", [P, 2, D], F32)
        y_bias = sb("y_bias", [P, 2, D], F32)
        bq_raw = sb("bq_raw", [P, CHUNKS], F32)
        bq_neg = sb("bq_neg", [P, CHUNKS], F32)
        bk_col = sb("bk_col", [P, CHUNKS], F32)
        bv_row = sb("bv_row", [P, HD], F32)
        bo_row = sb("bo_row", [P, D], F32)
        low = sb("low", [P, 2, 2 * GH], F32)
        total = sb("total", [P, 2, 2 * GH], F32)
        inv = sb("inv", [P, 2 * GH], F32)
        half = sb("half", [P, 2], F32)
        bn1 = sb("bn1", [P, 2, 6], F32)
        mv1 = sb("mv1", [P, 2, 2], F32)
        ve1 = sb("ve1", [P, 2], F32)
        rs1 = sb("rs1", [P, 2], F32)
        bn2 = sb("bn2", [P, 2, 6], F32)
        mv2 = sb("mv2", [P, 2, 2], F32)
        ve2 = sb("ve2", [P, 2], F32)
        rs2 = sb("rs2", [P, 2], F32)
        e_hi = sb("e_hi", [P, 2, 2, MAT], F16)
        e_lo = sb("e_lo", [P, 2, 2, MAT], F16)
        act_f = probs[:, :, 0, :, :].rearrange("p s h k -> p s (h k)").rearrange("p s (n t) -> p s n t", n=2)
        act_hi = qt_hi[:, :, :].rearrange("p (q n) t -> p q n t", n=2)
        act_lo = qt_lo[:, :, :].rearrange("p (q n) t -> p q n t", n=2)
        rt = sb("rt", [P, DC, EXPERTS], F32)
        rt_hi = sb("rt_hi", [P, DC, EXPERTS], F16)
        rt_lo = sb("rt_lo", [P, DC, EXPERTS], F16)
        logit = sb("logit", [P, BATCH, EXPERTS], F32)
        beat = sb("beat", [P, EXPERTS, BATCH, EXPERTS], F32)
        rank = sb("rank", [P, BATCH, EXPERTS], F32)
        top = sb("top", [P, BATCH], F32)
        shifted = sb("shifted", [P, BATCH, EXPERTS], F32)
        weight = sb("weight", [P, BATCH, EXPERTS], F32)
        chosen = sb("chosen", [P, BATCH, EXPERTS], F32)
        mass = sb("mass", [P, BATCH], F32)
        gate = sb("gate", [P, BATCH, EXPERTS], F32)

        bank = [ctx.enter_context(nc.psum_tensor(f"bank{n}", [P, 512], F32)) for n in range(8)]
        proj_bank, score_bank, trans_bank, z_bank, y_bank = bank[0:2], bank[2:4], bank[4:6], bank[6], bank[7]
        up_bank, down_bank, logit_bank = bank[0:4], bank[4:6], bank[6]

        x_loaded = sem("x_loaded")
        rows_loaded = sem("rows_loaded")
        ctx_loaded = sem("ctx_loaded")
        mask_loaded = sem("mask_loaded")
        small_loaded = sem("small_loaded")
        mat_loaded = [sem(f"mat_loaded{n}") for n in range(SLOTS)]
        half_set = sem("half_set")
        ident_zero = sem("ident_zero")
        ident_ready = sem("ident_ready")
        bq_ready = sem("bq_ready")
        penalty_ready = sem("penalty_ready")
        w_hi_done = sem("w_hi_done")
        w_ready = sem("w_ready")
        e_scaled = sem("e_scaled")
        e_hi_done = sem("e_hi_done")
        e_ready = sem("e_ready")
        ctx_hi_done = sem("ctx_hi_done")
        ctx_ready = sem("ctx_ready")
        bn1_done, mv1_done, ve1_done, rs1_done, xn_done = (sem(n) for n in ("bn1_done", "mv1_done", "ve1_done", "rs1_done", "xn_done"))
        bn2_done, mv2_done, ve2_done, rs2_done, x2n_done = (sem(n) for n in ("bn2_done", "mv2_done", "ve2_done", "rs2_done", "x2n_done"))
        t_full = sem("t_full")
        t_hi_done = sem("t_hi_done")
        t_lo_done = sem("t_lo_done")
        proj_full = sem("proj_full")
        proj_read = sem("proj_read")
        proj_hi_done = sem("proj_hi_done")
        proj_ready = sem("proj_ready")
        scores_full = sem("scores_full")
        scored = sem("scored")
        exp_done = sem("exp_done")
        inv_done = sem("inv_done")
        pv_done = sem("pv_done")
        z_done = sem("z_done")
        wo_done = sem("wo_done")
        y_biased = sem("y_biased")
        x2_done = sem("x2_done")
        rows_done = sem("rows_done")
        rt_hi_done, rt_ready = sem("rt_hi_done"), sem("rt_ready")
        logits_full, logits_read = sem("logits_full"), sem("logits_read")
        gating = sem("gating")
        exped = sem("exped")
        gate_ready = sem("gate_ready")
        up_full = sem("up_full")
        gelu_hi_done = sem("gelu_hi_done")
        gelu_done = sem("gelu_done")
        act_ready = sem("act_ready")
        down_used = sem("down_used")
        down_full = sem("down_full")
        added = sem("added")
        stored = sem("stored")

        block = ctx.enter_context(nc.Block())

        def bcast(ap, shape):
            return ap.to_broadcast(shape)

        def apart(engine):
            engine.nop(nofuse=True)

        @block.sync
        def _(sp):
            sp.dma_start(x_in[:, :, :], x_rows[:, 0:2, :]).then_inc(x_loaded, 16)
            for m in range(3):
                sp.dma_start(stage[:, m, :].rearrange("p (c n) -> p c n", n=attn_mats[m].shape[2]),
                             attn_mats[m]).then_inc(mat_loaded[m], 16)
                if m == 0:
                    sp.dma_start(ctxt[:, :, :], ctx_rows[:, :, 0:TOK]).then_inc(ctx_loaded, 16)
                    sp.dma_start(bq_raw[:, :], bq_t).then_inc(small_loaded, 16)
                    sp.dma_start(bk_col[:, :], bk_t).then_inc(small_loaded, 16)
                    sp.dma_start(bv_row[:, :], bcast(bv, [P, HD])).then_inc(small_loaded, 16)
                    sp.dma_start(bo_row[:, :], bcast(bo, [P, D])).then_inc(small_loaded, 16)
                    sp.dma_start(rt[:, :, :], router.rearrange("(c p) e -> p c e", p=P)).then_inc(small_loaded, 16)
            sp.dma_start(mask_in[:, :, :], mask_rows[:, 0:2, :]).then_inc(mask_loaded, 16)
            sp.dma_start(stage[:, 3, :].rearrange("p (c n) -> p c n", n=D), attn_mats[3]).then_inc(mat_loaded[3], 16)
            sp.dma_start(rows[:, :, :], x_rows).then_inc(rows_loaded, 16)

            with sp.Fori(1, PAIRS) as pair:
                sp.wait_ge(penalty_ready, pair)
                sp.dma_start(mask_in[:, :, :], mask_rows[:, bass.ds(pair * 2, 2), :]).then_inc(mask_loaded, 16)
                sp.wait_ge(xn_done, 2 * pair)
                sp.dma_start(x_in[:, :, :], x_rows[:, bass.ds(pair * 2, 2), :]).then_inc(x_loaded, 16)
                sp.wait_ge(ctx_ready, pair)
                sp.dma_start(ctxt[:, :, :], ctx_rows[:, :, bass.ds(pair * TOK, TOK)]).then_inc(ctx_loaded, 16)

            def stage_expert(pair, parity):
                for kind, w in ((0, up), (1, down)):
                    slot = 2 * parity + kind
                    if isinstance(pair, int):
                        sp.wait_ge(w_ready, 4)
                    else:
                        sp.wait_ge(e_ready, 4 * pair + (slot - 3))
                    src = w[bass.ds(pair * 2 + parity, 1), :, :].rearrange("a (c p) n -> p (a c) n", p=P)
                    sp.dma_start(stage[:, slot, :].rearrange("p (c n) -> p c n", n=w.shape[2]),
                                 src).then_inc(mat_loaded[slot], 16)

            for parity in range(2):
                stage_expert(0, parity)
            with sp.Fori(1, EXPERTS // 2) as pair:
                for parity in range(2):
                    stage_expert(pair, parity)

            for pair in range(PAIRS):
                sp.wait_ge(added, 2 * (TILES - PAIRS + pair + 1))
                sp.dma_start(out_rows[:, 2 * pair:2 * pair + 2, :],
                             rows[:, 2 * pair:2 * pair + 2, :]).then_inc(stored, 16)
            sp.wait_ge(stored, 16 * PAIRS)

        @block.tensor
        def _(pe):
            def three(dst, left_hi, left_lo, right_hi, right_lo, first, last, check=False):
                pe.matmul(dst, left_hi, right_hi, start=first, stop=False, skip_group_check=check)
                pe.matmul(dst, left_hi, right_lo, start=False, stop=False, skip_group_check=check)
                return pe.matmul(dst, left_lo, right_hi, start=False, stop=last, skip_group_check=check)

            def scores(i, g):
                pe.wait_ge(proj_ready, 3 * (HG * i + g) + 2)
                pe.wait_ge(scored, 8 * (HG * i + g))
                for b in range(2):
                    for j in range(GH // 2):
                        c = GH // 2 * g + j
                        for half_row in range(2):
                            part = slice(DK * half_row, DK * half_row + DK)
                            tok = slice(SEQ * b, SEQ * b + SEQ)
                            last = three(score_bank[half_row][:, (2 * b + j) * SEQ:(2 * b + j + 1) * SEQ],
                                         qt_hi[part, c, tok], qt_lo[part, c, tok],
                                         kt_hi[part, c, tok], kt_lo[part, c, tok], True, True)
                last.then_inc(scores_full, 1)

            def open_t(i, g, kind):
                n = t_use(i, g, kind)
                if not isinstance(n, int) or n >= 2:
                    pe.wait_ge(t_lo_done, n - 1)
                return trans_bank[t_bank(g, kind)]

            def z_transpose(i, g):
                dst = open_t(i, g, "z")
                pe.wait_ge(z_done, HG * i + g - 1)
                for b in range(2):
                    for j in range(2):
                        last = pe.transpose(dst[:, (2 * b + j) * P:(2 * b + j + 1) * P],
                                            z[:, b, 2 * j:2 * j + 2, :].rearrange("p a d -> p (a d)"), ident[:, :])
                last.then_inc(t_full, 1)

            def p_transpose(i, g, b):
                dst = open_t(i, g, f"p{b}")
                pe.wait_ge(exp_done, 8 * (HG * i + g - 1) + 4 * b + 4)
                for j in range(GH):
                    last = pe.transpose(dst[:, j * SEQ:(j + 1) * SEQ], probs[:, (g - 1) % 2, b, j, :], ident[:, :])
                last.then_inc(t_full, 1)

            def x_transpose(dst, src):
                for b in range(2):
                    for c in range(DC):
                        last = pe.transpose(dst[:, (c * 2 + b) * P:(c * 2 + b + 1) * P],
                                            src[:, b, c * P:(c + 1) * P], ident[:, :])
                last.then_inc(t_full, 1)

            def wo(i, g):
                gg = (g - 2) % HG
                pe.wait_ge(t_lo_done, t_use(i, g, "z") + 1)
                if gg == 0:
                    if not isinstance(i, int):
                        pe.wait_ge(y_biased, i)
                    elif i > 0:
                        pe.wait_ge(y_biased, i)
                    else:
                        pe.wait_ge(w_ready, 4)
                for j in range(2):
                    c = 2 * gg + j
                    for b in range(2):
                        w = slice(c * D, (c + 1) * D)
                        last = three(y_bank[:, b * D:(b + 1) * D], zt_hi[:, b, j, :], zt_lo[:, b, j, :],
                                     w_hi[:, 3, w], w_lo[:, 3, w], c == 0 and b == 0, c == CHUNKS - 1, True)
                last.then_inc(wo_done, 1)

            def pv(i, g):
                if not isinstance(i, int) or real(i, g - 2):
                    pe.wait_ge(z_done, HG * i + g - 1)
                pe.wait_ge(proj_ready, 3 * (HG * i + g))
                for b in range(2):
                    pe.wait_ge(t_lo_done, t_use(i, g, f"p{b}") + 1)
                    for j in range(GH):
                        h = GH * ((g - 1) % HG) + j
                        v = slice(h * DK, (h + 1) * DK)
                        last = three(z_bank[:, (GH * b + j) * DK:(GH * b + j + 1) * DK], pt_hi[:, b, j, :],
                                     pt_lo[:, b, j, :], v_hi[:, b, v], v_lo[:, b, v], True, True)
                    last.then_inc(pv_done, 1)

            def project(n_step, gg, kind, first_pair=False):
                use = n_step * 3 + kind
                if not isinstance(use, int) or use >= 2:
                    pe.wait_ge(proj_read, use - 1)
                dst = proj_bank[(3 * gg + kind) % 2]
                if gg == 0:
                    it = (n_step + 0) // HG if isinstance(n_step, int) else None
                    if kind == 0:
                        pe.wait_ge(t_lo_done, project.x_use)
                    if kind == 1:
                        pe.wait_ge(ctx_ready, project.pair + 1)
                    if isinstance(n_step, int) and n_step == 0:
                        pe.wait_ge(w_ready, kind + 1)
                for n in range(2):
                    for c in range(DC):
                        if kind == 2:
                            w = slice(c * HD + gg * GH * DK, c * HD + (gg + 1) * GH * DK)
                            tok = slice(n * SEQ, (n + 1) * SEQ)
                            last = three(dst[:, n * 256:(n + 1) * 256], ctxt_hi[:, c, tok], ctxt_lo[:, c, tok],
                                         w_hi[:, 2, w], w_lo[:, 2, w], c == 0, c == DC - 1)
                        else:
                            w = slice(c * HD + (2 * gg + n) * P, c * HD + (2 * gg + n + 1) * P)
                            hi, lo = (xnt_hi, xnt_lo) if kind == 0 else (ctxt_hi, ctxt_lo)
                            last = three(dst[:, n * 256:(n + 1) * 256], w_hi[:, kind, w], w_lo[:, kind, w],
                                         hi[:, c, :], lo[:, c, :], c == 0, c == DC - 1)
                last.then_inc(proj_full, 1)

            def slot(i, g):
                ahead = (g + 3) % HG
                if real(i, g + 3):
                    project.pair = i + 1 if g else i
                    project.x_use = t_use(i, 0, "xn") + 1 if ahead == 0 else None
                if real(i, g):
                    scores(i, g)
                if real(i, g - 2):
                    z_transpose(i, g)
                if real(i, g + 3):
                    project(HG * i + g + 3, ahead, 0)
                if real(i, g - 1):
                    p_transpose(i, g, 0)
                if real(i, g - 2):
                    wo(i, g)
                if real(i, g - 1):
                    p_transpose(i, g, 1)
                if real(i, g + 3):
                    project(HG * i + g + 3, ahead, 1)
                if real(i, g - 1):
                    pv(i, g)
                if real(i, g + 3):
                    project(HG * i + g + 3, ahead, 2)
                if "xn" in transposes(i, g):
                    dst = open_t(i, g, "xn")
                    pe.wait_ge(xn_done, 2 * (i + 2))
                    x_transpose(dst, xn)
                if "x2" in transposes(i, g):
                    dst = open_t(i, g, "x2")
                    pe.wait_ge(x2n_done, 2 * i)
                    x_transpose(dst, x2n)

            pe.wait_ge(ident_ready, 1)
            pe.wait_ge(xn_done, 2)
            x_transpose(trans_bank[0], xn)
            for s in range(3):
                project.pair, project.x_use = 0, 1
                for kind in range(3):
                    project(s, s, kind)
            for g in range(HG):
                slot(0, g)
            with pe.Fori(1, PAIRS - 1) as i:
                for g in range(HG):
                    slot(i, g)
            for g in range(HG):
                slot(PAIRS - 1, g)
            for g in range(3):
                slot(PAIRS, g)

            pe.wait_ge(t_lo_done, t_use(PAIRS, 2, "x2") + 1)
            pe.wait_ge(z_done, STEPS)
            pe.wait_ge(rt_ready, 1)
            for t in range(BATCH):
                tok = slice(t * SEQ, (t + 1) * SEQ)
                for c in range(DC):
                    last = three(logit_bank[:, t * EXPERTS:(t + 1) * EXPERTS], x2t_hi[:, c, tok],
                                 x2t_lo[:, c, tok], rt_hi[:, c, :], rt_lo[:, c, :], c == 0, c == DC - 1)
            last.then_inc(logits_full, 1)

            def up_product(t, q):
                e, pair = t // PAIRS, t % PAIRS
                if isinstance(t, int):
                    if 4 * t + q >= 4:
                        pe.wait_ge(gelu_done, 4 * t + q - 3)
                else:
                    pe.wait_ge(gelu_done, 4 * t + (q - 3))
                if q == 0:
                    pe.wait_ge(e_ready, 2 * e + 2)
                par = e % 2
                for n in range(2):
                    for c in range(DC):
                        col = par * (2 * MAT) + (c * HIDDEN + (2 * q + n) * P)
                        w_h = e_hi[:, :, :, :].rearrange("p a b n -> p (a b n)")[:, bass.ds(col, P)]
                        w_l = e_lo[:, :, :, :].rearrange("p a b n -> p (a b n)")[:, bass.ds(col, P)]
                        last = three(up_bank[q][:, n * TOK:(n + 1) * TOK], w_h, w_l,
                                     x2t_hi[:, c, bass.ds(pair * TOK, TOK)], x2t_lo[:, c, bass.ds(pair * TOK, TOK)],
                                     c == 0, c == DC - 1)
                last.then_inc(up_full, 1)

            def down_product(t, q):
                par = (t // PAIRS) % 2
                pe.wait_ge(act_ready, 4 * t + (q + 1))
                if q == 0:
                    pe.wait_ge(added, 2 * t)
                for n in range(2):
                    for sub in range(2):
                        tok = slice(sub * SEQ, (sub + 1) * SEQ)
                        col = par * (2 * MAT) + (MAT + (2 * q + n) * D)
                        w_h = e_hi[:, :, :, :].rearrange("p a b n -> p (a b n)")[:, bass.ds(col, D)]
                        w_l = e_lo[:, :, :, :].rearrange("p a b n -> p (a b n)")[:, bass.ds(col, D)]
                        last = three(down_bank[sub][:, 0:D], act_hi[:, q, n, tok], act_lo[:, q, n, tok],
                                     w_h, w_l, q == 0 and n == 0, q == 3 and n == 1)
                last.then_inc(down_used, 1)

            pe.wait_ge(t_lo_done, t_use(PAIRS, 2, "x2") + 1)
            pe.wait_ge(scored, 8 * STEPS)
            for q in range(4):
                up_product(0, q)
                if q >= 2:
                    down_product(0, q - 2)
            with pe.Fori(1, TILES) as t:
                for q in range(4):
                    up_product(t, q)
                    if q < 2:
                        down_product(t - 1, q + 2)
                    else:
                        down_product(t, q - 2)
            down_product(TILES - 1, 2)
            down_product(TILES - 1, 3)

        @block.scalar
        def _(act):
            def t_high(i, g, kind, dst):
                n = t_use(i, g, kind)
                act.wait_ge(t_full, n + 1)
                act.activation(dst, trans_bank[t_bank(g, kind)][:, :].rearrange("p (a b c) -> p a b c", a=2, b=dst.shape[2]),
                               ACT.Copy).then_inc(t_hi_done, 1)

            def exponentials(i, g, b):
                par = g % 2
                for j in range(GH):
                    n = GH * b + j
                    act.wait_ge(scored, 8 * (HG * i + g) + n + 1)
                    act.activation(probs[:, par, b, j, :], probs[:, par, b, j, :], ACT.Exp,
                                   bias=low[:, par, n:n + 1], scale=-1.0,
                                   accum_out=total[:, par, n:n + 1]).then_inc(exp_done, 1)

            def proj_high(n_step, gg, kind):
                act.wait_ge(proj_read, 3 * n_step + (kind + 1))
                if kind == 2:
                    dst = v_hi[:, :, gg * GH * DK:(gg + 1) * GH * DK]
                else:
                    dst = (qt_hi, kt_hi)[kind][:, 2 * gg:2 * gg + 2, :]
                act.activation(dst, proj_f[:, kind, :].rearrange("p (a n) -> p a n", a=2),
                               ACT.Copy).then_inc(proj_hi_done, 1)

            def ctx_high(pair):
                act.wait_ge(ctx_loaded, 16 * (pair + 1))
                if not isinstance(pair, int) or pair > 0:
                    act.wait_ge(proj_full, 12 * pair)
                act.activation(ctxt_hi[:, :, :], ctxt[:, :, :], ACT.Copy).then_inc(ctx_hi_done, 1)

            def slot(i, g):
                if real(i, g - 2):
                    if not isinstance(i, int) or HG * i + g - 2 >= 1:
                        act.wait_ge(wo_done, HG * i + g - 2)
                    t_high(i, g, "z", zt_hi[:, :, :, :])
                if real(i, g):
                    exponentials(i, g, 0)
                if real(i, g - 1):
                    for b in range(2):
                        if not isinstance(i, int) or HG * i + g - 1 >= 1:
                            act.wait_ge(pv_done, 2 * (HG * i + g - 2) + b + 1)
                        n = t_use(i, g, f"p{b}")
                        act.wait_ge(t_full, n + 1)
                        act.activation(pt_hi[:, b, :, :].rearrange("p a b -> p (a b)"), trans_bank[t_bank(g, f"p{b}")][:, :],
                                       ACT.Copy).then_inc(t_hi_done, 1)
                        if b == 0 and real(i, g + 3):
                            proj_high(HG * i + g + 3, (g + 3) % HG, 0)
                elif real(i, g + 3):
                    proj_high(HG * i + g + 3, (g + 3) % HG, 0)
                if real(i, g):
                    exponentials(i, g, 1)
                if real(i, g + 3):
                    proj_high(HG * i + g + 3, (g + 3) % HG, 1)
                    proj_high(HG * i + g + 3, (g + 3) % HG, 2)
                if "xn" in transposes(i, g):
                    ctx_high(i + 1)
                    t_high(i, g, "xn", xnt_hi[:, :, :].rearrange("p c (b t) -> p c b t", b=2))
                if "x2" in transposes(i, g):
                    col = (i - 1) * TOK
                    t_high(i, g, "x2", x2t_hi[:, :, bass.ds(col, TOK)].rearrange("p c (b t) -> p c b t", b=2))

            def weight_high(m):
                act.wait_ge(mat_loaded[m], 16)
                act.activation(w_hi[:, m, :], stage[:, m, :], ACT.Copy, scale=W_SCALE).then_inc(w_hi_done, 1)

            weight_high(0)
            ctx_high(0)
            act.wait_ge(t_full, 1)
            act.activation(xnt_hi[:, :, :].rearrange("p c t -> p (c t)"), trans_bank[0][:, :], ACT.Copy).then_inc(t_hi_done, 1)
            weight_high(1)
            proj_high(0, 0, 0)
            weight_high(2)
            proj_high(0, 0, 1)
            proj_high(0, 0, 2)
            weight_high(3)
            for s in range(1, 3):
                for kind in range(3):
                    proj_high(s, s, kind)
            act.wait_ge(small_loaded, 80)
            act.activation(rt_hi[:, :, :], rt[:, :, :], ACT.Copy, scale=W_SCALE).then_inc(rt_hi_done, 1)
            for g in range(HG):
                slot(0, g)
            with act.Fori(1, PAIRS - 1) as i:
                for g in range(HG):
                    slot(i, g)
            for g in range(HG):
                slot(PAIRS - 1, g)
            for g in range(3):
                slot(PAIRS, g)

            act.wait_ge(gating, GATING_BEFORE_EXP)
            act.activation(weight[:, :, :], shifted[:, :, :], ACT.Exp, scale=1.0 / W_SCALE).then_inc(exped, 1)

            def gelu(t, q):
                act.wait_ge(up_full, 4 * t + (q + 1))
                if isinstance(t, int) and t == 0:
                    if q >= 2:
                        act.wait_ge(act_ready, q - 1)
                else:
                    act.wait_ge(down_used, 4 * t + (q - 3))
                    act.wait_ge(act_ready, 4 * t + (q - 1))
                flat = up_bank[q][:, :].rearrange("p (n t) -> p n t", n=2)
                act.activation(act_hi[:, q, :, :], flat, ACT.Gelu_apprx_tanh, scale=1.0 / W_SCALE).then_inc(gelu_hi_done, 1)
                act.activation(act_f[:, q % 2, :, :], flat, ACT.Gelu_apprx_tanh, scale=1.0 / W_SCALE).then_inc(gelu_done, 1)

            for q in range(4):
                gelu(0, q)
            with act.Fori(1, TILES) as t:
                for q in range(4):
                    gelu(t, q)

        @block.vector
        def _(dve):
            def t_low(i, g, kind, hi, lo):
                n = t_use(i, g, kind)
                dve.wait_ge(t_hi_done, n + 1)
                dve.tensor_tensor(lo, trans_bank[t_bank(g, kind)][:, :].rearrange("p (a b c) -> p a b c", a=2, b=2)
                                  if len(lo.shape) == 4 else trans_bank[t_bank(g, kind)][:, :],
                                  hi, ALU.subtract).then_inc(t_lo_done, 1)

            def mask_scores(i, g):
                par = g % 2
                dve.wait_ge(scores_full, HG * i + g + 1)
                if not isinstance(i, int) or HG * i + g >= 2:
                    dve.wait_ge(t_full, t_use(*((i, g - 1) if g else (i - 1, HG - 1)), "p1") + 1)
                if g == 0:
                    dve.wait_ge(penalty_ready, i + 1)
                apart(dve)
                for b in range(2):
                    for j in range(GH):
                        n = GH * b + j
                        src = score_bank[j % 2][:, (2 * b + j // 2) * SEQ:(2 * b + j // 2 + 1) * SEQ]
                        dve.tensor_tensor_reduce(out=probs[:, par, b, j, :], in0=src,
                                                 in1=penalty[:, b, :],
                                                 scale=1.0, scalar=MASKED, op0=ALU.add, op1=ALU.min,
                                                 accum_out=low[:, par, n:n + 1]).then_inc(scored, 1)

            def proj_read_out(n_step, gg, kind):
                dve.wait_ge(proj_full, 3 * n_step + (kind + 1))
                if not isinstance(n_step, int) or n_step >= 1:
                    dve.wait_ge(proj_ready, 3 * n_step + (kind - 2))
                src = proj_bank[(3 * gg + kind) % 2][:, :].rearrange("p (a n) -> p a n", a=2)
                if kind == 2:
                    bias = bcast(bv_row[:, gg * 256:(gg + 1) * 256].rearrange("p (a n) -> p a n", a=1), [P, 2, 256])
                else:
                    cols = (bq_neg, bk_col)[kind][:, 2 * gg:2 * gg + 2].rearrange("p (a n) -> p a n", n=1)
                    bias = bcast(cols, [P, 2, 256])
                dve.scalar_tensor_tensor(out=proj_f[:, kind, :].rearrange("p (a n) -> p a n", a=2), in0=src,
                                         scalar=Q_SCALE if kind == 0 else 1.0 / W_SCALE, in1=bias,
                                         op0=ALU.mult, op1=ALU.add).then_inc(proj_read, 1)

            def statistics(src, bn, mv, bn_done, mv_done, count):
                for b in range(2):
                    dve.bn_stats(bn[:, b, :], src[:, b, :]).then_inc(bn_done, 1)
                dve.wait_ge(bn_done, 2 * count + 2)
                apart(dve)
                for b in range(2):
                    dve.bn_aggr(mv[:, b, :], bn[:, b, :]).then_inc(mv_done, 1)

            def normalise(dst, src, mv, rs, rs_done, done, count):
                dve.wait_ge(rs_done, count + 1)
                for b in range(2):
                    dve.tensor_scalar(dst[:, b, :], src[:, b, :], mv[:, b, 0:1], rs[:, b:b + 1],
                                      ALU.subtract, ALU.mult).then_inc(done, 1)

            def block_rows(pair):
                return lambda b: rows[:, bass.ds(2 * pair + b, 1), :].rearrange("p a d -> p (a d)")

            def residual(i):
                dve.wait_ge(wo_done, HG * i)
                dve.scalar_tensor_tensor(out=y_bias[:, :, :], in0=y_bank[:, :].rearrange("p (b d) -> p b d", b=2),
                                         scalar=1.0 / W_SCALE,
                                         in1=bcast(bo_row[:, :].rearrange("p (a n) -> p a n", a=1), [P, 2, D]),
                                         op0=ALU.mult, op1=ALU.add).then_inc(y_biased, 1)
                dve.wait_ge(y_biased, i)
                if isinstance(i, int) and i == 1 or not isinstance(i, int):
                    dve.wait_ge(rows_loaded, 16)
                dve.tensor_tensor(x2[:, :, :], rows[:, bass.ds(2 * (i - 1), 2), :], y_bias[:, :, :],
                                  ALU.add).then_inc(x2_done, 1)
                dve.wait_ge(x2_done, i)
                apart(dve)
                statistics(x2, bn2, mv2, bn2_done, mv2_done, i - 1)

            def slot(i, g):
                if "xn" in transposes(i, g):
                    dve.wait_ge(x_loaded, 16 * (i + 2))
                    apart(dve)
                    statistics(x_in, bn1, mv1, bn1_done, mv1_done, i + 1)
                if real(i, g - 2):
                    t_low(i, g, "z", zt_hi[:, :, :, :], zt_lo[:, :, :, :])
                if real(i, g):
                    mask_scores(i, g)
                if real(i, g + 3):
                    proj_read_out(HG * i + g + 3, (g + 3) % HG, 0)
                if "xn" in transposes(i, g):
                    normalise(xn, x_in, mv1, rs1, rs1_done, xn_done, i + 1)
                if "x2" in transposes(i, g):
                    dve.wait_ge(rows_done, i)
                    normalise(x2n, x2, mv2, rs2, rs2_done, x2n_done, i - 1)
                if real(i, g - 1):
                    s = HG * i + g - 1
                    dve.wait_ge(exp_done, 8 * s + 8)
                    dve.reciprocal(inv[:, :], total[:, (g - 1) % 2, :]).then_inc(inv_done, 1)
                    for b in range(2):
                        t_low(i, g, f"p{b}", pt_hi[:, b, :, :].rearrange("p a b -> p (a b)"),
                              pt_lo[:, b, :, :].rearrange("p a b -> p (a b)"))
                if real(i, g + 3):
                    proj_read_out(HG * i + g + 3, (g + 3) % HG, 1)
                if real(i, g - 1):
                    dve.wait_ge(pv_done, 2 * s + 2)
                    dve.wait_ge(inv_done, s + 1)
                    dve.tensor_tensor(z[:, :, :, :].rearrange("p b h d -> p (b h) d"),
                                      z_bank[:, :].rearrange("p (h d) -> p h d", d=DK),
                                      bcast(inv[:, :].rearrange("p (h n) -> p h n", n=1), [P, 2 * GH, DK]),
                                      ALU.mult).then_inc(z_done, 1)
                if real(i, g + 3):
                    proj_read_out(HG * i + g + 3, (g + 3) % HG, 2)
                if "xn" in transposes(i, g):
                    t_low(i, g, "xn", xnt_hi[:, :, :].rearrange("p c (b t) -> p c b t", b=2),
                          xnt_lo[:, :, :].rearrange("p c (b t) -> p c b t", b=2))
                if g == 1 and (not isinstance(i, int) or i >= 1):
                    residual(i)
                if "x2" in transposes(i, g):
                    col = bass.ds((i - 1) * TOK, TOK)
                    t_low(i, g, "x2", x2t_hi[:, :, col].rearrange("p c (b t) -> p c b t", b=2),
                          x2t_lo[:, :, col].rearrange("p c (b t) -> p c b t", b=2))

            def weight_low(m):
                dve.wait_ge(w_hi_done, m + 1)
                dve.scalar_tensor_tensor(out=w_lo[:, m, :], in0=stage[:, m, :], scalar=W_SCALE, in1=w_hi[:, m, :],
                                         op0=ALU.mult, op1=ALU.subtract).then_inc(w_ready, 1)

            dve.memset(half[:, :], -0.5).then_inc(half_set, 1)
            dve.wait_ge(x_loaded, 16)
            statistics(x_in, bn1, mv1, bn1_done, mv1_done, 0)
            dve.wait_ge(small_loaded, 80)
            dve.tensor_scalar(bq_neg[:, :], bq_raw[:, :], Q_SCALE * W_SCALE, None, ALU.mult).then_inc(bq_ready, 1)
            normalise(xn, x_in, mv1, rs1, rs1_done, xn_done, 0)
            weight_low(0)
            dve.wait_ge(t_hi_done, 1)
            dve.tensor_tensor(xnt_lo[:, :, :].rearrange("p c t -> p (c t)"), trans_bank[0][:, :],
                              xnt_hi[:, :, :].rearrange("p c t -> p (c t)"), ALU.subtract).then_inc(t_lo_done, 1)
            dve.wait_ge(bq_ready, 1)
            proj_read_out(0, 0, 0)
            weight_low(1)
            proj_read_out(0, 0, 1)
            weight_low(2)
            proj_read_out(0, 0, 2)
            weight_low(3)
            for s in range(1, 3):
                for kind in range(3):
                    proj_read_out(s, s, kind)
            dve.wait_ge(rt_hi_done, 1)
            dve.scalar_tensor_tensor(out=rt_lo[:, :, :], in0=rt[:, :, :], scalar=W_SCALE, in1=rt_hi[:, :, :],
                                     op0=ALU.mult, op1=ALU.subtract).then_inc(rt_ready, 1)
            for g in range(HG):
                slot(0, g)
            with dve.Fori(1, PAIRS - 1) as i:
                for g in range(HG):
                    slot(i, g)
            for g in range(HG):
                slot(PAIRS - 1, g)
            for g in range(3):
                slot(PAIRS, g)

            step = [0]

            def link(ins):
                step[0] += 1
                ins.then_inc(gating, 1)
                dve.wait_ge(gating, step[0])

            dve.wait_ge(logits_full, 1)
            link(dve.tensor_copy(logit[:, :, :], logit_bank[:, 0:BATCH * EXPERTS].rearrange("p (t e) -> p t e", e=EXPERTS)))
            link(dve.tensor_reduce(top[:, :], logit[:, :, :], axis=AX_X, op=ALU.max))
            link(dve.tensor_tensor(shifted[:, :, :], logit[:, :, :],
                                   bcast(top[:, :].rearrange("p (t n) -> p t n", n=1), [P, BATCH, EXPERTS]), ALU.subtract))
            assert step[0] == GATING_BEFORE_EXP
            for e in range(EXPERTS):
                one = logit[:, :, e:e + 1]
                dve_last = dve.tensor_tensor(beat[:, e, :, 0:e + 1], bcast(one, [P, BATCH, e + 1]),
                                             logit[:, :, 0:e + 1], ALU.is_gt)
                if e + 1 < EXPERTS:
                    n = EXPERTS - e - 1
                    dve_last = dve.tensor_tensor(beat[:, e, :, e + 1:EXPERTS], bcast(one, [P, BATCH, n]),
                                                 logit[:, :, e + 1:EXPERTS], ALU.is_ge)
            link(dve_last)
            width = EXPERTS
            while width > 2:
                width //= 2
                link(dve.tensor_tensor(beat[:, 0:width, :, :], beat[:, 0:width, :, :],
                                       beat[:, width:2 * width, :, :], ALU.add))
            link(dve.tensor_tensor(rank[:, :, :], beat[:, 0, :, :], beat[:, 1, :, :], ALU.add))
            dve.wait_ge(exped, 1)
            link(dve.scalar_tensor_tensor(out=chosen[:, :, :], in0=rank[:, :, :], scalar=float(TOPK) - 0.5,
                                          in1=weight[:, :, :], op0=ALU.is_lt, op1=ALU.mult))
            link(dve.tensor_reduce(mass[:, :], chosen[:, :, :], axis=AX_X, op=ALU.add))
            link(dve.tensor_scalar(mass[:, :], mass[:, :], W_SCALE, None, ALU.mult))
            link(dve.reciprocal(mass[:, :], mass[:, :]))
            link(dve.tensor_tensor(gate[:, :, :], chosen[:, :, :],
                                   bcast(mass[:, :].rearrange("p (t n) -> p t n", n=1), [P, BATCH, EXPERTS]), ALU.mult))

            def gelu_low(t, q):
                dve.wait_ge(gelu_done, 4 * t + (q + 1))
                dve.tensor_tensor(act_lo[:, q, :, :], act_f[:, q % 2, :, :], act_hi[:, q, :, :],
                                  ALU.subtract).then_inc(act_ready, 1)

            def add_tile(t):
                e, pair = t // PAIRS, t % PAIRS
                dve.wait_ge(down_used, 4 * t + 4)
                for sub in range(2):
                    r = block_rows(pair)(sub)
                    g_col = gate[:, :, :].rearrange("p t e -> p (t e)")[:, bass.ds((2 * pair + sub) * EXPERTS + e, 1)]
                    dve.scalar_tensor_tensor(out=r, in0=down_bank[sub][:, 0:D], scalar=g_col, in1=r,
                                             op0=ALU.mult, op1=ALU.add).then_inc(added, 1)

            for q in range(4):
                gelu_low(0, q)
            with dve.Fori(1, TILES) as t:
                gelu_low(t, 0)
                gelu_low(t, 1)
                add_tile(t - 1)
                gelu_low(t, 2)
                gelu_low(t, 3)
            add_tile(TILES - 1)

        @block.gpsimd
        def _(pool):
            def rstd(mv, ve, rs, mv_done, ve_done, rs_done, count):
                pool.wait_ge(mv_done, 2 * count + 2)
                apart(pool)
                pool.tensor_scalar(ve[:, :], mv[:, :, 1], EPS, None, ALU.add).then_inc(ve_done, 1)
                pool.wait_ge(ve_done, count + 1)
                pool.tensor_tensor(rs[:, :], ve[:, :], half[:, :], ALU.pow).then_inc(rs_done, 1)

            def mask_penalty(pair):
                pool.wait_ge(mask_loaded, 16 * (pair + 1))
                if not isinstance(pair, int) or pair > 0:
                    pool.wait_ge(scored, 8 * HG * pair)
                apart(pool)
                pool.tensor_scalar(penalty[:, :, :], mask_in[:, :, :], 0.0, MASKED,
                                   ALU.is_equal, ALU.mult).then_inc(penalty_ready, 1)

            def proj_low(n_step, gg, kind):
                pool.wait_ge(proj_hi_done, 3 * n_step + (kind + 1))
                if kind == 2:
                    cols = slice(gg * GH * DK, (gg + 1) * GH * DK)
                    hi, lo = v_hi[:, :, cols], v_lo[:, :, cols]
                else:
                    cols = slice(2 * gg, 2 * gg + 2)
                    hi, lo = (qt_hi, kt_hi)[kind][:, cols, :], (qt_lo, kt_lo)[kind][:, cols, :]
                pool.tensor_tensor(lo, proj_f[:, kind, :].rearrange("p (a n) -> p a n", a=2), hi,
                                   ALU.subtract).then_inc(proj_ready, 1)

            def ctx_low(pair):
                pool.wait_ge(ctx_hi_done, pair + 1)
                pool.tensor_tensor(ctxt_lo[:, :, :], ctxt[:, :, :], ctxt_hi[:, :, :],
                                   ALU.subtract).then_inc(ctx_ready, 1)

            def slot(i, g):
                if "xn" in transposes(i, g):
                    rstd(mv1, ve1, rs1, mv1_done, ve1_done, rs1_done, i + 1)
                if real(i, g + 3):
                    for kind in range(3):
                        proj_low(HG * i + g + 3, (g + 3) % HG, kind)
                if "xn" in transposes(i, g):
                    ctx_low(i + 1)
                if g == 1 and (not isinstance(i, int) or i >= 1):
                    rstd(mv2, ve2, rs2, mv2_done, ve2_done, rs2_done, i - 1)
                    pool.tensor_copy(rows[:, bass.ds(2 * (i - 1), 2), :], x2[:, :, :]).then_inc(rows_done, 1)
                if g == HG - 1 and (not isinstance(i, int) or i + 1 < PAIRS):
                    mask_penalty(i + 1)

            def split_expert(pair, parity):
                for kind in range(2):
                    slot_ = 2 * parity + kind
                    n = 4 * pair + (2 * parity + kind)
                    pool.wait_ge(mat_loaded[slot_], 16 * pair + 32)
                    if kind == 0 and not (isinstance(pair, int) and pair == 0):
                        pool.wait_ge(down_used, 4 * PAIRS * (2 * pair + (parity - 1)))
                    apart(pool)
                    pool.tensor_scalar(e_hi[:, parity, kind, :], stage[:, slot_, :], W_SCALE, None,
                                       ALU.mult).then_inc(e_hi_done, 1)
                    pool.tensor_scalar(stage[:, slot_, :], stage[:, slot_, :], W_SCALE, None,
                                       ALU.mult).then_inc(e_scaled, 1)
                    pool.wait_ge(e_scaled, n + 1)
                    pool.wait_ge(e_hi_done, n + 1)
                    pool.tensor_tensor(e_lo[:, parity, kind, :], stage[:, slot_, :], e_hi[:, parity, kind, :],
                                       ALU.subtract).then_inc(e_ready, 1)

            pool.memset(ident[:, :], 0.0).then_inc(ident_zero, 1)
            pool.wait_ge(ident_zero, 1)
            pool.affine_select(out=ident[:, :], in_=ident[:, :], compare_op=ALU.not_equal, fill=1.0, base=0,
                               pattern=[[-1, P]], channel_multiplier=1).then_inc(ident_ready, 1)
            pool.wait_ge(half_set, 1)
            rstd(mv1, ve1, rs1, mv1_done, ve1_done, rs1_done, 0)
            ctx_low(0)
            for kind in range(3):
                proj_low(0, 0, kind)
            for s in range(1, 3):
                for kind in range(3):
                    proj_low(s, s, kind)
            mask_penalty(0)
            for g in range(HG):
                slot(0, g)
            with pool.Fori(1, PAIRS - 1) as i:
                for g in range(HG):
                    slot(i, g)
            for g in range(HG):
                slot(PAIRS - 1, g)
            for g in range(3):
                slot(PAIRS, g)
            for parity in range(2):
                split_expert(0, parity)
            with pool.Fori(1, EXPERTS // 2) as pair:
                for parity in range(2):
                    split_expert(pair, parity)


GATING_BEFORE_EXP = 3

_ORDER = ["x", "ctx_t", "mask", "wq_t", "wk_t", "wv_t", "wo_t", "bq_t", "bk_t", "bv", "bo", "router", "up", "down"]


def kernel(x, ctx_1024, mask_BxSxS2_ik1, L0_xattn_WQ_w, L0_xattn_WQ_b, L0_xattn_WK_w, L0_xattn_WK_b,
           L0_xattn_WV_w, L0_xattn_WV_b, L0_xattn_WO_w, L0_xattn_WO_b, L0_ffn_router_w, L0_ffn_up_w, L0_ffn_down_w):
    import numpy as np
    import concourse.bacc as bacc
    from concourse.bass_utils import run_bass_kernel_spmd

    def t(a):
        return np.ascontiguousarray(np.asarray(a).T)

    laid = {
        "x": np.asarray(x),
        "ctx_t": t(np.asarray(ctx_1024).reshape(BATCH * SEQ, D)),
        "mask": np.asarray(mask_BxSxS2_ik1),
        "wq_t": t(L0_xattn_WQ_w), "wk_t": t(L0_xattn_WK_w), "wv_t": t(L0_xattn_WV_w), "wo_t": t(L0_xattn_WO_w),
        "bq_t": t(np.asarray(L0_xattn_WQ_b).reshape(CHUNKS, P)),
        "bk_t": t(np.asarray(L0_xattn_WK_b).reshape(CHUNKS, P)),
        "bv": np.asarray(L0_xattn_WV_b).reshape(1, HD),
        "bo": np.asarray(L0_xattn_WO_b).reshape(1, D),
        "router": np.asarray(L0_ffn_router_w), "up": np.asarray(L0_ffn_up_w), "down": np.asarray(L0_ffn_down_w),
    }
    nc = bacc.Bacc("TRN2", target_bir_lowering=False, num_devices=1)
    arrays, args = {}, []
    for name in _ORDER:
        a = np.ascontiguousarray(laid[name])
        arrays[f"in_{name}"] = a
        args.append(nc.dram_tensor(f"in_{name}", a.shape, mybir.dt.from_np(a.dtype), kind="ExternalInput").ap())
    out = nc.dram_tensor("out", (BATCH, SEQ, D), F32, kind="ExternalOutput").ap()
    xattn_ffn(nc, *args, out)
    r = run_bass_kernel_spmd(nc, [arrays], core_ids=[0])
    return r.results[0]["out"]
```

```python
from contextlib import ExitStack

import concourse.bass as bass
from concourse import mybir

P = 128
F32, F16, I32 = mybir.dt.float32, mybir.dt.float16, mybir.dt.int32
ALU = mybir.AluOpType
ACT = mybir.ActivationFunctionType
AX_X = mybir.AxisListType.X

BATCH, SEQ, D = 16, 128, 256
HEADS, DK = 16, 64
HD = HEADS * DK
EXPERTS, TOPK, HIDDEN = 8, 4, 1024
DC = D // P
CHUNKS = HD // P
HC = HIDDEN // P
PAIRS = BATCH // 2
HG = 4
GH = HEADS // HG
STEPS = PAIRS * HG
TOK = 2 * SEQ
TOKENS = BATCH * SEQ
LIST_TILES = TOKENS // TOK
ALL_TILES = EXPERTS * LIST_TILES
TILES = (TOPK * TOKENS + EXPERTS * (TOK - 1)) // TOK
MAT = 2048
MATS = 2 * EXPERTS
EARLY = 10
LATE_MATS = MATS - EARLY
W_SCALE = 32.0
Q_SCALE = -1.0 / (W_SCALE * DK ** 0.5)
MASKED = 1.0e30
EPS = 1e-5


def real(i, offset):
    return not isinstance(i, int) or 0 <= HG * i + offset < STEPS


def real_pair(i, offset):
    return not isinstance(i, int) or 0 <= i + offset < PAIRS


SPLIT_USES = ("z", "p0", "p1", "xn", "x2")


def bank_uses(i, group):
    uses = []
    if real(i, group - 2):
        uses.append("z")
    if group == 3 and real_pair(i, -1):
        uses.append("logits")
    if real(i, group - 1):
        uses += ["p0", "p1"]
    if group == 0 and real_pair(i, 1):
        uses.append("xn")
    if group == 2 and real_pair(i, -1):
        uses.append("x2")
    if group == 3 and real_pair(i, -1):
        uses.append("ranks")
    return uses


def use_number(i, group, kind, kinds):
    if isinstance(i, int):
        before = 1
        for s in range(HG * i + group):
            before += sum(k in kinds for k in bank_uses(s // HG, s % HG))
        mine = bank_uses(i, group)
        return before + sum(k in kinds for k in mine[:mine.index(kind)])
    per_trip = sum(k in kinds for g in range(HG) for k in bank_uses(1, g))
    return i * per_trip + (use_number(1, group, kind, kinds) - per_trip)


def t_use(i, group, kind):
    return use_number(i, group, kind, SPLIT_USES + ("logits", "ranks"))


def hi_use(i, group, kind):
    return use_number(i, group, kind, SPLIT_USES)


def t_bank(i, group, kind):
    return t_use(i if isinstance(i, int) else 1, group, kind) % 2


def xattn_ffn(nc, x, ctx_t, mask, attn_w, bq_t, bk_t, bv, bo, router, expert_w, out):
    assert sum(len(bank_uses(1, g)) for g in range(HG)) % 2 == 0
    x_rows = x.rearrange("b s d -> s b d")
    out_rows = out.rearrange("b s d -> s b d")
    mask_rows = mask.rearrange("b q k -> q b k")
    ctx_rows = ctx_t.rearrange("(c p) t -> p c t", p=P)
    lists = nc.dram_tensor("lists", (EXPERTS * TOKENS, 2), I32, kind="Internal").ap()
    normed = nc.dram_tensor("normed", (TOKENS, D), F32, kind="Internal").ap()
    normed_rows = normed.rearrange("(b s) d -> s b d", s=SEQ)
    out_flat = out.rearrange("b s d -> (b s) d")

    ctx = ExitStack()
    with ctx:
        def sb(name, shape, dt):
            return ctx.enter_context(nc.sbuf_tensor(name, shape, dt))

        def sem(name):
            return ctx.enter_context(nc.semaphore(name))

        e_w = sb("e_w", [P, MATS, 2, MAT], F16)
        e_flat = e_w[:, :, :, :].rearrange("p m h n -> p (m h n)")
        stage = sb("stage", [P, 2, MAT], F32)
        w_hi, w_lo = e_w[:, EARLY:EARLY + 4, 0, :], e_w[:, EARLY:EARLY + 4, 1, :]
        attn_stage = e_flat[:, 0:4 * 2 * MAT].bitcast(F32).rearrange("p (m n) -> p m n", m=4)
        qt_hi, qt_lo, kt_hi, kt_lo = (e_w[:, EARLY + 4 + m, h, :].rearrange("p (c t) -> p c t", t=TOK)
                                      for m in range(2) for h in range(2))
        v_hi = sb("v_hi", [P, 2, HD], F16)
        v_lo = sb("v_lo", [P, 2, HD], F16)
        ident = sb("ident", [P, P], F32)
        x_res = sb("x_res", [P, 2, D], F32)
        x2t_hi = sb("x2t_hi", [P, DC, TOK], F16)
        x2t_lo = sb("x2t_lo", [P, DC, TOK], F16)
        xnt_hi = sb("xnt_hi", [P, DC, TOK], F16)
        xnt_lo = sb("xnt_lo", [P, DC, TOK], F16)
        ctxt = sb("ctxt", [P, DC, TOK], F32)
        ctxt_hi = sb("ctxt_hi", [P, DC, TOK], F16)
        ctxt_lo = sb("ctxt_lo", [P, DC, TOK], F16)
        proj_f = sb("proj_f", [P, 3, 512], F32)
        mask_in = sb("mask_in", [P, 2, SEQ], I32)
        penalty = sb("penalty", [P, 2, SEQ], F32)
        x_in = sb("x_in", [P, 2, D], F32)
        x2 = sb("x2", [P, 2, D], F32)
        probs = sb("probs", [P, 2, 2, GH, SEQ], F32)
        pt = sb("pt", [P, 2, 2, GH, SEQ], F16)
        pt_hi, pt_lo = pt[:, 0, :, :, :], pt[:, 1, :, :, :]
        z = sb("z", [P, 2, GH, DK], F32)
        zt_hi = sb("zt_hi", [P, 2, 2, SEQ], F16)
        zt_lo = sb("zt_lo", [P, 2, 2, SEQ], F16)
        rows = sb("rows", [P, 2, 2, D], F32)
        xn, x2n = rows[:, 0, :, :], rows[:, 1, :, :]
        y_bias = sb("y_bias", [P, 2, D], F32)
        bq_raw = sb("bq_raw", [P, CHUNKS], F32)
        bq_neg = sb("bq_neg", [P, CHUNKS], F32)
        bk_col = sb("bk_col", [P, CHUNKS], F32)
        bv_row = sb("bv_row", [P, HD], F32)
        bo_row = sb("bo_row", [P, D], F32)
        low = sb("low", [P, 2, 2 * GH], F32)
        total = sb("total", [P, 2, 2 * GH], F32)
        inv = sb("inv", [P, 2 * GH], F32)
        half = sb("half", [P, 2], F32)
        bn1 = sb("bn1", [P, 2, 6], F32)
        mv1 = sb("mv1", [P, 2, 2], F32)
        ve1 = sb("ve1", [P, 2], F32)
        rs1 = sb("rs1", [P, 2], F32)
        bn2 = sb("bn2", [P, 2, 6], F32)
        mv2 = sb("mv2", [P, 2, 2], F32)
        ve2 = sb("ve2", [P, 2], F32)
        rs2 = sb("rs2", [P, 2], F32)
        rt = sb("rt", [P, DC, EXPERTS], F32)
        rt_hi = sb("rt_hi", [P, DC, EXPERTS], F16)
        rt_lo = sb("rt_lo", [P, DC, EXPERTS], F16)
        before = sb("before", [P, P], F16)
        ones = sb("ones", [P, P], F16)
        tie = sb("tie", [P, 2, EXPERTS, EXPERTS], F32)
        list_base = sb("list_base", [P, 2, EXPERTS], F32)
        from_end = sb("from_end", [P, 2], F32)
        logit = sb("logit", [P, 2, EXPERTS], F32)
        top = sb("top", [P, 2], F32)
        shifted = sb("shifted", [P, 2, EXPERTS], F32)
        weight = sb("weight", [P, 2, EXPERTS], F32)
        lead = sb("lead", [P, 2, EXPERTS, EXPERTS], F32)
        tied = sb("tied", [P, 2, EXPERTS, EXPERTS], F32)
        rank = sb("rank", [P, 2, EXPERTS], F32)
        chosen = sb("chosen", [P, 2, EXPERTS], F32)
        picked = sb("picked", [P, 2, EXPERTS], F16)
        picked_sum = sb("picked_sum", [P, EXPERTS], F16)
        mass = sb("mass", [P, 2], F32)
        inv_mass = sb("inv_mass", [P, 2], F32)
        place = sb("place", [P, 2, EXPERTS], F32)
        slot_of = sb("slot_of", [P, 2, EXPERTS], I32)
        entry = sb("entry", [P, 2, EXPERTS, 2], I32)
        pick_wide = sb("pick_wide", [P, EXPERTS, LIST_TILES], F16)
        base_row = sb("base_row", [1, EXPERTS, LIST_TILES], F16)
        tile_col = sb("tile_col", [ALL_TILES, 1], F32)
        tile_col16 = sb("tile_col16", [ALL_TILES, 1], F16)
        tile_row = sb("tile_row", [ALL_TILES, ALL_TILES], F32)
        start_col = sb("start_col", [ALL_TILES, 1], F32)
        is_real = sb("is_real", [ALL_TILES, 1], F16)
        order = sb("order", [ALL_TILES, 6], F32)
        one_hot = sb("one_hot", [ALL_TILES, ALL_TILES], F16)
        table = sb("table", [1, ALL_TILES], I32)
        probs_flat = probs[:, :, :, :, :].rearrange("p s b h k -> p (s b h k)")
        act_f = probs_flat[:, 0:1024].rearrange("p (s n t) -> p s n t", s=2, n=2)
        act_hi = probs_flat[:, 1024:2048].bitcast(F16).rearrange("p (q n t) -> p q n t", q=4, n=2)
        act_lo = pt[:, :, :, :, :].rearrange("p a b h k -> p (a b h k)").rearrange("p (q n t) -> p q n t", q=4, n=2)
        xt_hi = v_hi[:, :, :].rearrange("p a n -> p (a n)")[:, 0:2 * DC * TOK]
        xt_lo = v_lo[:, :, :].rearrange("p a n -> p (a n)")[:, 0:2 * DC * TOK]
        y_out = proj_f[:, 0, :].rearrange("p (b d) -> p b d", b=2)
        gathered = rows
        gather_ids = sb("gather_ids", [P, 2, 2, 2], I32)
        add_ids = sb("add_ids", [P, 2, 2], I32)

        bank = [ctx.enter_context(nc.psum_tensor(f"bank{n}", [P, 512], F32)) for n in range(8)]
        proj_bank, score_bank, trans_bank, z_bank, y_bank = bank[0:2], bank[2:4], bank[4:6], bank[6], bank[7]
        up_bank, down_bank, xt_bank, table_bank = bank[0:4], bank[4:6], bank[6], bank[7]

        x_loaded, res_loaded, ctx_loaded, mask_loaded = (sem(n) for n in ("x_loaded", "res_loaded", "ctx_loaded", "mask_loaded"))
        small_loaded = sem("small_loaded")
        attn_loaded = [sem(f"attn_loaded{m}") for m in range(4)]
        mat_loaded = sem("mat_loaded")
        x2_stored, normed_stored = sem("x2_stored"), sem("normed_stored")
        half_set, bq_ready = sem("half_set"), sem("bq_ready")
        ident_zero, ident_ready = sem("ident_zero"), sem("ident_ready")
        const_raw, const_ready, const16_ready = sem("const_raw"), sem("const_ready"), sem("const16_ready")
        penalty_ready = sem("penalty_ready")
        w_hi_done, w_ready = sem("w_hi_done"), sem("w_ready")
        mat_scaled, mat_hi_done, mat_ready = sem("mat_scaled"), sem("mat_hi_done"), sem("mat_ready")
        ctx_hi_done = sem("ctx_hi_done")
        ctx_ready = sem("ctx_ready")
        bn1_done, mv1_done, ve1_done, rs1_done, xn_done = (sem(n) for n in ("bn1_done", "mv1_done", "ve1_done", "rs1_done", "xn_done"))
        bn2_done, mv2_done, ve2_done, rs2_done, x2n_done = (sem(n) for n in ("bn2_done", "mv2_done", "ve2_done", "rs2_done", "x2n_done"))
        t_full = sem("t_full")
        t_hi_done = sem("t_hi_done")
        t_lo_done = sem("t_lo_done")
        proj_full = sem("proj_full")
        proj_read = sem("proj_read")
        proj_hi_done = sem("proj_hi_done")
        proj_ready = sem("proj_ready")
        scores_full = sem("scores_full")
        scored = sem("scored")
        exp_done = sem("exp_done")
        inv_done = sem("inv_done")
        pv_done = sem("pv_done")
        z_done = sem("z_done")
        wo_done = sem("wo_done")
        y_biased = sem("y_biased")
        x2_done = sem("x2_done")
        rt_hi_done, rt_ready = sem("rt_hi_done"), sem("rt_ready")
        routing = sem("routing")
        gates_exped = sem("gates_exped")
        sum_read = sem("sum_read")
        ids_next = sem("ids_next")
        scattered = sem("scattered")
        table_math = sem("table_math")
        table_mm = sem("table_mm")
        gather_ids_in, add_ids_in = sem("gather_ids_in"), sem("add_ids_in")
        gather_done = sem("gather_done")
        xt_full, xt_hi_done, xt_ready = sem("xt_full"), sem("xt_hi_done"), sem("xt_ready")
        up_full = sem("up_full")
        gelu_hi_done = sem("gelu_hi_done")
        gelu_done = sem("gelu_done")
        act_ready = sem("act_ready")
        down_used = sem("down_used")
        y_ready = sem("y_ready")
        add_done = sem("add_done")

        block = ctx.enter_context(nc.Block())

        def bcast(ap, shape):
            return ap.to_broadcast(shape)

        def apart(engine):
            engine.nop(nofuse=True)

        @block.sync
        def _(sp):
            def two(rows, pair):
                return rows[:, bass.ds(2 * pair, 2), :]

            def load_mat(n):
                if not isinstance(n, int) or n >= 2:
                    sp.wait_ge(mat_ready, n - 1)
                    apart(sp)
                    sp.wait_ge(mat_loaded, 16 * n)
                    apart(sp)
                sp.dma_start(stage[:, bass.ds(n % 2, 1), :], expert_w[bass.ds(n, 1), :, :].rearrange("a p n -> p a n")
                             ).then_inc(mat_loaded, 16)

            def trip(i):
                if real_pair(i, 2):
                    sp.wait_ge(xn_done, 2 * i + 4)
                    apart(sp)
                    sp.dma_start(x_in[:, :, :], two(x_rows, i + 2)).then_inc(x_loaded, 16)
                    sp.wait_ge(ctx_ready, i + 2)
                    apart(sp)
                    sp.dma_start(ctxt[:, :, :], ctx_rows[:, :, bass.ds((i + 2) * TOK, TOK)]).then_inc(ctx_loaded, 16)
                if real_pair(i, -1):
                    sp.wait_ge(x2_done, i)
                    apart(sp)
                    sp.dma_start(two(out_rows, i - 1), x2[:, :, :]).then_inc(x2_stored, 16)
                    if real_pair(i, 0):
                        sp.dma_start(x_res[:, :, :], two(x_rows, i)).then_inc(res_loaded, 16)
                    sp.wait_ge(x2n_done, 2 * i)
                    apart(sp)
                    sp.dma_start(two(normed_rows, i - 1), x2n[:, :, :]).then_inc(normed_stored, 16)
                if real_pair(i, 2):
                    sp.wait_ge(penalty_ready, i + 2)
                    apart(sp)
                    sp.dma_start(mask_in[:, :, :], two(mask_rows, i + 2)).then_inc(mask_loaded, 16)
                if not isinstance(i, int) or i + 2 < EARLY:
                    load_mat(i + 2)

            sp.dma_start(x_in[:, :, :], x_rows[:, 0:2, :]).then_inc(x_loaded, 16)
            sp.dma_start(attn_stage[:, 0, :], attn_w[0, :, :]).then_inc(attn_loaded[0], 16)
            sp.dma_start(ctxt[:, :, :], ctx_rows[:, :, 0:TOK]).then_inc(ctx_loaded, 16)
            sp.dma_start(bq_raw[:, :], bq_t).then_inc(small_loaded, 16)
            sp.dma_start(bk_col[:, :], bk_t).then_inc(small_loaded, 16)
            sp.dma_start(bv_row[:, :], bcast(bv, [P, HD])).then_inc(small_loaded, 16)
            sp.dma_start(bo_row[:, :], bcast(bo, [P, D])).then_inc(small_loaded, 16)
            sp.dma_start(rt[:, :, :], router.rearrange("(c p) e -> p c e", p=P)).then_inc(small_loaded, 16)
            for m in range(1, 3):
                sp.dma_start(attn_stage[:, m, :], attn_w[m, :, :]).then_inc(attn_loaded[m], 16)
            sp.dma_start(mask_in[:, :, :], mask_rows[:, 0:2, :]).then_inc(mask_loaded, 16)
            sp.dma_start(attn_stage[:, 3, :], attn_w[3, :, :]).then_inc(attn_loaded[3], 16)
            sp.dma_start(x_res[:, :, :], x_rows[:, 0:2, :]).then_inc(res_loaded, 16)
            sp.wait_ge(xn_done, 2)
            sp.dma_start(x_in[:, :, :], x_rows[:, 2:4, :]).then_inc(x_loaded, 16)
            sp.wait_ge(ctx_ready, 1)
            sp.dma_start(ctxt[:, :, :], ctx_rows[:, :, TOK:2 * TOK]).then_inc(ctx_loaded, 16)
            load_mat(0)
            sp.wait_ge(mat_loaded, 16)
            load_mat(1)
            sp.wait_ge(penalty_ready, 1)
            sp.dma_start(mask_in[:, :, :], mask_rows[:, 2:4, :]).then_inc(mask_loaded, 16)
            trip(0)
            with sp.Fori(1, PAIRS - 2) as i:
                trip(i)
            for i in range(PAIRS - 2, PAIRS + 1):
                trip(i)

            def entries(t):
                apart(sp)
                first = sp.value_load(table[0:1, bass.ds(t, 1)], min_val=0, max_val=ALL_TILES - 1) * TOK
                return lists[bass.ds(first, TOK), :].rearrange("(b p) c -> p b c", p=SEQ)

            def load_gather_ids(t):
                sp.wait_ge(gather_ids_in, 16 * t)
                apart(sp)
                sp.wait_ge(gather_done, 32 * (t - 1))
                src = entries(t)
                sp.dma_start(gather_ids[:, bass.ds(t % 2, 1), :, :].rearrange("p a b c -> p (a b) c"), src
                             ).then_inc(gather_ids_in, 16)

            def tile(t):
                if not isinstance(t, int) or t + 2 < TILES:
                    load_gather_ids(t + 2)
                if not isinstance(t, int) or t >= 1:
                    if not isinstance(t, int) or t >= 2:
                        sp.wait_ge(add_done, 32 * (t - 1))
                    sp.dma_start(add_ids[:, :, :], entries(t - 1)).then_inc(add_ids_in, 16)

            sp.wait_ge(table_math, TABLE_STEPS)
            sp.wait_ge(scattered, 16 * 2 * EXPERTS * PAIRS)
            for t in range(2):
                if t == 1:
                    sp.wait_ge(gather_ids_in, 16)
                sp.dma_start(gather_ids[:, t, :, :], entries(t)).then_inc(gather_ids_in, 16)
            load_mat(EARLY)
            tile(0)
            tile(1)
            with sp.Fori(2, TILES - 2) as t:
                tile(t)
            for t in range(TILES - 2, TILES + 1):
                tile(t)
            sp.wait_ge(add_done, 32 * TILES)
            sp.wait_ge(x2_stored, 16 * PAIRS)

        @block.tensor
        def _(pe):
            def three(dst, left_hi, left_lo, right_hi, right_lo, first, last, check=False):
                pe.matmul(dst, left_hi, right_hi, start=first, stop=False, skip_group_check=check)
                pe.matmul(dst, left_hi, right_lo, start=False, stop=False, skip_group_check=check)
                return pe.matmul(dst, left_lo, right_hi, start=False, stop=last, skip_group_check=check)

            def scores(i, g):
                pe.wait_ge(proj_ready, 3 * (HG * i + g) + 2)
                pe.wait_ge(scored, 8 * (HG * i + g))
                for b in range(2):
                    for j in range(GH // 2):
                        c = GH // 2 * g + j
                        for half_row in range(2):
                            part = slice(DK * half_row, DK * half_row + DK)
                            tok = slice(SEQ * b, SEQ * b + SEQ)
                            last = three(score_bank[half_row][:, (2 * b + j) * SEQ:(2 * b + j + 1) * SEQ],
                                         qt_hi[part, c, tok], qt_lo[part, c, tok],
                                         kt_hi[part, c, tok], kt_lo[part, c, tok], True, True)
                last.then_inc(scores_full, 1)

            def open_t(i, g, kind):
                n = t_use(i, g, kind)
                if not isinstance(n, int) or n >= 2:
                    pe.wait_ge(t_lo_done, n - 1)
                return trans_bank[t_bank(i, g, kind)]

            def z_transpose(i, g):
                dst = open_t(i, g, "z")
                pe.wait_ge(z_done, HG * i + g - 1)
                for b in range(2):
                    for j in range(2):
                        last = pe.transpose(dst[:, (2 * b + j) * P:(2 * b + j + 1) * P],
                                            z[:, b, 2 * j:2 * j + 2, :].rearrange("p a d -> p (a d)"), ident[:, :])
                last.then_inc(t_full, 1)

            def p_transpose(i, g, b):
                dst = open_t(i, g, f"p{b}")
                pe.wait_ge(exp_done, 8 * (HG * i + g - 1) + 4 * b + 4)
                for j in range(GH):
                    last = pe.transpose(dst[:, j * SEQ:(j + 1) * SEQ], probs[:, (g - 1) % 2, b, j, :], ident[:, :])
                last.then_inc(t_full, 1)

            def x_transpose(dst, src, done):
                for b in range(2):
                    for c in range(DC):
                        last = pe.transpose(dst[:, (c * 2 + b) * P:(c * 2 + b + 1) * P],
                                            src[:, b, c * P:(c + 1) * P], ident[:, :])
                last.then_inc(done, 1)

            def wo(i, g):
                gg = (g - 2) % HG
                pe.wait_ge(t_lo_done, t_use(i, g, "z") + 1)
                if gg == 0:
                    if not isinstance(i, int):
                        pe.wait_ge(y_biased, i)
                    elif i > 0:
                        pe.wait_ge(y_biased, i)
                    else:
                        pe.wait_ge(w_ready, 4)
                for j in range(2):
                    c = 2 * gg + j
                    for b in range(2):
                        w = slice(c * D, (c + 1) * D)
                        last = three(y_bank[:, b * D:(b + 1) * D], zt_hi[:, b, j, :], zt_lo[:, b, j, :],
                                     w_hi[:, 3, w], w_lo[:, 3, w], c == 0 and b == 0, c == CHUNKS - 1, True)
                last.then_inc(wo_done, 1)

            def pv(i, g):
                if not isinstance(i, int) or real(i, g - 2):
                    pe.wait_ge(z_done, HG * i + g - 1)
                pe.wait_ge(proj_ready, 3 * (HG * i + g))
                for b in range(2):
                    pe.wait_ge(t_lo_done, t_use(i, g, f"p{b}") + 1)
                    for j in range(GH):
                        h = GH * ((g - 1) % HG) + j
                        v = slice(h * DK, (h + 1) * DK)
                        last = three(z_bank[:, (GH * b + j) * DK:(GH * b + j + 1) * DK], pt_hi[:, b, j, :],
                                     pt_lo[:, b, j, :], v_hi[:, b, v], v_lo[:, b, v], True, True)
                    last.then_inc(pv_done, 1)

            def project(n_step, gg, kind, first_pair=False):
                use = n_step * 3 + kind
                if not isinstance(use, int) or use >= 2:
                    pe.wait_ge(proj_read, use - 1)
                dst = proj_bank[(3 * gg + kind) % 2]
                if gg == 0:
                    it = (n_step + 0) // HG if isinstance(n_step, int) else None
                    if kind == 0:
                        pe.wait_ge(t_lo_done, project.x_use)
                    if kind == 1:
                        pe.wait_ge(ctx_ready, project.pair + 1)
                    if isinstance(n_step, int) and n_step == 0:
                        pe.wait_ge(w_ready, kind + 1)
                for n in range(2):
                    for c in range(DC):
                        if kind == 2:
                            w = slice(c * HD + gg * GH * DK, c * HD + (gg + 1) * GH * DK)
                            tok = slice(n * SEQ, (n + 1) * SEQ)
                            last = three(dst[:, n * 256:(n + 1) * 256], ctxt_hi[:, c, tok], ctxt_lo[:, c, tok],
                                         w_hi[:, 2, w], w_lo[:, 2, w], c == 0, c == DC - 1)
                        else:
                            w = slice(c * HD + (2 * gg + n) * P, c * HD + (2 * gg + n + 1) * P)
                            hi, lo = (xnt_hi, xnt_lo) if kind == 0 else (ctxt_hi, ctxt_lo)
                            last = three(dst[:, n * 256:(n + 1) * 256], w_hi[:, kind, w], w_lo[:, kind, w],
                                         hi[:, c, :], lo[:, c, :], c == 0, c == DC - 1)
                last.then_inc(proj_full, 1)

            def logits(i, g):
                dst = open_t(i, g, "logits")
                pe.wait_ge(t_lo_done, t_use(i, 2, "x2") + 1)
                if isinstance(i, int) and i == 1:
                    pe.wait_ge(rt_ready, 1)
                for b in range(2):
                    tok = slice(b * SEQ, (b + 1) * SEQ)
                    for c in range(DC):
                        last = three(dst[:, b * EXPERTS:(b + 1) * EXPERTS], x2t_hi[:, c, tok],
                                     x2t_lo[:, c, tok], rt_hi[:, c, :], rt_lo[:, c, :], c == 0, c == DC - 1)
                last.then_inc(t_full, 1)

            def ranks(i, g):
                dst = open_t(i, g, "ranks")
                pe.wait_ge(routing, ROUTE_STEPS * (i - 1) + ROUTE_PICKED)
                for b in range(2):
                    part = dst[:, b * EXPERTS:(b + 1) * EXPERTS]
                    pe.matmul(part, ones[:, :], picked_sum[:, :], start=True, stop=False)
                    if b == 1:
                        pe.matmul(part, ones[:, :], picked[:, 0, :], start=False, stop=False)
                    last = pe.matmul(part, before[:, :], picked[:, b, :], start=False, stop=True)
                last.then_inc(t_full, 1)

            def slot(i, g):
                ahead = (g + 3) % HG
                if real(i, g + 3):
                    project.pair = i + 1 if g else i
                    project.x_use = t_use(i, 0, "xn") + 1 if ahead == 0 else None
                if real(i, g):
                    scores(i, g)
                if real(i, g - 2):
                    z_transpose(i, g)
                if "logits" in bank_uses(i, g):
                    logits(i, g)
                if real(i, g + 3):
                    project(HG * i + g + 3, ahead, 0)
                if real(i, g - 1):
                    p_transpose(i, g, 0)
                if real(i, g - 2):
                    wo(i, g)
                if real(i, g - 1):
                    p_transpose(i, g, 1)
                if real(i, g + 3):
                    project(HG * i + g + 3, ahead, 1)
                if real(i, g - 1):
                    pv(i, g)
                if real(i, g + 3):
                    project(HG * i + g + 3, ahead, 2)
                if "xn" in bank_uses(i, g):
                    dst = open_t(i, g, "xn")
                    pe.wait_ge(xn_done, 2 * (i + 2))
                    x_transpose(dst, xn, t_full)
                if "x2" in bank_uses(i, g):
                    dst = open_t(i, g, "x2")
                    pe.wait_ge(x2n_done, 2 * i)
                    x_transpose(dst, x2n, t_full)
                if "ranks" in bank_uses(i, g):
                    ranks(i, g)

            pe.wait_ge(ident_ready, 1)
            pe.wait_ge(xn_done, 2)
            x_transpose(trans_bank[0], xn, t_full)
            for s in range(3):
                project.pair, project.x_use = 0, 1
                for kind in range(3):
                    project(s, s, kind)
            for g in range(HG):
                slot(0, g)
            with pe.Fori(1, PAIRS - 1) as i:
                for g in range(HG):
                    slot(i, g)
            for i in range(PAIRS - 1, PAIRS + 1):
                for g in range(HG):
                    slot(i, g)

            pe.wait_ge(table_math, 1)
            pe.wait_ge(t_lo_done, t_use(PAIRS, 3, "ranks") + 1)
            pe.matmul(table_bank[0:ALL_TILES, 0:1], pick_wide[:, :, :].rearrange("p e j -> p (e j)"), ones[:, 0:1],
                      start=True, stop=False)
            pe.matmul(table_bank[0:ALL_TILES, 0:1], base_row[:, :, :].rearrange("p e j -> p (e j)"), ones[0:1, 0:1],
                      start=False, stop=True).then_inc(table_mm, 1)
            pe.wait_ge(table_math, 2)
            pe.matmul(table_bank[0:ALL_TILES, 0:1], before[0:ALL_TILES, 0:ALL_TILES], is_real[:, :],
                      start=True, stop=True)
            pe.matmul(table_bank[0:ALL_TILES, 1:2], ones[0:ALL_TILES, 0:ALL_TILES], is_real[:, :],
                      start=True, stop=True).then_inc(table_mm, 1)
            pe.wait_ge(table_math, 7)
            pe.matmul(table_bank[0:1, 0:ALL_TILES], tile_col16[:, :], one_hot[:, :],
                      start=True, stop=True).then_inc(table_mm, 1)

            def base_of(t):
                number = pe.value_load(table[0:1, bass.ds(t, 1)], min_val=0, max_val=ALL_TILES - 1)
                expert = pe.snap(number // LIST_TILES)
                return expert, pe.snap(expert * (4 * MAT))

            def gathered_transpose(t):
                pe.wait_ge(gather_done, 32 * (t + 1))
                if not isinstance(t, int) or t > 0:
                    pe.wait_ge(xt_ready, t)
                src = gathered[:, bass.ds(t % 2, 1), :, :].rearrange("p a b d -> p (a b) d")
                x_transpose(xt_bank, src, xt_full)

            def up_product(t, q, expert, base):
                if isinstance(t, int):
                    if 4 * t + q >= 4:
                        pe.wait_ge(gelu_done, 4 * t + q - 3)
                else:
                    pe.wait_ge(gelu_done, 4 * t + (q - 3))
                if q == 0:
                    pe.wait_ge(mat_ready, 2 * expert + 2)
                    pe.wait_ge(xt_ready, t + 1)
                side = (t % 2) * (DC * TOK)
                for n in range(2):
                    for c in range(DC):
                        col = c * HIDDEN + (2 * q + n) * P
                        last = three(up_bank[q][:, n * TOK:(n + 1) * TOK],
                                     e_flat[:, bass.ds(base + col, P)], e_flat[:, bass.ds(base + (MAT + col), P)],
                                     xt_hi[:, bass.ds(side + c * TOK, TOK)], xt_lo[:, bass.ds(side + c * TOK, TOK)],
                                     c == 0, c == DC - 1)
                last.then_inc(up_full, 1)

            def down_product(t, q, base):
                pe.wait_ge(act_ready, 4 * t + (q + 1))
                if q == 0 and (not isinstance(t, int) or t > 0):
                    pe.wait_ge(y_ready, 2 * t)
                for n in range(2):
                    for sub in range(2):
                        tok = slice(sub * SEQ, (sub + 1) * SEQ)
                        col = 2 * MAT + (2 * q + n) * D
                        last = three(down_bank[sub][:, 0:D], act_hi[:, q, n, tok], act_lo[:, q, n, tok],
                                     e_flat[:, bass.ds(base + col, D)], e_flat[:, bass.ds(base + (MAT + col), D)],
                                     q == 0 and n == 0, q == 3 and n == 1)
                last.then_inc(down_used, 1)

            pe.wait_ge(table_math, TABLE_STEPS)
            gathered_transpose(0)
            expert, base = base_of(0)
            for q in range(4):
                up_product(0, q, expert, base)
                if q == 1:
                    gathered_transpose(1)
                if q >= 2:
                    down_product(0, q - 2, base)

            def tile(t, last_base):
                expert, base = base_of(t)
                up_product(t, 0, expert, base)
                down_product(t - 1, 2, last_base)
                up_product(t, 1, expert, base)
                down_product(t - 1, 3, last_base)
                gathered_transpose(t + 1)
                up_product(t, 2, expert, base)
                down_product(t, 0, base)
                up_product(t, 3, expert, base)
                down_product(t, 1, base)
                return base

            with pe.Fori(0, (TILES - 2) // 2) as two:
                _, last_base = base_of(2 * two)
                last_base = tile(2 * two + 1, last_base)
                tile(2 * two + 2, last_base)
            _, last_base = base_of(TILES - 3)
            last_base = tile(TILES - 2, last_base)
            expert, base = base_of(TILES - 1)
            for q in range(4):
                up_product(TILES - 1, q, expert, base)
                down_product(TILES - 2 + q // 2, (q + 2) % 4, (last_base, base)[q // 2])
            down_product(TILES - 1, 2, base)
            down_product(TILES - 1, 3, base)

        @block.scalar
        def _(act):
            def t_high(i, g, kind, dst):
                n = t_use(i, g, kind)
                act.wait_ge(t_full, n + 1)
                act.activation(dst, trans_bank[t_bank(i, g, kind)][:, :].rearrange("p (a b c) -> p a b c", a=2, b=dst.shape[2]),
                               ACT.Copy).then_inc(t_hi_done, 1)

            def exponentials(i, g, b, heads=range(GH)):
                par = g % 2
                for j in heads:
                    n = GH * b + j
                    act.wait_ge(scored, 8 * (HG * i + g) + n + 1)
                    act.activation(probs[:, par, b, j, :], probs[:, par, b, j, :], ACT.Exp,
                                   bias=low[:, par, n:n + 1], scale=-1.0,
                                   accum_out=total[:, par, n:n + 1]).then_inc(exp_done, 1)

            def probs_high(i, g, b):
                if not isinstance(i, int) or HG * i + g - 1 >= 1:
                    act.wait_ge(pv_done, 2 * (HG * i + g - 2) + b + 1)
                act.wait_ge(t_full, t_use(i, g, f"p{b}") + 1)
                act.activation(pt_hi[:, b, :, :].rearrange("p a b -> p (a b)"), trans_bank[t_bank(i, g, f"p{b}")][:, :],
                               ACT.Copy).then_inc(t_hi_done, 1)

            def mat_scale(n):
                if isinstance(n, int) and n == 0:
                    act.wait_ge(w_ready, 4)
                act.wait_ge(mat_loaded, 16 * (n + 1))
                src = stage[:, bass.ds(n % 2, 1), :].rearrange("p a n -> p (a n)")
                act.activation(src, src, ACT.Copy, scale=W_SCALE).then_inc(mat_scaled, 1)

            def mat_high(n):
                src = stage[:, bass.ds(n % 2, 1), :].rearrange("p a n -> p (a n)")
                act.wait_ge(mat_scaled, n + 1)
                act.activation(e_flat[:, bass.ds(n * (2 * MAT), MAT)], src, ACT.Copy).then_inc(mat_hi_done, 1)

            def proj_high(n_step, gg, kind):
                act.wait_ge(proj_read, 3 * n_step + (kind + 1))
                if kind == 2:
                    dst = v_hi[:, :, gg * GH * DK:(gg + 1) * GH * DK]
                else:
                    dst = (qt_hi, kt_hi)[kind][:, 2 * gg:2 * gg + 2, :]
                act.activation(dst, proj_f[:, kind, :].rearrange("p (a n) -> p a n", a=2),
                               ACT.Copy).then_inc(proj_hi_done, 1)

            def ctx_high(pair):
                act.wait_ge(ctx_loaded, 16 * (pair + 1))
                if not isinstance(pair, int) or pair > 0:
                    act.wait_ge(proj_full, 12 * pair)
                act.activation(ctxt_hi[:, :, :], ctxt[:, :, :], ACT.Copy).then_inc(ctx_hi_done, 1)

            def slot(i, g):
                if real(i, g - 2):
                    if not isinstance(i, int) or HG * i + g - 2 >= 1:
                        act.wait_ge(wo_done, HG * i + g - 2)
                    t_high(i, g, "z", zt_hi[:, :, :, :])
                if real(i, g):
                    exponentials(i, g, 0, range(0, 2))
                if real(i, g - 1):
                    probs_high(i, g, 0)
                if real(i, g):
                    exponentials(i, g, 0, range(2, GH))
                if real(i, g + 3):
                    proj_high(HG * i + g + 3, (g + 3) % HG, 0)
                if real(i, g - 1):
                    probs_high(i, g, 1)
                if real(i, g):
                    exponentials(i, g, 1)
                if real(i, g + 3):
                    proj_high(HG * i + g + 3, (g + 3) % HG, 1)
                if "logits" in bank_uses(i, g):
                    act.wait_ge(routing, ROUTE_STEPS * (i - 1) + ROUTE_SHIFTED)
                    act.activation(weight[:, :, :], shifted[:, :, :], ACT.Exp, scale=1.0 / W_SCALE).then_inc(gates_exped, 1)
                if "xn" in bank_uses(i, g):
                    t_high(i, g, "xn", xnt_hi[:, :, :].rearrange("p c (b t) -> p c b t", b=2))
                if "x2" in bank_uses(i, g):
                    t_high(i, g, "x2", x2t_hi[:, :, :].rearrange("p c (b t) -> p c b t", b=2))
                if real(i, g + 3):
                    proj_high(HG * i + g + 3, (g + 3) % HG, 2)
                if "xn" in bank_uses(i, g):
                    ctx_high(i + 1)
                for n in early_mats(i, g):
                    mat_scale(n)
                    mat_high(n)

            def weight_high(m):
                act.wait_ge(attn_loaded[m], 16)
                act.activation(w_hi[:, m, :], attn_stage[:, m, :], ACT.Copy, scale=W_SCALE).then_inc(w_hi_done, 1)

            weight_high(0)
            ctx_high(0)
            act.wait_ge(t_full, 1)
            act.activation(xnt_hi[:, :, :].rearrange("p c t -> p (c t)"), trans_bank[0][:, :], ACT.Copy).then_inc(t_hi_done, 1)
            weight_high(1)
            proj_high(0, 0, 0)
            weight_high(2)
            proj_high(0, 0, 1)
            proj_high(0, 0, 2)
            weight_high(3)
            for s in range(1, 3):
                for kind in range(3):
                    proj_high(s, s, kind)
            act.wait_ge(small_loaded, 80)
            act.activation(rt_hi[:, :, :], rt[:, :, :], ACT.Copy, scale=W_SCALE).then_inc(rt_hi_done, 1)
            for g in range(HG):
                slot(0, g)
            with act.Fori(1, PAIRS - 1) as i:
                for g in range(HG):
                    slot(i, g)
            for i in range(PAIRS - 1, PAIRS + 1):
                for g in range(HG):
                    slot(i, g)

            def gelu(t, q):
                act.wait_ge(up_full, 4 * t + (q + 1))
                if isinstance(t, int) and t == 0:
                    if q >= 2:
                        act.wait_ge(act_ready, q - 1)
                else:
                    act.wait_ge(down_used, 4 * t + (q - 3))
                    act.wait_ge(act_ready, 4 * t + (q - 1))
                flat = up_bank[q][:, :].rearrange("p (n t) -> p n t", n=2)
                act.activation(act_hi[:, q, :, :], flat, ACT.Gelu_apprx_tanh, scale=1.0 / W_SCALE).then_inc(gelu_hi_done, 1)
                act.activation(act_f[:, q % 2, :, :], flat, ACT.Gelu_apprx_tanh, scale=1.0 / W_SCALE).then_inc(gelu_done, 1)

            def xt_high(t):
                act.wait_ge(xt_full, t + 1)
                act.activation(xt_hi[:, bass.ds((t % 2) * (DC * TOK), DC * TOK)], xt_bank[:, :],
                               ACT.Copy).then_inc(xt_hi_done, 1)

            def tile(t):
                for q in range(4):
                    gelu(t, q)
                    if q == 1 and (not isinstance(t, int) or t + 1 < TILES):
                        xt_high(t + 1)

            xt_high(0)
            tile(0)

            def late_mat(m, more):
                n = m + EARLY
                mat_scale(n)
                if more:
                    act.wait_ge(mat_ready, n)
                    act.dma_start(stage[:, bass.ds((n + 1) % 2, 1), :],
                                  expert_w[bass.ds(n + 1, 1), :, :].rearrange("a p n -> p a n")).then_inc(mat_loaded, 16)
                tile(2 * m + 1)
                mat_high(n)
                tile(2 * m + 2)

            with act.Fori(0, LATE_MATS - 1) as m:
                late_mat(m, True)
            late_mat(LATE_MATS - 1, False)
            with act.Fori(2 * LATE_MATS + 1, TILES - 1) as t:
                tile(t)
            tile(TILES - 1)

        @block.vector
        def _(dve):
            def t_low(i, g, kind, hi, lo):
                dve.wait_ge(t_hi_done, hi_use(i, g, kind) + 1)
                dve.tensor_tensor(lo, trans_bank[t_bank(i, g, kind)][:, :].rearrange("p (a b c) -> p a b c", a=2, b=2)
                                  if len(lo.shape) == 4 else trans_bank[t_bank(i, g, kind)][:, :],
                                  hi, ALU.subtract).then_inc(t_lo_done, 1)

            def mask_scores(i, g, b):
                par = g % 2
                if b == 0:
                    dve.wait_ge(scores_full, HG * i + g + 1)
                    if not isinstance(i, int) or HG * i + g >= 2:
                        dve.wait_ge(t_full, t_use(*((i, g - 1) if g else (i - 1, HG - 1)), "p1") + 1)
                    if g == 0:
                        dve.wait_ge(penalty_ready, i + 1)
                    apart(dve)
                for j in range(GH):
                    n = GH * b + j
                    src = score_bank[j % 2][:, (2 * b + j // 2) * SEQ:(2 * b + j // 2 + 1) * SEQ]
                    dve.tensor_tensor_reduce(out=probs[:, par, b, j, :], in0=src, in1=penalty[:, b, :],
                                             scale=1.0, scalar=MASKED, op0=ALU.add, op1=ALU.min,
                                             accum_out=low[:, par, n:n + 1]).then_inc(scored, 1)

            def proj_read_out(n_step, gg, kind):
                dve.wait_ge(proj_full, 3 * n_step + (kind + 1))
                if not isinstance(n_step, int) or n_step >= 1:
                    dve.wait_ge(proj_ready, 3 * n_step + (kind - 2))
                src = proj_bank[(3 * gg + kind) % 2][:, :].rearrange("p (a n) -> p a n", a=2)
                if kind == 2:
                    bias = bcast(bv_row[:, gg * 256:(gg + 1) * 256].rearrange("p (a n) -> p a n", a=1), [P, 2, 256])
                else:
                    cols = (bq_neg, bk_col)[kind][:, 2 * gg:2 * gg + 2].rearrange("p (a n) -> p a n", n=1)
                    bias = bcast(cols, [P, 2, 256])
                dve.scalar_tensor_tensor(out=proj_f[:, kind, :].rearrange("p (a n) -> p a n", a=2), in0=src,
                                         scalar=Q_SCALE if kind == 0 else 1.0 / W_SCALE, in1=bias,
                                         op0=ALU.mult, op1=ALU.add).then_inc(proj_read, 1)

            def statistics(src, bn, mv, bn_done, mv_done, count):
                for b in range(2):
                    dve.bn_stats(bn[:, b, :], src[:, b, :]).then_inc(bn_done, 1)
                dve.wait_ge(bn_done, 2 * count + 2)
                apart(dve)
                for b in range(2):
                    dve.bn_aggr(mv[:, b, :], bn[:, b, :]).then_inc(mv_done, 1)

            def normalise(dst, src, mv, rs, rs_done, done, count):
                dve.wait_ge(rs_done, count + 1)
                for b in range(2):
                    dve.tensor_scalar(dst[:, b, :], src[:, b, :], mv[:, b, 0:1], rs[:, b:b + 1],
                                      ALU.subtract, ALU.mult).then_inc(done, 1)

            def residual(i):
                dve.wait_ge(wo_done, HG * i)
                dve.scalar_tensor_tensor(out=y_bias[:, :, :], in0=y_bank[:, :].rearrange("p (b d) -> p b d", b=2),
                                         scalar=1.0 / W_SCALE,
                                         in1=bcast(bo_row[:, :].rearrange("p (a n) -> p a n", a=1), [P, 2, D]),
                                         op0=ALU.mult, op1=ALU.add).then_inc(y_biased, 1)
                dve.wait_ge(y_biased, i)
                dve.wait_ge(res_loaded, 16 * i)
                if not isinstance(i, int) or i >= 2:
                    dve.wait_ge(x2_stored, 16 * (i - 1))
                dve.tensor_tensor(x2[:, :, :], x_res[:, :, :], y_bias[:, :, :], ALU.add).then_inc(x2_done, 1)
                dve.wait_ge(x2_done, i)
                apart(dve)
                statistics(x2, bn2, mv2, bn2_done, mv2_done, i - 1)

            def link(pair, number, ins):
                ins.then_inc(routing, 1)
                dve.wait_ge(routing, ROUTE_STEPS * pair + number)

            def wide(ap, shape, axis):
                return bcast(ap.unsqueeze(axis), shape)

            def route_shift(i, g):
                pair, full = i - 1, [P, 2, EXPERTS]
                dve.wait_ge(t_full, t_use(i, g, "logits") + 1)
                dve.tensor_copy(logit[:, :, :], trans_bank[t_bank(i, g, "logits")][:, 0:2 * EXPERTS]
                                .rearrange("p (b e) -> p b e", b=2)).then_inc(t_lo_done, 1)
                dve.wait_ge(t_lo_done, t_use(i, g, "logits") + 1)
                apart(dve)
                link(pair, 1, dve.tensor_reduce(top[:, :], logit[:, :, :], axis=AX_X, op=ALU.max))
                link(pair, ROUTE_SHIFTED, dve.tensor_tensor(shifted[:, :, :], logit[:, :, :], wide(top[:, :], full, 2),
                                                            ALU.subtract))

            def route_pick(i):
                pair, full = i - 1, [P, 2, EXPERTS, EXPERTS]
                link(pair, 3, dve.tensor_tensor(lead[:, :, :, :], wide(logit[:, :, :], full, 2),
                                                wide(logit[:, :, :], full, 3), ALU.subtract))
                flat = [a[:, :, :, :].rearrange("p b e f -> p (b e f)") for a in (lead, tie, tied)]
                link(pair, 4, dve.scalar_tensor_tensor(out=flat[2], in0=flat[0], scalar=0.0, in1=flat[1],
                                                       op0=ALU.is_equal, op1=ALU.mult))
                link(pair, 5, dve.scalar_tensor_tensor(out=flat[0], in0=flat[0], scalar=0.0, in1=flat[2],
                                                       op0=ALU.is_gt, op1=ALU.add))
                link(pair, 6, dve.tensor_reduce(rank[:, :, :].rearrange("p b e -> p (b e)"),
                                                lead[:, :, :, :].rearrange("p b e f -> p (b e) f"), axis=AX_X, op=ALU.add))
                link(pair, ROUTE_PICKED, dve.tensor_scalar(picked[:, :, :], rank[:, :, :], float(TOPK) - 0.5, None, ALU.is_lt))

            def route_place(i, g):
                pair = i - 1
                dve.wait_ge(gates_exped, i)
                link(pair, 8, dve.scalar_tensor_tensor(out=chosen[:, :, :], in0=rank[:, :, :], scalar=float(TOPK) - 0.5,
                                                       in1=weight[:, :, :], op0=ALU.is_lt, op1=ALU.mult))
                link(pair, 9, dve.tensor_reduce(mass[:, :], chosen[:, :, :], axis=AX_X, op=ALU.add))
                link(pair, 10, dve.reciprocal(inv_mass[:, :], mass[:, :]))
                if not isinstance(i, int) or i >= 2:
                    dve.wait_ge(scattered, 16 * 2 * EXPERTS * (i - 1))
                link(pair, 11, dve.tensor_tensor(entry[:, :, :, 1].bitcast(F32), chosen[:, :, :],
                                                 wide(inv_mass[:, :], [P, 2, EXPERTS], 2), ALU.mult))
                dve.wait_ge(ids_next, i)
                link(pair, 12, dve.scalar_tensor_tensor(out=place[:, :, :], in0=picked[:, :, :], scalar=0.0,
                                                        in1=wide(from_end[:, :], [P, 2, EXPERTS], 2),
                                                        op0=ALU.is_equal, op1=ALU.mult))
                link(pair, 13, dve.tensor_tensor(place[:, :, :], place[:, :, :], list_base[:, :, :], ALU.add))
                dve.wait_ge(t_full, t_use(i, g, "ranks") + 1)
                dve.tensor_tensor(slot_of[:, :, :], trans_bank[t_bank(i, g, "ranks")][:, 0:2 * EXPERTS]
                                  .rearrange("p (b e) -> p b e", b=2), place[:, :, :], ALU.add).then_inc(t_lo_done, 1)
                for b in range(2):
                    link(pair, 14 + b, dve.tensor_tensor(picked_sum[:, :], picked_sum[:, :], picked[:, b, :], ALU.add))

            def slot(i, g):
                if "xn" in bank_uses(i, g):
                    dve.wait_ge(x_loaded, 16 * (i + 2))
                    apart(dve)
                    statistics(x_in, bn1, mv1, bn1_done, mv1_done, i + 1)
                if real(i, g):
                    mask_scores(i, g, 0)
                if real(i, g - 2):
                    t_low(i, g, "z", zt_hi[:, :, :, :], zt_lo[:, :, :, :])
                if "logits" in bank_uses(i, g):
                    route_shift(i, g)
                if real(i, g):
                    if "logits" in bank_uses(i, g):
                        apart(dve)
                    mask_scores(i, g, 1)
                if real(i, g + 3):
                    proj_read_out(HG * i + g + 3, (g + 3) % HG, 0)
                if real(i, g - 1):
                    s = HG * i + g - 1
                    for b in range(2):
                        t_low(i, g, f"p{b}", pt_hi[:, b, :, :].rearrange("p a b -> p (a b)"),
                              pt_lo[:, b, :, :].rearrange("p a b -> p (a b)"))
                if "xn" in bank_uses(i, g):
                    normalise(xn, x_in, mv1, rs1, rs1_done, xn_done, i + 1)
                if "x2" in bank_uses(i, g):
                    if not isinstance(i, int) or i >= 2:
                        dve.wait_ge(normed_stored, 16 * (i - 1))
                    normalise(x2n, x2, mv2, rs2, rs2_done, x2n_done, i - 1)
                if "logits" in bank_uses(i, g):
                    route_pick(i)
                if real(i, g + 3):
                    proj_read_out(HG * i + g + 3, (g + 3) % HG, 1)
                if real(i, g - 1):
                    dve.wait_ge(exp_done, 8 * s + 8)
                    dve.reciprocal(inv[:, :], total[:, (g - 1) % 2, :]).then_inc(inv_done, 1)
                    dve.wait_ge(pv_done, 2 * s + 2)
                    dve.wait_ge(inv_done, s + 1)
                    dve.tensor_tensor(z[:, :, :, :].rearrange("p b h d -> p (b h) d"),
                                      z_bank[:, :].rearrange("p (h d) -> p h d", d=DK),
                                      bcast(inv[:, :].rearrange("p (h n) -> p h n", n=1), [P, 2 * GH, DK]),
                                      ALU.mult).then_inc(z_done, 1)
                if g == 1 and real_pair(i, -1):
                    residual(i)
                if real(i, g + 3):
                    proj_read_out(HG * i + g + 3, (g + 3) % HG, 2)
                if "xn" in bank_uses(i, g):
                    t_low(i, g, "xn", xnt_hi[:, :, :].rearrange("p c (b t) -> p c b t", b=2),
                          xnt_lo[:, :, :].rearrange("p c (b t) -> p c b t", b=2))
                if "x2" in bank_uses(i, g):
                    t_low(i, g, "x2", x2t_hi[:, :, :].rearrange("p c (b t) -> p c b t", b=2),
                          x2t_lo[:, :, :].rearrange("p c (b t) -> p c b t", b=2))
                if "ranks" in bank_uses(i, g):
                    route_place(i, g)

            def weight_low(m):
                dve.wait_ge(w_hi_done, m + 1)
                dve.scalar_tensor_tensor(out=w_lo[:, m, :], in0=attn_stage[:, m, :], scalar=W_SCALE, in1=w_hi[:, m, :],
                                         op0=ALU.mult, op1=ALU.subtract).then_inc(w_ready, 1)

            dve.memset(half[:, :], -0.5).then_inc(half_set, 1)
            dve.memset(picked_sum[:, :], 0.0).then_inc(const16_ready, 1)
            dve.memset(ones[:, :], 1.0).then_inc(const16_ready, 1)
            dve.wait_ge(x_loaded, 16)
            statistics(x_in, bn1, mv1, bn1_done, mv1_done, 0)
            dve.wait_ge(small_loaded, 80)
            dve.tensor_scalar(bq_neg[:, :], bq_raw[:, :], Q_SCALE * W_SCALE, None, ALU.mult).then_inc(bq_ready, 1)
            normalise(xn, x_in, mv1, rs1, rs1_done, xn_done, 0)
            weight_low(0)
            dve.wait_ge(t_hi_done, 1)
            dve.tensor_tensor(xnt_lo[:, :, :].rearrange("p c t -> p (c t)"), trans_bank[0][:, :],
                              xnt_hi[:, :, :].rearrange("p c t -> p (c t)"), ALU.subtract).then_inc(t_lo_done, 1)
            dve.wait_ge(bq_ready, 1)
            proj_read_out(0, 0, 0)
            weight_low(1)
            proj_read_out(0, 0, 1)
            weight_low(2)
            proj_read_out(0, 0, 2)
            weight_low(3)
            for s in range(1, 3):
                for kind in range(3):
                    proj_read_out(s, s, kind)
            dve.wait_ge(const_ready, 1)
            dve.tensor_copy(tile_col16[:, :], tile_col[:, :]).then_inc(const16_ready, 1)
            dve.tensor_copy(base_row[:, :, :], lead[0:1, 0, :, :]).then_inc(const16_ready, 1)
            dve.wait_ge(rt_hi_done, 1)
            dve.scalar_tensor_tensor(out=rt_lo[:, :, :], in0=rt[:, :, :], scalar=W_SCALE, in1=rt_hi[:, :, :],
                                     op0=ALU.mult, op1=ALU.subtract).then_inc(rt_ready, 1)
            for i in range(2):
                for g in range(HG):
                    slot(i, g)
            with dve.Fori(2, PAIRS - 1) as i:
                for g in range(HG):
                    slot(i, g)
            for i in range(PAIRS - 1, PAIRS + 1):
                for g in range(HG):
                    slot(i, g)

            def table_step(number, ins):
                ins.then_inc(table_math, 1)
                dve.wait_ge(table_math, number)

            earlier, all_real, place_if_not, extra, spare, at = (order[:, k:k + 1] for k in range(6))
            table_step(1, dve.tensor_copy(pick_wide[:, :, :], wide(picked_sum[:, :], [P, EXPERTS, LIST_TILES], 2)))
            dve.wait_ge(table_mm, 1)
            table_step(2, dve.tensor_tensor(is_real[:, :], table_bank[0:ALL_TILES, 0:1], start_col[:, :], ALU.is_gt))
            dve.wait_ge(table_mm, 2)
            table_step(3, dve.tensor_copy(order[:, 0:2], table_bank[0:ALL_TILES, 0:2]))
            table_step(4, dve.scalar_tensor_tensor(out=place_if_not, in0=earlier, scalar=-2.0, in1=all_real,
                                                   op0=ALU.mult, op1=ALU.add))
            table_step(5, dve.tensor_tensor(extra, place_if_not, tile_col[:, :], ALU.add))
            table_step(6, dve.scalar_tensor_tensor(out=spare, in0=is_real[:, :], scalar=0.0, in1=extra,
                                                   op0=ALU.is_equal, op1=ALU.mult))
            dve.tensor_tensor(at, spare, earlier, ALU.add).then_inc(inv_done, 1)
            dve.wait_ge(inv_done, STEPS + 1)
            table_step(7, dve.tensor_scalar(one_hot[:, :], tile_row[:, :], at, None, ALU.is_equal))
            dve.wait_ge(table_mm, 3)
            table_step(TABLE_STEPS, dve.tensor_copy(table[:, :], table_bank[0:1, 0:ALL_TILES]))

            def gelu_low(t, q):
                dve.wait_ge(gelu_done, 4 * t + (q + 1))
                dve.tensor_tensor(act_lo[:, q, :, :], act_f[:, q % 2, :, :], act_hi[:, q, :, :],
                                  ALU.subtract).then_inc(act_ready, 1)

            def xt_low(t):
                dve.wait_ge(xt_hi_done, t + 1)
                side = bass.ds((t % 2) * (DC * TOK), DC * TOK)
                dve.tensor_tensor(xt_lo[:, side], xt_bank[:, :], xt_hi[:, side], ALU.subtract).then_inc(xt_ready, 1)

            def gated(t):
                dve.wait_ge(down_used, 4 * t + 4)
                dve.wait_ge(add_ids_in, 16 * (t + 1))
                if not isinstance(t, int) or t >= 1:
                    dve.wait_ge(add_done, 32 * t)
                for sub in range(2):
                    dve.tensor_scalar(y_out[:, sub, :], down_bank[sub][:, 0:D], add_ids[:, sub, 1:2].bitcast(F32),
                                      1.0 / W_SCALE, ALU.mult, ALU.mult).then_inc(y_ready, 1)

            xt_low(0)
            gelu_low(0, 0)
            gelu_low(0, 1)
            xt_low(1)
            gelu_low(0, 2)
            gelu_low(0, 3)
            with dve.Fori(1, TILES - 1) as t:
                gelu_low(t, 0)
                gelu_low(t, 1)
                gated(t - 1)
                xt_low(t + 1)
                gelu_low(t, 2)
                gelu_low(t, 3)
            gelu_low(TILES - 1, 0)
            gelu_low(TILES - 1, 1)
            gated(TILES - 2)
            gelu_low(TILES - 1, 2)
            gelu_low(TILES - 1, 3)
            gated(TILES - 1)

        @block.gpsimd
        def _(pool):
            def rstd(mv, ve, rs, mv_done, ve_done, rs_done, count):
                pool.wait_ge(mv_done, 2 * count + 2)
                apart(pool)
                pool.tensor_scalar(ve[:, :], mv[:, :, 1], EPS, None, ALU.add).then_inc(ve_done, 1)
                pool.wait_ge(ve_done, count + 1)
                pool.tensor_tensor(rs[:, :], ve[:, :], half[:, :], ALU.pow).then_inc(rs_done, 1)

            def mask_penalty(pair):
                pool.wait_ge(mask_loaded, 16 * (pair + 1))
                if not isinstance(pair, int) or pair > 0:
                    pool.wait_ge(scored, 8 * HG * pair)
                apart(pool)
                pool.tensor_scalar(penalty[:, :, :], mask_in[:, :, :], 0.0, MASKED,
                                   ALU.is_equal, ALU.mult).then_inc(penalty_ready, 1)

            def proj_low(n_step, gg, kind):
                pool.wait_ge(proj_hi_done, 3 * n_step + (kind + 1))
                if kind == 2:
                    cols = slice(gg * GH * DK, (gg + 1) * GH * DK)
                    hi, lo = v_hi[:, :, cols], v_lo[:, :, cols]
                else:
                    cols = slice(2 * gg, 2 * gg + 2)
                    hi, lo = (qt_hi, kt_hi)[kind][:, cols, :], (qt_lo, kt_lo)[kind][:, cols, :]
                pool.tensor_tensor(lo, proj_f[:, kind, :].rearrange("p (a n) -> p a n", a=2), hi,
                                   ALU.subtract).then_inc(proj_ready, 1)

            def ctx_low(pair):
                pool.wait_ge(ctx_hi_done, pair + 1)
                pool.tensor_tensor(ctxt_lo[:, :, :], ctxt[:, :, :], ctxt_hi[:, :, :],
                                   ALU.subtract).then_inc(ctx_ready, 1)

            def mat_low(n):
                pool.wait_ge(mat_hi_done, n + 1)
                apart(pool)
                pool.tensor_tensor(e_flat[:, bass.ds(n * (2 * MAT) + MAT, MAT)],
                                   stage[:, bass.ds(n % 2, 1), :].rearrange("p a n -> p (a n)"),
                                   e_flat[:, bass.ds(n * (2 * MAT), MAT)], ALU.subtract).then_inc(mat_ready, 1)

            def scatter(pair, part):
                pool.wait_ge(t_lo_done, scatter.use + 1)
                apart(pool)
                for n in part:
                    b, e = n // EXPERTS, n % EXPERTS
                    pool.indirect_dma_start(out=lists, out_offset=bass.IndirectOffsetOnAxis(ap=slot_of[:, b, e:e + 1], axis=0),
                                            in_=entry[:, b, e, :], in_offset=None).then_inc(scattered, 16)

            def slot(i, g):
                if "xn" in bank_uses(i, g):
                    rstd(mv1, ve1, rs1, mv1_done, ve1_done, rs1_done, i + 1)
                if real(i, g + 3):
                    for kind in range(3):
                        proj_low(HG * i + g + 3, (g + 3) % HG, kind)
                if "xn" in bank_uses(i, g):
                    ctx_low(i + 1)
                if g == 1 and real_pair(i, -1):
                    rstd(mv2, ve2, rs2, mv2_done, ve2_done, rs2_done, i - 1)
                if g < 3 and real_pair(i, -2):
                    scatter.use = t_use(i - 1, 3, "ranks")
                    scatter(i - 2, (range(0, 6), range(6, 11), range(11, 16))[g])
                if g == HG - 1 and real_pair(i, -1):
                    if isinstance(i, int) and i == 1:
                        pool.wait_ge(const_ready, 1)
                        pool.engine_nop().then_inc(ids_next, 1)
                    else:
                        pool.wait_ge(scattered, 16 * 2 * EXPERTS * (i - 1))
                        pool.wait_ge(routing, ROUTE_STEPS * (i - 1))
                        apart(pool)
                        pool.tensor_scalar(from_end[:, :], from_end[:, :], -float(TOK), None, ALU.add)
                        pool.tensor_scalar(entry[:, :, :, 0], entry[:, :, :, 0], float(TOK), None,
                                           ALU.add).then_inc(ids_next, 1)
                if g == HG - 1 and real_pair(i, 1):
                    mask_penalty(i + 1)
                for n in early_mats(i, g):
                    mat_low(n)

            pool.memset(ident[:, :], 0.0).then_inc(ident_zero, 1)
            pool.wait_ge(ident_zero, 1)
            pool.affine_select(out=ident[:, :], in_=ident[:, :], compare_op=ALU.not_equal, fill=1.0, base=0,
                               pattern=[[-1, P]], channel_multiplier=1).then_inc(ident_ready, 1)
            for ap, pattern, base, per_partition in (
                    (list_base[:, :, :], [[0, 2], [TOKENS, EXPERTS]], 0, 0),
                    (from_end[:, :], [[-SEQ, 2]], TOKENS - 1, -1),
                    (entry[:, :, :, 0], [[SEQ, 2], [0, EXPERTS]], 0, 1),
                    (tile_col[:, :], [[0, 1]], 0, 1),
                    (start_col[:, :], [[0, 1]], 0, TOK),
                    (tile_row[:, :], [[1, ALL_TILES]], 0, 0),
                    (lead[0:1, 0, :, :], [[TOKENS, EXPERTS], [0, LIST_TILES]], 0, 0)):
                pool.iota(ap, pattern=pattern, base=base, channel_multiplier=per_partition,
                          allow_small_or_imprecise_dtypes=True)
            pool.memset(tie[:, :, :, :], 1.0)
            pool.memset(before[:, :], 1.0).then_inc(const_raw, 1)
            pool.wait_ge(const_raw, 1)
            pool.affine_select(out=tie[:, :, :, :], in_=tie[:, :, :, :], compare_op=ALU.is_gt, fill=0.0, base=0,
                               pattern=[[0, 2], [1, EXPERTS], [-1, EXPERTS]], channel_multiplier=0)
            pool.affine_select(out=before[:, :], in_=before[:, :], compare_op=ALU.is_gt, fill=0.0, base=0,
                               pattern=[[1, P]], channel_multiplier=-1).then_inc(const_ready, 1)
            pool.wait_ge(half_set, 1)
            rstd(mv1, ve1, rs1, mv1_done, ve1_done, rs1_done, 0)
            ctx_low(0)
            for kind in range(3):
                proj_low(0, 0, kind)
            for s in range(1, 3):
                for kind in range(3):
                    proj_low(s, s, kind)
            mask_penalty(0)
            for i in range(2):
                for g in range(HG):
                    slot(i, g)
            with pool.Fori(2, PAIRS - 1) as i:
                for g in range(HG):
                    slot(i, g)
            for i in range(PAIRS - 1, PAIRS + 2):
                for g in range(HG):
                    slot(i, g)

            def gather(t, part):
                pool.wait_ge(gather_ids_in, 16 * (t + 1))
                if not isinstance(t, int) or t > 1:
                    pool.wait_ge(xt_full, t - 1)
                if not isinstance(t, int) or t > 0:
                    pool.wait_ge(gather_done, 32 * t)
                apart(pool)
                for sub in range(2):
                    pool.indirect_dma_start(out=gathered[:, part, sub, :], out_offset=None, in_=normed,
                                            in_offset=bass.IndirectOffsetOnAxis(ap=gather_ids[:, part, sub, 0:1], axis=0)
                                            ).then_inc(gather_done, 16)

            def add(t):
                pool.wait_ge(y_ready, 2 * t + 2)
                if not isinstance(t, int) or t > 0:
                    pool.wait_ge(add_done, 32 * t)
                apart(pool)
                for sub in range(2):
                    pool.indirect_dma_start(out=out_flat, out_offset=bass.IndirectOffsetOnAxis(ap=add_ids[:, sub, 0:1], axis=0),
                                            in_=y_out[:, sub, :], in_offset=None, compute_op=ALU.add).then_inc(add_done, 16)

            pool.wait_ge(normed_stored, 16 * PAIRS)
            pool.wait_ge(x2_stored, 16 * PAIRS)
            for t in range(3):
                gather(t, t % 2)
            with pool.Fori(0, LATE_MATS) as m:
                gather(2 * m + 3, 1)
                add(2 * m)
                gather(2 * m + 4, 0)
                mat_low(m + EARLY)
                add(2 * m + 1)
            with pool.Fori(LATE_MATS, (TILES - 3) // 2) as two:
                for side in range(2):
                    t = 2 * two + (1 + side)
                    gather(t + 2, 1 - side)
                    add(t - 1)
            for t in range(TILES - 2, TILES + 1):
                if t + 2 < TILES:
                    gather(t + 2, t % 2)
                add(t - 1)


ROUTE_SHIFTED, ROUTE_PICKED, ROUTE_STEPS = 2, 7, 15
TABLE_STEPS = 8


def early_mats(i, g):
    if isinstance(i, int) and i == 0:
        return {2: [0], 3: [1]}.get(g, [])
    if isinstance(i, int) and i == PAIRS - 1:
        return {1: [PAIRS], 3: [PAIRS + 1]}.get(g, [])
    return [i + 1] if g == 3 and not (isinstance(i, int) and i >= PAIRS) else []


_ORDER = ["x", "ctx_t", "mask", "attn_w", "bq_t", "bk_t", "bv", "bo", "router", "expert_w"]


def kernel(x, ctx_1024, mask_BxSxS2_ik1, L0_xattn_WQ_w, L0_xattn_WQ_b, L0_xattn_WK_w, L0_xattn_WK_b,
           L0_xattn_WV_w, L0_xattn_WV_b, L0_xattn_WO_w, L0_xattn_WO_b, L0_ffn_router_w, L0_ffn_up_w, L0_ffn_down_w):
    import numpy as np
    import concourse.bacc as bacc
    from concourse.bass_utils import run_bass_kernel_spmd

    def t(a):
        return np.ascontiguousarray(np.asarray(a).T)

    def by_partition(w):
        w = np.asarray(w)
        return np.ascontiguousarray(w.reshape(-1, P, w.shape[1]).transpose(1, 0, 2)).reshape(P, -1)

    up, down = np.asarray(L0_ffn_up_w), np.asarray(L0_ffn_down_w)
    laid = {
        "x": np.asarray(x),
        "ctx_t": t(np.asarray(ctx_1024).reshape(BATCH * SEQ, D)),
        "mask": np.asarray(mask_BxSxS2_ik1),
        "attn_w": np.stack([by_partition(t(w)) for w in (L0_xattn_WQ_w, L0_xattn_WK_w, L0_xattn_WV_w, L0_xattn_WO_w)]),
        "bq_t": t(np.asarray(L0_xattn_WQ_b).reshape(CHUNKS, P)),
        "bk_t": t(np.asarray(L0_xattn_WK_b).reshape(CHUNKS, P)),
        "bv": np.asarray(L0_xattn_WV_b).reshape(1, HD),
        "bo": np.asarray(L0_xattn_WO_b).reshape(1, D),
        "router": np.asarray(L0_ffn_router_w),
        "expert_w": np.stack([by_partition(w[e]) for e in range(EXPERTS) for w in (up, down)]),
    }
    nc = bacc.Bacc("TRN2", target_bir_lowering=False, num_devices=1)
    arrays, args = {}, []
    for name in _ORDER:
        a = np.ascontiguousarray(laid[name])
        arrays[f"in_{name}"] = a
        args.append(nc.dram_tensor(f"in_{name}", a.shape, mybir.dt.from_np(a.dtype), kind="ExternalInput").ap())
    out = nc.dram_tensor("out", (BATCH, SEQ, D), F32, kind="ExternalOutput").ap()
    xattn_ffn(nc, *args, out)
    r = run_bass_kernel_spmd(nc, [arrays], core_ids=[0])
    return r.results[0]["out"]
```

```python
from contextlib import ExitStack

import concourse.bass as bass
from concourse import mybir

P = 128
F32, F16, I32 = mybir.dt.float32, mybir.dt.float16, mybir.dt.int32
ALU = mybir.AluOpType
ACT = mybir.ActivationFunctionType
AX_X = mybir.AxisListType.X

BATCH, SEQ, D = 16, 128, 256
HEADS, DK = 16, 64
HD = HEADS * DK
EXPERTS, TOPK, HIDDEN = 8, 4, 1024
DC = D // P
CHUNKS = HD // P
HC = HIDDEN // P
PAIRS = BATCH // 2
HG = 4
GH = HEADS // HG
STEPS = PAIRS * HG
TOK = 2 * SEQ
TOKENS = BATCH * SEQ
LIST_TILES = TOKENS // TOK
ALL_TILES = EXPERTS * LIST_TILES
TILES = (TOPK * TOKENS + EXPERTS * (TOK - 1)) // TOK
MAT = 2048
MATS = 2 * EXPERTS
EARLY = 10
LATE_MATS = MATS - EARLY
W_SCALE = 32.0
Q_SCALE = -1.0 / (W_SCALE * DK ** 0.5)
MASKED = 1.0e30
EPS = 1e-5


def real(i, offset):
    return not isinstance(i, int) or 0 <= HG * i + offset < STEPS


def real_pair(i, offset):
    return not isinstance(i, int) or 0 <= i + offset < PAIRS


def ranks_at_once(i):
    return isinstance(i, int) and PAIRS - 1 <= i <= PAIRS


SPLIT_USES = ("z", "p0", "p1", "xn", "x2")


def bank_uses(i, group):
    uses = []
    if real(i, group - 2):
        uses.append("z")
    if real(i, group - 1):
        uses += ["p0", "p1"]
    if group == 3 and real_pair(i, -1):
        uses.append("logits")
    if group == 3 and ranks_at_once(i):
        uses.append("ranks")
    if group == 0 and real_pair(i, 1):
        uses.append("xn")
    if group == 0 and real_pair(i, -2) and not ranks_at_once(i - 1):
        uses.append("ranks")
    if group == 2 and real_pair(i, -1):
        uses.append("x2")
    return uses


def use_number(i, group, kind, kinds):
    if isinstance(i, int):
        before = 1
        for s in range(HG * i + group):
            before += sum(k in kinds for k in bank_uses(s // HG, s % HG))
        mine = bank_uses(i, group)
        return before + sum(k in kinds for k in mine[:mine.index(kind)])
    per_trip = sum(k in kinds for g in range(HG) for k in bank_uses(2, g))
    return i * per_trip + (use_number(2, group, kind, kinds) - 2 * per_trip)


def t_use(i, group, kind):
    return use_number(i, group, kind, SPLIT_USES + ("logits", "ranks"))


def hi_use(i, group, kind):
    return use_number(i, group, kind, SPLIT_USES)


def t_bank(i, group, kind):
    return t_use(i if isinstance(i, int) else 2, group, kind) % 2


def xattn_ffn(nc, x, ctx_t, mask, attn_w, bq_t, bk_t, bv_t, bo, router, expert_w, out):
    assert sum(len(bank_uses(2, g)) for g in range(HG)) % 2 == 0
    x_rows = x.rearrange("b s d -> s b d")
    out_rows = out.rearrange("b s d -> s b d")
    mask_rows = mask.rearrange("b q k -> q b k")
    ctx_rows = ctx_t.rearrange("(c p) t -> p c t", p=P)
    lists = nc.dram_tensor("lists", (EXPERTS * TOKENS, 2), I32, kind="Internal").ap()
    normed = nc.dram_tensor("normed", (TOKENS, D), F32, kind="Internal").ap()
    normed_rows = normed.rearrange("(b s) d -> s b d", s=SEQ)
    out_flat = out.rearrange("b s d -> (b s) d")

    ctx = ExitStack()
    with ctx:
        def sb(name, shape, dt):
            return ctx.enter_context(nc.sbuf_tensor(name, shape, dt))

        def sem(name):
            return ctx.enter_context(nc.semaphore(name))

        e_w = sb("e_w", [P, MATS, 2, MAT], F16)
        e_flat = e_w[:, :, :, :].rearrange("p m h n -> p (m h n)")
        stage = sb("stage", [P, 2, MAT], F32)
        w_hi, w_lo = e_w[:, EARLY:EARLY + 4, 0, :], e_w[:, EARLY:EARLY + 4, 1, :]
        attn_stage = e_flat[:, 0:4 * 2 * MAT].bitcast(F32).rearrange("p (m n) -> p m n", m=4)
        qt_hi, qt_lo, kt_hi, kt_lo = (e_w[:, EARLY + 4 + m, h, :].rearrange("p (c t) -> p c t", t=TOK)
                                      for m in range(2) for h in range(2))
        v_hi = sb("v_hi", [P, 2, HD], F16)
        v_lo = sb("v_lo", [P, 2, HD], F16)
        ident = sb("ident", [P, P], F32)
        x_res = sb("x_res", [P, 2, D], F32)
        x2t_hi = sb("x2t_hi", [P, DC, TOK], F16)
        x2t_lo = sb("x2t_lo", [P, DC, TOK], F16)
        xnt_hi = sb("xnt_hi", [P, DC, TOK], F16)
        xnt_lo = sb("xnt_lo", [P, DC, TOK], F16)
        ctxt = sb("ctxt", [P, DC, TOK], F32)
        ctxt_hi = sb("ctxt_hi", [P, DC, TOK], F16)
        ctxt_lo = sb("ctxt_lo", [P, DC, TOK], F16)
        proj_f = sb("proj_f", [P, 2, 512], F32)
        mask_in = sb("mask_in", [P, 2, SEQ], I32)
        penalty = sb("penalty", [P, 2, SEQ], F32)
        x_in = sb("x_in", [P, 2, D], F32)
        x2 = sb("x2", [P, 2, D], F32)
        probs = sb("probs", [P, 2, 2, GH, SEQ], F32)
        pt = sb("pt", [P, 2, 2, GH, SEQ], F16)
        pt_hi, pt_lo = pt[:, 0, :, :, :], pt[:, 1, :, :, :]
        z = sb("z", [P, 2, GH, DK], F32)
        zt_hi = sb("zt_hi", [P, 2, 2, SEQ], F16)
        zt_lo = sb("zt_lo", [P, 2, 2, SEQ], F16)
        rows = sb("rows", [P, 2, 2, D], F32)
        xn, x2n = rows[:, 0, :, :], rows[:, 1, :, :]
        y_bias = sb("y_bias", [P, 2, D], F32)
        bq_raw = sb("bq_raw", [P, CHUNKS], F32)
        bq_neg = sb("bq_neg", [P, CHUNKS], F32)
        bk_col = sb("bk_col", [P, CHUNKS], F32)
        bv_col = sb("bv_col", [P, CHUNKS], F32)
        bo_row = sb("bo_row", [P, D], F32)
        low = sb("low", [P, 2, 2 * GH], F32)
        total = sb("total", [P, 2, 2 * GH], F32)
        inv = sb("inv", [P, 2 * GH], F32)
        minus_half = sb("minus_half", [P, 2], F32)
        bn1 = sb("bn1", [P, 2, 6], F32)
        mv1 = sb("mv1", [P, 2, 2], F32)
        ve1 = sb("ve1", [P, 2], F32)
        rs1 = sb("rs1", [P, 2], F32)
        bn2 = sb("bn2", [P, 2, 6], F32)
        mv2 = sb("mv2", [P, 2, 2], F32)
        ve2 = sb("ve2", [P, 2], F32)
        rs2 = sb("rs2", [P, 2], F32)
        rt = sb("rt", [P, DC, EXPERTS], F32)
        rt_hi = sb("rt_hi", [P, DC, EXPERTS], F16)
        rt_lo = sb("rt_lo", [P, DC, EXPERTS], F16)
        before = sb("before", [P, P], F16)
        ones = sb("ones", [P, P], F16)
        tie = sb("tie", [P, 2, EXPERTS, EXPERTS], F32)
        list_base = sb("list_base", [P, 2, EXPERTS], F32)
        from_end = sb("from_end", [P, 2], F32)
        logit = sb("logit", [P, 2, EXPERTS], F32)
        top = sb("top", [P, 2], F32)
        shifted = sb("shifted", [P, 2, EXPERTS], F32)
        weight = sb("weight", [P, 2, EXPERTS], F32)
        lead = sb("lead", [P, 2, EXPERTS, EXPERTS], F32)
        tied = sb("tied", [P, 2, EXPERTS, EXPERTS], F32)
        rank = sb("rank", [P, 2, EXPERTS], F32)
        chosen = sb("chosen", [P, 2, EXPERTS], F32)
        picked = sb("picked", [P, 2, EXPERTS], F16)
        picked_sum = sb("picked_sum", [P, EXPERTS], F16)
        mass = sb("mass", [P, 2], F32)
        inv_mass = sb("inv_mass", [P, 2], F32)
        place = sb("place", [P, 2, EXPERTS], F32)
        slot_of = sb("slot_of", [P, 2, EXPERTS], I32)
        entry = sb("entry", [P, 2, EXPERTS, 2], I32)
        pick_wide = sb("pick_wide", [P, EXPERTS, LIST_TILES], F16)
        base_row = sb("base_row", [1, EXPERTS, LIST_TILES], F16)
        tile_col = sb("tile_col", [ALL_TILES, 1], F32)
        tile_col16 = sb("tile_col16", [ALL_TILES, 1], F16)
        tile_row = sb("tile_row", [ALL_TILES, ALL_TILES], F32)
        start_col = sb("start_col", [ALL_TILES, 1], F32)
        is_real = sb("is_real", [ALL_TILES, 1], F16)
        order = sb("order", [ALL_TILES, 6], F32)
        one_hot = sb("one_hot", [ALL_TILES, ALL_TILES], F16)
        table = sb("table", [1, ALL_TILES], I32)
        probs_flat = probs[:, :, :, :, :].rearrange("p s b h k -> p (s b h k)")
        act_f = probs_flat[:, 0:1024].rearrange("p (s n t) -> p s n t", s=2, n=2)
        act_hi = probs_flat[:, 1024:2048].bitcast(F16).rearrange("p (q n t) -> p q n t", q=4, n=2)
        act_lo = pt[:, :, :, :, :].rearrange("p a b h k -> p (a b h k)").rearrange("p (q n t) -> p q n t", q=4, n=2)
        xt_hi = v_hi[:, :, :].rearrange("p a n -> p (a n)")[:, 0:2 * DC * TOK]
        xt_lo = v_lo[:, :, :].rearrange("p a n -> p (a n)")[:, 0:2 * DC * TOK]
        y_out = proj_f[:, 0, :].rearrange("p (b d) -> p b d", b=2)
        bv_hi, bv_lo = (a[:, :, :].rearrange("p b d -> p (b d)").bitcast(F16) for a in (y_bias, x2))
        gathered = rows
        gather_ids = sb("gather_ids", [P, 2, 2, 2], I32)
        add_ids = sb("add_ids", [P, 2, 2], I32)

        bank = [ctx.enter_context(nc.psum_tensor(f"bank{n}", [P, 512], F32)) for n in range(8)]
        proj_bank, score_bank, trans_bank, z_bank, y_bank = bank[0:2], bank[2:4], bank[4:6], bank[6], bank[7]
        up_bank, down_bank, xt_bank, table_bank = bank[0:4], bank[4:6], bank[6], bank[7]

        x_loaded, res_loaded, ctx_loaded, mask_loaded = (sem(n) for n in ("x_loaded", "res_loaded", "ctx_loaded", "mask_loaded"))
        small_loaded = sem("small_loaded")
        attn_loaded = [[sem(f"attn_loaded{m}_{part}") for part in range(2)] for m in range(4)]
        qk_bias_loaded, bv_loaded = sem("qk_bias_loaded"), sem("bv_loaded")
        mat_loaded = sem("mat_loaded")
        x2_stored, normed_stored = sem("x2_stored"), sem("normed_stored")
        minus_half_set, bq_ready = sem("minus_half_set"), sem("bq_ready")
        ident_zero, ident_ready = sem("ident_zero"), sem("ident_ready")
        const_raw, const_ready, const16_ready = sem("const_raw"), sem("const_ready"), sem("const16_ready")
        penalty_ready = sem("penalty_ready")
        w_hi_done, w_ready = sem("w_hi_done"), sem("w_ready")
        mat_scaled, mat_hi_done, mat_ready = sem("mat_scaled"), sem("mat_hi_done"), sem("mat_ready")
        ctx_hi_done = sem("ctx_hi_done")
        ctx_ready = sem("ctx_ready")
        bn1_done, mv1_done, ve1_done, rs1_done, xn_done = (sem(n) for n in ("bn1_done", "mv1_done", "ve1_done", "rs1_done", "xn_done"))
        bn2_done, mv2_done, ve2_done, rs2_done, x2n_done = (sem(n) for n in ("bn2_done", "mv2_done", "ve2_done", "rs2_done", "x2n_done"))
        t_full = sem("t_full")
        t_hi_done = sem("t_hi_done")
        t_lo_done = sem("t_lo_done")
        proj_full = sem("proj_full")
        q_read, k_read, v_ready = sem("q_read"), sem("k_read"), sem("v_ready")
        proj_hi_done = sem("proj_hi_done")
        qk_ready = sem("qk_ready")
        bv_hi_done, bv_ready, bias_full, bo_ready = (sem(n) for n in ("bv_hi_done", "bv_ready", "bias_full", "bo_ready"))
        scores_full = sem("scores_full")
        scored = sem("scored")
        exp_done = sem("exp_done")
        inv_done = sem("inv_done")
        pv_done = sem("pv_done")
        z_done = sem("z_done")
        wo_done = sem("wo_done")
        y_biased = sem("y_biased")
        x2_done = sem("x2_done")
        rt_hi_done, rt_ready = sem("rt_hi_done"), sem("rt_ready")
        routing = sem("routing")
        gates_exped = sem("gates_exped")
        ids_next = sem("ids_next")
        scattered = sem("scattered")
        first_scattered = sem("first_scattered")
        table_math = sem("table_math")
        table_mm = sem("table_mm")
        gather_ids_in, add_ids_in = sem("gather_ids_in"), sem("add_ids_in")
        gather_done = sem("gather_done")
        xt_full, xt_hi_done, xt_ready = sem("xt_full"), sem("xt_hi_done"), sem("xt_ready")
        up_full = sem("up_full")
        gelu_hi_done = sem("gelu_hi_done")
        gelu_done = sem("gelu_done")
        act_ready = sem("act_ready")
        down_used = sem("down_used")
        y_ready = sem("y_ready")
        add_done = sem("add_done")

        block = ctx.enter_context(nc.Block())

        def bcast(ap, shape):
            return ap.to_broadcast(shape)

        def piece(w, m, gg):
            return w[:, m, :] if m == 3 else w[:, m, :].rearrange("p (c n) -> p c n", c=DC)[:, :, gg * GH * DK:(gg + 1) * GH * DK]

        def mat_staged(n, first, count):
            return stage[:, bass.ds(n % 2, 1), first * MAT // QUARTERS:(first + count) * MAT // QUARTERS].rearrange("p a n -> p (a n)")

        def mat_part(n, low_part, first, count):
            return e_flat[:, bass.ds(n * (2 * MAT) + (low_part * MAT + first * MAT // QUARTERS), count * MAT // QUARTERS)]

        def apart(engine):
            engine.nop(nofuse=True)

        @block.sync
        def _(sp):
            def two(rows, pair):
                return rows[:, bass.ds(2 * pair, 2), :]

            def load_mat(n):
                if not isinstance(n, int) or n >= 2:
                    sp.wait_ge(mat_ready, QUARTERS * (n - 1))
                    apart(sp)
                    sp.wait_ge(mat_loaded, 16 * n)
                    apart(sp)
                sp.dma_start(stage[:, bass.ds(n % 2, 1), :], expert_w[bass.ds(n, 1), :, :].rearrange("a p n -> p a n")
                             ).then_inc(mat_loaded, 16)

            def trip(i):
                if real_pair(i, 2):
                    sp.wait_ge(xn_done, 2 * i + 4)
                    apart(sp)
                    sp.dma_start(x_in[:, :, :], two(x_rows, i + 2)).then_inc(x_loaded, 16)
                    sp.wait_ge(ctx_ready, i + 2)
                    apart(sp)
                    sp.dma_start(ctxt[:, :, :], ctx_rows[:, :, bass.ds((i + 2) * TOK, TOK)]).then_inc(ctx_loaded, 16)
                if real_pair(i, -1):
                    sp.wait_ge(x2_done, i)
                    apart(sp)
                    sp.dma_start(two(out_rows, i - 1), x2[:, :, :]).then_inc(x2_stored, 16)
                    if real_pair(i, 0):
                        sp.dma_start(x_res[:, :, :], two(x_rows, i)).then_inc(res_loaded, 16)
                    sp.wait_ge(x2n_done, 2 * i)
                    apart(sp)
                    sp.dma_start(two(normed_rows, i - 1), x2n[:, :, :]).then_inc(normed_stored, 16)
                if real_pair(i, 2):
                    sp.wait_ge(penalty_ready, i + 2)
                    apart(sp)
                    sp.dma_start(mask_in[:, :, :], two(mask_rows, i + 2)).then_inc(mask_loaded, 16)
                if not isinstance(i, int) or i + 2 < EARLY:
                    load_mat(i + 2)

            sp.dma_start(x_in[:, :, :], x_rows[:, 0:2, :]).then_inc(x_loaded, 16)

            def load_weights(m, part):
                cols = (slice(0, GH * DK), slice(GH * DK, HD))[part]
                sp.dma_start(attn_stage[:, m, :].rearrange("p (c n) -> p c n", c=DC)[:, :, cols],
                             attn_w[m, :, :].rearrange("p (c n) -> p c n", c=DC)[:, :, cols]).then_inc(attn_loaded[m][part], 16)

            load_weights(0, 0)
            sp.dma_start(ctxt[:, :, :], ctx_rows[:, :, 0:TOK]).then_inc(ctx_loaded, 16)
            sp.dma_start(bq_raw[:, :], bq_t).then_inc(qk_bias_loaded, 16)
            load_weights(1, 0)
            sp.dma_start(bk_col[:, :], bk_t).then_inc(qk_bias_loaded, 16)
            load_weights(2, 0)
            for m in range(3):
                load_weights(m, 1)
            sp.dma_start(bv_col[:, :], bv_t).then_inc(bv_loaded, 16)
            sp.dma_start(mask_in[:, :, :], mask_rows[:, 0:2, :]).then_inc(mask_loaded, 16)
            sp.dma_start(attn_stage[:, 3, :], attn_w[3, :, :]).then_inc(attn_loaded[3][0], 16)
            sp.dma_start(bo_row[:, :], bcast(bo, [P, D])).then_inc(small_loaded, 16)
            sp.dma_start(rt[:, :, :], router.rearrange("(c p) e -> p c e", p=P)).then_inc(small_loaded, 16)
            sp.dma_start(x_res[:, :, :], x_rows[:, 0:2, :]).then_inc(res_loaded, 16)
            sp.wait_ge(xn_done, 2)
            sp.dma_start(x_in[:, :, :], x_rows[:, 2:4, :]).then_inc(x_loaded, 16)
            sp.wait_ge(ctx_ready, 1)
            sp.dma_start(ctxt[:, :, :], ctx_rows[:, :, TOK:2 * TOK]).then_inc(ctx_loaded, 16)
            load_mat(0)
            sp.wait_ge(mat_loaded, 16)
            load_mat(1)
            sp.wait_ge(penalty_ready, 1)
            sp.dma_start(mask_in[:, :, :], mask_rows[:, 2:4, :]).then_inc(mask_loaded, 16)
            trip(0)
            with sp.Fori(1, PAIRS - 2) as i:
                trip(i)
            for i in range(PAIRS - 2, PAIRS + 1):
                trip(i)

            def entries(t):
                apart(sp)
                first = sp.value_load(table[0:1, bass.ds(t, 1)], min_val=0, max_val=ALL_TILES - 1) * TOK
                return lists[bass.ds(first, TOK), :].rearrange("(b p) c -> p b c", p=SEQ)

            def load_gather_ids(t):
                sp.wait_ge(gather_ids_in, 16 * t)
                apart(sp)
                sp.wait_ge(gather_done, 32 * (t - 1))
                src = entries(t)
                sp.dma_start(gather_ids[:, bass.ds(t % 2, 1), :, :].rearrange("p a b c -> p (a b) c"), src
                             ).then_inc(gather_ids_in, 16)

            def tile(t):
                if not isinstance(t, int) or t + 2 < TILES:
                    load_gather_ids(t + 2)
                if not isinstance(t, int) or t >= 1:
                    if not isinstance(t, int) or t >= 2:
                        sp.wait_ge(add_done, 32 * (t - 1))
                    sp.dma_start(add_ids[:, :, :], entries(t - 1)).then_inc(add_ids_in, 16)

            sp.wait_ge(scattered, 16 * 2 * EXPERTS * (PAIRS - 1))
            sp.wait_ge(first_scattered, 16 * 2)
            sp.dma_start(gather_ids[:, 0, :, :], lists[0:TOK, :].rearrange("(b p) c -> p b c", p=SEQ)
                         ).then_inc(gather_ids_in, 16)
            sp.wait_ge(table_math, TABLE_STEPS)
            sp.wait_ge(scattered, 16 * 2 * (EXPERTS * PAIRS - 1))
            sp.wait_ge(gather_ids_in, 16)
            sp.dma_start(gather_ids[:, 1, :, :], entries(1)).then_inc(gather_ids_in, 16)
            load_mat(EARLY)
            tile(0)
            tile(1)
            with sp.Fori(2, TILES - 2) as t:
                tile(t)
            for t in range(TILES - 2, TILES + 1):
                tile(t)
            sp.wait_ge(add_done, 32 * TILES)
            sp.wait_ge(x2_stored, 16 * PAIRS)

        @block.tensor
        def _(pe):
            def three(dst, left_hi, left_lo, right_hi, right_lo, first, last, check=False):
                pe.matmul(dst, left_hi, right_hi, start=first, stop=False, skip_group_check=check)
                pe.matmul(dst, left_hi, right_lo, start=False, stop=False, skip_group_check=check)
                return pe.matmul(dst, left_lo, right_hi, start=False, stop=last, skip_group_check=check)

            def scores(i, g):
                pe.wait_ge(qk_ready, 2 * (HG * i + g) + 2)
                pe.wait_ge(scored, 8 * (HG * i + g))
                for b in range(2):
                    for j in range(GH // 2):
                        c = GH // 2 * g + j
                        for half_row in range(2):
                            part = slice(DK * half_row, DK * half_row + DK)
                            tok = slice(SEQ * b, SEQ * b + SEQ)
                            last = three(score_bank[half_row][:, (2 * b + j) * SEQ:(2 * b + j + 1) * SEQ],
                                         qt_hi[part, c, tok], qt_lo[part, c, tok],
                                         kt_hi[part, c, tok], kt_lo[part, c, tok], True, True)
                last.then_inc(scores_full, 1)

            def open_t(i, g, kind):
                n = t_use(i, g, kind)
                if not isinstance(n, int) or n >= 2:
                    pe.wait_ge(t_lo_done, n - 1)
                return trans_bank[t_bank(i, g, kind)]

            def z_transpose(i, g):
                dst = open_t(i, g, "z")
                pe.wait_ge(z_done, HG * i + g - 1)
                for b in range(2):
                    for j in range(2):
                        last = pe.transpose(dst[:, (2 * b + j) * P:(2 * b + j + 1) * P],
                                            z[:, b, 2 * j:2 * j + 2, :].rearrange("p a d -> p (a d)"), ident[:, :])
                last.then_inc(t_full, 1)

            def p_transpose(i, g, b):
                dst = open_t(i, g, f"p{b}")
                pe.wait_ge(exp_done, 8 * (HG * i + g - 1) + 4 * b + 4)
                for j in range(GH):
                    last = pe.transpose(dst[:, j * SEQ:(j + 1) * SEQ], probs[:, (g - 1) % 2, b, j, :], ident[:, :])
                last.then_inc(t_full, 1)

            def x_transpose(dst, src, done):
                for b in range(2):
                    for c in range(DC):
                        last = pe.transpose(dst[:, (c * 2 + b) * P:(c * 2 + b + 1) * P],
                                            src[:, b, c * P:(c + 1) * P], ident[:, :])
                last.then_inc(done, 1)

            def wo(i, g):
                gg = (g - 2) % HG
                pe.wait_ge(t_lo_done, t_use(i, g, "z") + 1)
                if gg == 0:
                    if isinstance(i, int) and i == 0:
                        pe.wait_ge(bo_ready, 1)
                    else:
                        pe.wait_ge(y_biased, i)
                for j in range(2):
                    c = 2 * gg + j
                    for b in range(2):
                        w = slice(c * D, (c + 1) * D)
                        last = three(y_bank[:, b * D:(b + 1) * D], zt_hi[:, b, j, :], zt_lo[:, b, j, :],
                                     w_hi[:, 3, w], w_lo[:, 3, w], c == 0 and b == 0, c == CHUNKS - 1, True)
                last.then_inc(wo_done, 1)

            def pv(i, g):
                if not isinstance(i, int) or real(i, g - 2):
                    pe.wait_ge(z_done, HG * i + g - 1)
                pe.wait_ge(v_ready, HG * i + g)
                for b in range(2):
                    pe.wait_ge(t_lo_done, t_use(i, g, f"p{b}") + 1)
                    for j in range(GH):
                        h = GH * ((g - 1) % HG) + j
                        v = slice(h * DK, (h + 1) * DK)
                        last = three(z_bank[:, (GH * b + j) * DK:(GH * b + j + 1) * DK], pt_hi[:, b, j, :],
                                     pt_lo[:, b, j, :], v_hi[:, b, v], v_lo[:, b, v], True, True)
                    last.then_inc(pv_done, 1)

            def project(n_step, gg, kind, first_pair=False):
                if kind == 2:
                    pe.wait_ge(q_read, n_step + 1)
                elif not isinstance(n_step, int) or n_step > 0:
                    if kind == 0:
                        pe.wait_ge(k_read, 2 * n_step)
                    else:
                        pe.wait_ge(v_ready, n_step)
                dst = proj_bank[(3 * gg + kind) % 2]
                if isinstance(n_step, int) and n_step < HG:
                    pe.wait_ge(w_ready, W_PIECES.index((kind, n_step)) + 1)
                if gg == 0:
                    if kind == 0:
                        pe.wait_ge(t_lo_done, project.x_use)
                    if kind == 1:
                        pe.wait_ge(ctx_ready, project.pair + 1)
                for n in range(2):
                    for c in range(DC):
                        if kind == 2:
                            w = slice(c * HD + gg * GH * DK, c * HD + (gg + 1) * GH * DK)
                            tok = slice(n * SEQ, (n + 1) * SEQ)
                            last = three(dst[:, n * 256:(n + 1) * 256], ctxt_hi[:, c, tok], ctxt_lo[:, c, tok],
                                         w_hi[:, 2, w], w_lo[:, 2, w], c == 0, c == DC - 1)
                        else:
                            w = slice(c * HD + (2 * gg + n) * P, c * HD + (2 * gg + n + 1) * P)
                            hi, lo = (xnt_hi, xnt_lo) if kind == 0 else (ctxt_hi, ctxt_lo)
                            last = three(dst[:, n * 256:(n + 1) * 256], w_hi[:, kind, w], w_lo[:, kind, w],
                                         hi[:, c, :], lo[:, c, :], c == 0, c == DC - 1)
                last.then_inc(proj_full, 1)

            def logits(i, g):
                dst = open_t(i, g, "logits")
                pe.wait_ge(t_lo_done, t_use(i, 2, "x2") + 1)
                if isinstance(i, int) and i == 1:
                    pe.wait_ge(rt_ready, 1)
                for b in range(2):
                    tok = slice(b * SEQ, (b + 1) * SEQ)
                    for c in range(DC):
                        last = three(dst[:, b * EXPERTS:(b + 1) * EXPERTS], x2t_hi[:, c, tok],
                                     x2t_lo[:, c, tok], rt_hi[:, c, :], rt_lo[:, c, :], c == 0, c == DC - 1)
                last.then_inc(t_full, 1)

            def ranks(i, g):
                dst = open_t(i, g, "ranks")
                pair = i - 1 if g else i - 2
                pe.wait_ge(routing, ROUTE_STEPS * pair + (ROUTE_PICKED - 1))
                for b in range(2):
                    part = dst[:, b * EXPERTS:(b + 1) * EXPERTS]
                    pe.matmul(part, ones[:, :], picked_sum[:, :], start=True, stop=False)
                    if b == 1:
                        pe.matmul(part, ones[:, :], picked[:, 0, :], start=False, stop=False)
                    last = pe.matmul(part, before[:, :], picked[:, b, :], start=False, stop=True)
                last.then_inc(t_full, 1)

            def slot(i, g):
                ahead = (g + 3) % HG
                if real(i, g + 3):
                    project.pair = i + 1 if g else i
                    project.x_use = t_use(i, 0, "xn") + 1 if ahead == 0 else None
                if real(i, g):
                    scores(i, g)
                if real(i, g - 2):
                    z_transpose(i, g)
                if real(i, g - 1):
                    p_transpose(i, g, 0)
                if real(i, g + 3):
                    project(HG * i + g + 3, ahead, 0)
                if real(i, g - 1) and not real(i, g + 3):
                    p_transpose(i, g, 1)
                if real(i, g - 2):
                    wo(i, g)
                if real(i, g - 1) and real(i, g + 3):
                    p_transpose(i, g, 1)
                if real(i, g + 3):
                    project(HG * i + g + 3, ahead, 1)
                if "logits" in bank_uses(i, g):
                    logits(i, g)
                if real(i, g - 1):
                    pv(i, g)
                if "xn" in bank_uses(i, g):
                    dst = open_t(i, g, "xn")
                    pe.wait_ge(xn_done, 2 * (i + 2))
                    x_transpose(dst, xn, t_full)
                if "x2" in bank_uses(i, g):
                    dst = open_t(i, g, "x2")
                    pe.wait_ge(x2n_done, 2 * i)
                    x_transpose(dst, x2n, t_full)
                if real(i, g + 3):
                    project(HG * i + g + 3, ahead, 2)
                if "ranks" in bank_uses(i, g):
                    ranks(i, g)

            pe.wait_ge(ident_ready, 1)
            pe.wait_ge(xn_done, 2)
            x_transpose(trans_bank[0], xn, t_full)
            for s in range(3):
                project.pair, project.x_use = 0, 1
                for kind in range(3):
                    project(s, s, kind)
            slot(0, 0)
            slot(0, 1)
            pe.wait_ge(w_ready, len(W_PIECES))
            pe.wait_ge(bv_ready, 1)
            for c in range(CHUNKS):
                col, w = slice(c * P, (c + 1) * P), slice(c * D, (c + 1) * D)
                last = three(y_bank[:, 0:D], bv_hi[:, col], bv_lo[:, col], w_hi[:, 3, w], w_lo[:, 3, w],
                             c == 0, c == CHUNKS - 1)
            last.then_inc(bias_full, 1)
            for g in range(2, HG):
                slot(0, g)
            for g in range(HG):
                slot(1, g)
            with pe.Fori(2, PAIRS - 1) as i:
                for g in range(HG):
                    slot(i, g)
            for i in range(PAIRS - 1, PAIRS + 1):
                for g in range(HG):
                    slot(i, g)

            pe.wait_ge(table_math, 1)
            pe.wait_ge(t_lo_done, t_use(PAIRS, 3, "ranks") + 1)
            pe.matmul(table_bank[0:ALL_TILES, 0:1], pick_wide[:, :, :].rearrange("p e j -> p (e j)"), ones[:, 0:1],
                      start=True, stop=False)
            pe.matmul(table_bank[0:ALL_TILES, 0:1], base_row[:, :, :].rearrange("p e j -> p (e j)"), ones[0:1, 0:1],
                      start=False, stop=True).then_inc(table_mm, 1)
            pe.wait_ge(table_math, 2)
            pe.matmul(table_bank[0:ALL_TILES, 0:1], before[0:ALL_TILES, 0:ALL_TILES], is_real[:, :],
                      start=True, stop=True)
            pe.matmul(table_bank[0:ALL_TILES, 1:2], ones[0:ALL_TILES, 0:ALL_TILES], is_real[:, :],
                      start=True, stop=True).then_inc(table_mm, 1)
            pe.wait_ge(table_math, 7)
            pe.matmul(table_bank[0:1, 0:ALL_TILES], tile_col16[:, :], one_hot[:, :],
                      start=True, stop=True).then_inc(table_mm, 1)

            def base_of(t):
                number = pe.value_load(table[0:1, bass.ds(t, 1)], min_val=0, max_val=ALL_TILES - 1)
                expert = pe.snap(number // LIST_TILES)
                return expert, pe.snap(expert * (4 * MAT))

            def gathered_transpose(t):
                pe.wait_ge(gather_done, 32 * (t + 1))
                if not isinstance(t, int) or t > 0:
                    pe.wait_ge(xt_ready, t)
                src = gathered[:, bass.ds(t % 2, 1), :, :].rearrange("p a b d -> p (a b) d")
                x_transpose(xt_bank, src, xt_full)

            def up_product(t, q, expert, base):
                if isinstance(t, int):
                    if 4 * t + q >= 4:
                        pe.wait_ge(gelu_done, 4 * t + q - 3)
                else:
                    pe.wait_ge(gelu_done, 4 * t + (q - 3))
                if q == 0:
                    pe.wait_ge(mat_ready, 2 * QUARTERS * (expert + 1))
                    pe.wait_ge(xt_ready, t + 1)
                side = (t % 2) * (DC * TOK)
                for n in range(2):
                    for c in range(DC):
                        col = c * HIDDEN + (2 * q + n) * P
                        last = three(up_bank[q][:, n * TOK:(n + 1) * TOK],
                                     e_flat[:, bass.ds(base + col, P)], e_flat[:, bass.ds(base + (MAT + col), P)],
                                     xt_hi[:, bass.ds(side + c * TOK, TOK)], xt_lo[:, bass.ds(side + c * TOK, TOK)],
                                     c == 0, c == DC - 1)
                last.then_inc(up_full, 1)

            def down_product(t, q, base):
                pe.wait_ge(act_ready, 4 * t + (q + 1))
                if q == 0 and (not isinstance(t, int) or t > 0):
                    pe.wait_ge(y_ready, 2 * t)
                for n in range(2):
                    for sub in range(2):
                        tok = slice(sub * SEQ, (sub + 1) * SEQ)
                        col = 2 * MAT + (2 * q + n) * D
                        last = three(down_bank[sub][:, 0:D], act_hi[:, q, n, tok], act_lo[:, q, n, tok],
                                     e_flat[:, bass.ds(base + col, D)], e_flat[:, bass.ds(base + (MAT + col), D)],
                                     q == 0 and n == 0, q == 3 and n == 1)
                last.then_inc(down_used, 1)

            pe.wait_ge(table_math, TABLE_STEPS)
            gathered_transpose(0)
            expert, base = base_of(0)
            for q in range(4):
                up_product(0, q, expert, base)
                if q >= 2:
                    down_product(0, q - 2, base)
            gathered_transpose(1)

            def tile(t, last_base):
                expert, base = base_of(t)
                up_product(t, 0, expert, base)
                down_product(t - 1, 2, last_base)
                up_product(t, 1, expert, base)
                down_product(t - 1, 3, last_base)
                gathered_transpose(t + 1)
                up_product(t, 2, expert, base)
                down_product(t, 0, base)
                up_product(t, 3, expert, base)
                down_product(t, 1, base)
                return base

            with pe.Fori(0, (TILES - 2) // 2) as two:
                _, last_base = base_of(2 * two)
                last_base = tile(2 * two + 1, last_base)
                tile(2 * two + 2, last_base)
            _, last_base = base_of(TILES - 3)
            last_base = tile(TILES - 2, last_base)
            expert, base = base_of(TILES - 1)
            for q in range(4):
                up_product(TILES - 1, q, expert, base)
                down_product(TILES - 2 + q // 2, (q + 2) % 4, (last_base, base)[q // 2])
            down_product(TILES - 1, 2, base)
            down_product(TILES - 1, 3, base)

        @block.scalar
        def _(act):
            def t_high(i, g, kind, dst):
                n = t_use(i, g, kind)
                act.wait_ge(t_full, n + 1)
                act.activation(dst, trans_bank[t_bank(i, g, kind)][:, :].rearrange("p (a b c) -> p a b c", a=2, b=dst.shape[2]),
                               ACT.Copy).then_inc(t_hi_done, 1)

            def exponentials(i, g, b, heads=range(GH)):
                par = g % 2
                for j in heads:
                    n = GH * b + j
                    act.wait_ge(scored, 8 * (HG * i + g) + n + 1)
                    act.activation(probs[:, par, b, j, :], probs[:, par, b, j, :], ACT.Exp,
                                   bias=low[:, par, n:n + 1], scale=-1.0,
                                   accum_out=total[:, par, n:n + 1]).then_inc(exp_done, 1)

            def probs_high(i, g, b):
                if not isinstance(i, int) or HG * i + g - 1 >= 1:
                    act.wait_ge(pv_done, 2 * (HG * i + g - 2) + b + 1)
                act.wait_ge(t_full, t_use(i, g, f"p{b}") + 1)
                act.activation(pt_hi[:, b, :, :].rearrange("p a b -> p (a b)"), trans_bank[t_bank(i, g, f"p{b}")][:, :],
                               ACT.Copy).then_inc(t_hi_done, 1)

            def mat_scale(n, first=0, count=QUARTERS):
                if first == 0:
                    act.wait_ge(mat_loaded, 16 * (n + 1))
                src = mat_staged(n, first, count)
                act.activation(src, src, ACT.Copy, scale=W_SCALE).then_inc(mat_scaled, count)

            def mat_high(n, first=0, count=QUARTERS):
                if isinstance(n, int) and n == 0:
                    act.wait_ge(w_ready, len(W_PIECES))
                act.wait_ge(mat_scaled, QUARTERS * n + (first + count))
                act.activation(mat_part(n, 0, first, count), mat_staged(n, first, count), ACT.Copy).then_inc(mat_hi_done, count)

            def keys_read_out(n_step, gg):
                act.wait_ge(proj_full, 3 * n_step + 2)
                if not isinstance(n_step, int) or n_step >= 1:
                    act.wait_ge(qk_ready, 2 * n_step)
                for n in range(2):
                    part = slice(n * TOK, (n + 1) * TOK)
                    act.activation(proj_f[:, 1, part], proj_bank[(3 * gg + 1) % 2][:, part], ACT.Identity,
                                   bias=bk_col[:, 2 * gg + n:2 * gg + n + 1], scale=1.0 / W_SCALE).then_inc(k_read, 1)

            def proj_high(n_step, gg, kind):
                if kind == 2:
                    act.wait_ge(proj_full, 3 * n_step + 3)
                    act.activation(v_hi[:, :, gg * GH * DK:(gg + 1) * GH * DK],
                                   proj_bank[(3 * gg + 2) % 2][:, :].rearrange("p (a n) -> p a n", a=2),
                                   ACT.Copy, scale=1.0 / W_SCALE).then_inc(proj_hi_done, 1)
                else:
                    if kind == 0:
                        act.wait_ge(q_read, n_step + 1)
                    else:
                        act.wait_ge(k_read, 2 * n_step + 2)
                    act.activation((qt_hi, kt_hi)[kind][:, 2 * gg:2 * gg + 2, :],
                                   proj_f[:, kind, :].rearrange("p (a n) -> p a n", a=2),
                                   ACT.Copy).then_inc(proj_hi_done, 1)

            def ctx_high(pair):
                act.wait_ge(ctx_loaded, 16 * (pair + 1))
                if not isinstance(pair, int) or pair > 0:
                    act.wait_ge(proj_full, 12 * pair)
                act.activation(ctxt_hi[:, :, :], ctxt[:, :, :], ACT.Copy).then_inc(ctx_hi_done, 1)

            def slot(i, g):
                if real(i, g - 2):
                    if not isinstance(i, int) or HG * i + g - 2 >= 1:
                        act.wait_ge(wo_done, HG * i + g - 2)
                    t_high(i, g, "z", zt_hi[:, :, :, :])
                late = g == 0 and "ranks" in bank_uses(i, g)
                if real(i, g) and not late:
                    exponentials(i, g, 0, range(0, GH // 2))
                if real(i, g - 1):
                    probs_high(i, g, 0)
                if real(i, g):
                    exponentials(i, g, 0, range(0 if late else GH // 2, GH))
                if real(i, g - 1) and late:
                    probs_high(i, g, 1)
                if real_pair(i, 0) and late:
                    mat_scale(i, g, 1)
                    mat_high(i, g, 1)
                if real(i, g + 3) and late:
                    keys_read_out(HG * i + g + 3, (g + 3) % HG)
                if real(i, g + 3):
                    proj_high(HG * i + g + 3, (g + 3) % HG, 0)
                if real(i, g - 1) and not late:
                    probs_high(i, g, 1)
                if real(i, g):
                    exponentials(i, g, 1, range(0, GH // 2))
                if "xn" in bank_uses(i, g) and late:
                    t_high(i, g, "xn", xnt_hi[:, :, :].rearrange("p c (b t) -> p c b t", b=2))
                if real(i, g):
                    exponentials(i, g, 1, range(GH // 2, GH))
                if "xn" in bank_uses(i, g) and not late:
                    t_high(i, g, "xn", xnt_hi[:, :, :].rearrange("p c (b t) -> p c b t", b=2))
                if "x2" in bank_uses(i, g):
                    t_high(i, g, "x2", x2t_hi[:, :, :].rearrange("p c (b t) -> p c b t", b=2))
                if real(i, g + 3) and not late:
                    keys_read_out(HG * i + g + 3, (g + 3) % HG)
                if real_pair(i, 0) and not late:
                    mat_scale(i, g, 1)
                if real(i, g + 3):
                    proj_high(HG * i + g + 3, (g + 3) % HG, 1)
                if real(i, g + 3):
                    proj_high(HG * i + g + 3, (g + 3) % HG, 2)
                if "xn" in bank_uses(i, g):
                    ctx_high(i + 1)
                if "logits" in bank_uses(i, g):
                    act.wait_ge(routing, ROUTE_STEPS * (i - 1) + (ROUTE_SHIFTED - 1))
                    act.activation(weight[:, :, :], shifted[:, :, :], ACT.Exp, scale=1.0 / W_SCALE).then_inc(gates_exped, 1)
                if real_pair(i, 0) and not late:
                    mat_high(i, g, 1)

            def weight_high(number):
                m, gg = W_PIECES[number]
                act.wait_ge(attn_loaded[m][min(gg, 1)], 16)
                act.activation(piece(w_hi, m, gg), piece(attn_stage, m, gg), ACT.Copy, scale=W_SCALE).then_inc(w_hi_done, 1)

            weight_high(0)
            ctx_high(0)
            weight_high(1)
            act.wait_ge(t_full, 1)
            act.activation(xnt_hi[:, :, :].rearrange("p c t -> p (c t)"), trans_bank[0][:, :], ACT.Copy).then_inc(t_hi_done, 1)
            weight_high(2)
            for use in range(9):
                weight_high(use + 3)
                if use == 1:
                    act.wait_ge(qk_bias_loaded, 32)
                if use % 3 == 1:
                    keys_read_out(use // 3, use // 3)
                proj_high(use // 3, use // 3, use % 3)
            weight_high(12)
            slot(0, 0)
            act.wait_ge(small_loaded, 32)
            act.activation(rt_hi[:, :, :], rt[:, :, :], ACT.Copy, scale=W_SCALE).then_inc(rt_hi_done, 1)
            for g in range(1, HG):
                slot(0, g)
            for g in range(HG):
                slot(1, g)
            with act.Fori(2, PAIRS - 1) as i:
                for g in range(HG):
                    slot(i, g)
            for i in range(PAIRS - 1, PAIRS + 1):
                for g in range(HG):
                    slot(i, g)
            for n in range(PAIRS, EARLY):
                mat_scale(n)
                mat_high(n)

            def gelu(t, q):
                act.wait_ge(up_full, 4 * t + (q + 1))
                if isinstance(t, int) and t == 0:
                    if q >= 2:
                        act.wait_ge(act_ready, q - 1)
                else:
                    act.wait_ge(down_used, 4 * t + (q - 3))
                    act.wait_ge(act_ready, 4 * t + (q - 1))
                flat = up_bank[q][:, :].rearrange("p (n t) -> p n t", n=2)
                act.activation(act_hi[:, q, :, :], flat, ACT.Gelu_apprx_tanh, scale=1.0 / W_SCALE).then_inc(gelu_hi_done, 1)
                act.activation(act_f[:, q % 2, :, :], flat, ACT.Gelu_apprx_tanh, scale=1.0 / W_SCALE).then_inc(gelu_done, 1)

            def xt_high(t):
                act.wait_ge(xt_full, t + 1)
                act.activation(xt_hi[:, bass.ds((t % 2) * (DC * TOK), DC * TOK)], xt_bank[:, :],
                               ACT.Copy).then_inc(xt_hi_done, 1)

            def tile(t):
                for q in range(4):
                    gelu(t, q)
                    if q == (3 if isinstance(t, int) and t == 0 else 1) and (not isinstance(t, int) or t + 1 < TILES):
                        xt_high(t + 1)

            xt_high(0)
            tile(0)

            def late_mat(m, more):
                n = m + EARLY
                mat_scale(n)
                if more:
                    act.wait_ge(mat_ready, QUARTERS * n)
                    act.dma_start(stage[:, bass.ds((n + 1) % 2, 1), :],
                                  expert_w[bass.ds(n + 1, 1), :, :].rearrange("a p n -> p a n")).then_inc(mat_loaded, 16)
                tile(2 * m + 1)
                mat_high(n)
                tile(2 * m + 2)

            with act.Fori(0, LATE_MATS - 1) as m:
                late_mat(m, True)
            late_mat(LATE_MATS - 1, False)
            with act.Fori(2 * LATE_MATS + 1, TILES - 1) as t:
                tile(t)
            tile(TILES - 1)

        @block.vector
        def _(dve):
            def t_low(i, g, kind, hi, lo):
                dve.wait_ge(t_hi_done, hi_use(i, g, kind) + 1)
                dve.tensor_tensor(lo, trans_bank[t_bank(i, g, kind)][:, :].rearrange("p (a b c) -> p a b c", a=2, b=2)
                                  if len(lo.shape) == 4 else trans_bank[t_bank(i, g, kind)][:, :],
                                  hi, ALU.subtract).then_inc(t_lo_done, 1)

            def mask_scores(i, g, b):
                par = g % 2
                if b == 0:
                    dve.wait_ge(scores_full, HG * i + g + 1)
                    if not isinstance(i, int) or HG * i + g >= 2:
                        dve.wait_ge(t_full, t_use(*((i, g - 1) if g else (i - 1, HG - 1)), "p1") + 1)
                    if g == 0:
                        dve.wait_ge(penalty_ready, i + 1)
                    apart(dve)
                for j in range(GH):
                    n = GH * b + j
                    src = score_bank[j % 2][:, (2 * b + j // 2) * SEQ:(2 * b + j // 2 + 1) * SEQ]
                    dve.tensor_tensor_reduce(out=probs[:, par, b, j, :], in0=src, in1=penalty[:, b, :],
                                             scale=1.0, scalar=MASKED, op0=ALU.add, op1=ALU.min,
                                             accum_out=low[:, par, n:n + 1]).then_inc(scored, 1)

            def proj_read_out(n_step, gg, kind):
                src = proj_bank[(3 * gg + kind) % 2][:, :].rearrange("p (a n) -> p a n", a=2)
                if kind == 2:
                    cols = slice(gg * GH * DK, (gg + 1) * GH * DK)
                    dve.wait_ge(proj_hi_done, 3 * n_step + 3)
                    dve.scalar_tensor_tensor(out=v_lo[:, :, cols], in0=src, scalar=1.0 / W_SCALE, in1=v_hi[:, :, cols],
                                             op0=ALU.mult, op1=ALU.subtract).then_inc(v_ready, 1)
                    return
                dve.wait_ge(proj_full, 3 * n_step + 1)
                if not isinstance(n_step, int) or n_step >= 1:
                    dve.wait_ge(qk_ready, 2 * n_step - 1)
                cols = bq_neg[:, 2 * gg:2 * gg + 2].rearrange("p (a n) -> p a n", n=1)
                dve.scalar_tensor_tensor(out=proj_f[:, 0, :].rearrange("p (a n) -> p a n", a=2), in0=src,
                                         scalar=Q_SCALE, in1=bcast(cols, [P, 2, TOK]),
                                         op0=ALU.mult, op1=ALU.add).then_inc(q_read, 1)

            def block_stats(src, bn, bn_done):
                for b in range(2):
                    dve.bn_stats(bn[:, b, :], src[:, b, :]).then_inc(bn_done, 1)

            def mean_variance(bn, mv, bn_done, mv_done, count):
                dve.wait_ge(bn_done, 2 * count + 2)
                apart(dve)
                for b in range(2):
                    dve.bn_aggr(mv[:, b, :], bn[:, b, :]).then_inc(mv_done, 1)

            def normalise(dst, src, mv, rs, rs_done, done, count):
                dve.wait_ge(rs_done, count + 1)
                for b in range(2):
                    dve.tensor_scalar(dst[:, b, :], src[:, b, :], mv[:, b, 0:1], rs[:, b:b + 1],
                                      ALU.subtract, ALU.mult).then_inc(done, 1)

            def y_out_of_bank(i):
                dve.wait_ge(wo_done, HG * i)
                dve.scalar_tensor_tensor(out=y_bias[:, :, :], in0=y_bank[:, :].rearrange("p (b d) -> p b d", b=2),
                                         scalar=1.0 / W_SCALE,
                                         in1=bcast(bo_row[:, :].rearrange("p (a n) -> p a n", a=1), [P, 2, D]),
                                         op0=ALU.mult, op1=ALU.add).then_inc(y_biased, 1)

            def residual(i):
                dve.wait_ge(y_biased, i)
                dve.wait_ge(res_loaded, 16 * i)
                if not isinstance(i, int) or i >= 2:
                    dve.wait_ge(x2_stored, 16 * (i - 1))
                dve.tensor_tensor(x2[:, :, :], x_res[:, :, :], y_bias[:, :, :], ALU.add).then_inc(x2_done, 1)

            def wide(ap, shape, axis):
                return bcast(ap.unsqueeze(axis), shape)

            def route(i, g, number):
                pair, full = (i - 1 if g else i - 2), [P, 2, EXPERTS]
                square = [P, 2, EXPERTS, EXPERTS]
                flat_lead, flat_tie, flat_tied = (a[:, :, :, :].rearrange("p b e f -> p (b e f)") for a in (lead, tie, tied))
                if number == 1:
                    dve.wait_ge(t_full, t_use(i, g, "logits") + 1)
                    dve.tensor_copy(logit[:, :, :], trans_bank[t_bank(i, g, "logits")][:, 0:2 * EXPERTS]
                                    .rearrange("p (b e) -> p b e", b=2)).then_inc(t_lo_done, 1)
                    return
                if number == 2:
                    dve.wait_ge(t_lo_done, t_use(i, g, "logits") + 1)
                    apart(dve)
                    step = dve.tensor_reduce(top[:, :], logit[:, :, :], axis=AX_X, op=ALU.max)
                else:
                    dve.wait_ge(routing, ROUTE_STEPS * pair + (number - 2))
                if number == ROUTE_SHIFTED:
                    step = dve.tensor_tensor(shifted[:, :, :], logit[:, :, :], wide(top[:, :], full, 2), ALU.subtract)
                if number == 4:
                    step = dve.tensor_tensor(lead[:, :, :, :], wide(logit[:, :, :], square, 2),
                                             wide(logit[:, :, :], square, 3), ALU.subtract)
                if number == 5:
                    step = dve.scalar_tensor_tensor(out=flat_tied, in0=flat_lead, scalar=0.0, in1=flat_tie,
                                                    op0=ALU.is_equal, op1=ALU.mult)
                if number == 6:
                    step = dve.scalar_tensor_tensor(out=flat_lead, in0=flat_lead, scalar=0.0, in1=flat_tied,
                                                    op0=ALU.is_gt, op1=ALU.add)
                if number == 7:
                    step = dve.tensor_reduce(rank[:, :, :].rearrange("p b e -> p (b e)"),
                                             lead[:, :, :, :].rearrange("p b e f -> p (b e) f"), axis=AX_X, op=ALU.add)
                if number == ROUTE_PICKED:
                    step = dve.tensor_scalar(picked[:, :, :], rank[:, :, :], float(TOPK) - 0.5, None, ALU.is_lt)
                if number == 9:
                    dve.wait_ge(gates_exped, pair + 1)
                    step = dve.scalar_tensor_tensor(out=chosen[:, :, :], in0=rank[:, :, :], scalar=float(TOPK) - 0.5,
                                                    in1=weight[:, :, :], op0=ALU.is_lt, op1=ALU.mult)
                if number == 10:
                    step = dve.tensor_reduce(mass[:, :], chosen[:, :, :], axis=AX_X, op=ALU.add)
                if number == 11:
                    step = dve.reciprocal(inv_mass[:, :], mass[:, :])
                if number == 12:
                    if not isinstance(pair, int) or pair >= 1:
                        dve.wait_ge(scattered, 16 * 2 * EXPERTS * pair)
                    step = dve.tensor_tensor(entry[:, :, :, 1].bitcast(F32), chosen[:, :, :],
                                             wide(inv_mass[:, :], full, 2), ALU.mult)
                if number == 13:
                    dve.wait_ge(ids_next, pair + 1)
                    step = dve.scalar_tensor_tensor(out=place[:, :, :], in0=picked[:, :, :], scalar=0.0,
                                                    in1=wide(from_end[:, :], full, 2),
                                                    op0=ALU.is_equal, op1=ALU.mult)
                if number == 14:
                    step = dve.tensor_tensor(place[:, :, :], place[:, :, :], list_base[:, :, :], ALU.add)
                if number == 15:
                    dve.wait_ge(t_full, t_use(i, g, "ranks") + 1)
                    dve.tensor_tensor(slot_of[:, :, :], trans_bank[t_bank(i, g, "ranks")][:, 0:2 * EXPERTS]
                                      .rearrange("p (b e) -> p b e", b=2), place[:, :, :], ALU.add).then_inc(t_lo_done, 1)
                if number in (15, 16):
                    step = dve.tensor_tensor(picked_sum[:, :], picked_sum[:, :], picked[:, number - 15, :], ALU.add)
                step.then_inc(routing, 1)

            def slot(i, g):
                next_x, routes, places = ("xn" in bank_uses(i, g), "logits" in bank_uses(i, g), g == 0 and "ranks" in bank_uses(i, g))
                finishes = g == 1 and real_pair(i, -1)
                ahead = HG * i + g + 3, (g + 3) % HG

                def probs_low(b):
                    t_low(i, g, f"p{b}", pt_hi[:, b, :, :].rearrange("p a b -> p (a b)"),
                          pt_lo[:, b, :, :].rearrange("p a b -> p (a b)"))

                if real(i, g) and not places:
                    mask_scores(i, g, 0)
                if real(i, g - 2):
                    t_low(i, g, "z", zt_hi[:, :, :, :], zt_lo[:, :, :, :])
                if real(i, g) and places:
                    apart(dve)
                    mask_scores(i, g, 0)
                if real(i, g - 1) and places:
                    probs_low(0)
                if next_x:
                    dve.wait_ge(x_loaded, 16 * (i + 2))
                    apart(dve)
                    block_stats(x_in, bn1, bn1_done)
                if places:
                    route(i, g, 9)
                if next_x:
                    mean_variance(bn1, mv1, bn1_done, mv1_done, i + 1)
                if real(i, g):
                    if places:
                        apart(dve)
                    mask_scores(i, g, 1)
                if real(i, g - 1) and places:
                    probs_low(1)
                if real(i, g + 3):
                    proj_read_out(*ahead, 0)
                if real(i, g - 1) and not places:
                    probs_low(0)
                    probs_low(1)
                if next_x:
                    normalise(xn, x_in, mv1, rs1, rs1_done, xn_done, i + 1)
                if places:
                    route(i, g, 10)
                if "x2" in bank_uses(i, g):
                    if not isinstance(i, int) or i >= 2:
                        dve.wait_ge(normed_stored, 16 * (i - 1))
                    normalise(x2n, x2, mv2, rs2, rs2_done, x2n_done, i - 1)
                if finishes:
                    y_out_of_bank(i)
                if routes:
                    route(i, g, 1)
                if finishes:
                    residual(i)
                if routes:
                    route(i, g, 2)
                if real(i, g - 1):
                    s = HG * i + g - 1
                    dve.wait_ge(exp_done, 8 * s + 8)
                    dve.reciprocal(inv[:, :], total[:, (g - 1) % 2, :]).then_inc(inv_done, 1)
                if routes:
                    route(i, g, ROUTE_SHIFTED)
                if places:
                    route(i, g, 11)
                if real(i, g - 1):
                    dve.wait_ge(pv_done, 2 * s + 2)
                    dve.wait_ge(inv_done, s + 1)
                    dve.tensor_tensor(z[:, :, :, :].rearrange("p b h d -> p (b h) d"),
                                      z_bank[:, :].rearrange("p (h d) -> p h d", d=DK),
                                      bcast(inv[:, :].rearrange("p (h n) -> p h n", n=1), [P, 2 * GH, DK]),
                                      ALU.mult).then_inc(z_done, 1)
                if finishes:
                    dve.wait_ge(x2_done, i)
                    apart(dve)
                    block_stats(x2, bn2, bn2_done)
                if routes:
                    route(i, g, 4)
                if finishes:
                    mean_variance(bn2, mv2, bn2_done, mv2_done, i - 1)
                if places:
                    route(i, g, 12)
                if next_x:
                    t_low(i, g, "xn", xnt_hi[:, :, :].rearrange("p c (b t) -> p c b t", b=2),
                          xnt_lo[:, :, :].rearrange("p c (b t) -> p c b t", b=2))
                if "x2" in bank_uses(i, g):
                    t_low(i, g, "x2", x2t_hi[:, :, :].rearrange("p c (b t) -> p c b t", b=2),
                          x2t_lo[:, :, :].rearrange("p c (b t) -> p c b t", b=2))
                if places:
                    for number in range(13, 17):
                        route(i, g, number)
                if real(i, g + 3):
                    proj_read_out(*ahead, 2)
                if routes:
                    for number in range(5, (16 if "ranks" in bank_uses(i, g) else ROUTE_PICKED) + 1):
                        route(i, g, number)

            def weight_low(number):
                m, gg = W_PIECES[number]
                dve.wait_ge(w_hi_done, number + 1)
                dve.scalar_tensor_tensor(out=piece(w_lo, m, gg), in0=piece(attn_stage, m, gg), scalar=W_SCALE,
                                         in1=piece(w_hi, m, gg), op0=ALU.mult, op1=ALU.subtract).then_inc(w_ready, 1)

            dve.memset(minus_half[:, :], -0.5).then_inc(minus_half_set, 1)
            dve.memset(picked_sum[:, :], 0.0).then_inc(const16_ready, 1)
            dve.memset(ones[:, :], 1.0).then_inc(const16_ready, 1)
            dve.wait_ge(x_loaded, 16)
            block_stats(x_in, bn1, bn1_done)
            mean_variance(bn1, mv1, bn1_done, mv1_done, 0)
            weight_low(0)
            dve.wait_ge(qk_bias_loaded, 32)
            dve.tensor_scalar(bq_neg[:, :], bq_raw[:, :], Q_SCALE * W_SCALE, None, ALU.mult).then_inc(bq_ready, 1)
            normalise(xn, x_in, mv1, rs1, rs1_done, xn_done, 0)
            weight_low(1)
            dve.wait_ge(t_hi_done, 1)
            dve.tensor_tensor(xnt_lo[:, :, :].rearrange("p c t -> p (c t)"), trans_bank[0][:, :],
                              xnt_hi[:, :, :].rearrange("p c t -> p (c t)"), ALU.subtract).then_inc(t_lo_done, 1)
            weight_low(2)
            dve.wait_ge(bq_ready, 1)
            rows_of_bv = bcast(bv_col[:, :].rearrange("p (c n) -> p c n", n=1), [P, CHUNKS, P])
            bv_parts = [a[:, :].rearrange("p (c n) -> p c n", c=CHUNKS) for a in (bv_hi, bv_lo)]
            for use in range(9):
                if use % 3 != 1:
                    proj_read_out(use // 3, use // 3, use % 3)
                weight_low(use + 3)
                if use == 5:
                    dve.wait_ge(bv_loaded, 16)
                    dve.tensor_scalar(bv_parts[0], rows_of_bv, W_SCALE, None, ALU.mult).then_inc(bv_hi_done, 1)
                if use == 8:
                    dve.wait_ge(bv_hi_done, 1)
                    dve.scalar_tensor_tensor(out=bv_parts[1], in0=rows_of_bv, scalar=W_SCALE, in1=bv_parts[0],
                                             op0=ALU.mult, op1=ALU.subtract).then_inc(bv_ready, 1)
            slot(0, 0)
            weight_low(12)
            slot(0, 1)
            dve.wait_ge(small_loaded, 32)
            dve.wait_ge(bias_full, 1)
            dve.scalar_tensor_tensor(out=bo_row[:, :], in0=y_bank[:, 0:D], scalar=1.0 / (W_SCALE * W_SCALE),
                                     in1=bo_row[:, :], op0=ALU.mult, op1=ALU.add).then_inc(bo_ready, 1)
            slot(0, 2)
            dve.wait_ge(const_ready, 1)
            dve.tensor_copy(tile_col16[:, :], tile_col[:, :]).then_inc(const16_ready, 1)
            dve.tensor_copy(base_row[:, :, :], lead[0:1, 0, :, :]).then_inc(const16_ready, 1)
            dve.wait_ge(rt_hi_done, 1)
            dve.scalar_tensor_tensor(out=rt_lo[:, :, :], in0=rt[:, :, :], scalar=W_SCALE, in1=rt_hi[:, :, :],
                                     op0=ALU.mult, op1=ALU.subtract).then_inc(rt_ready, 1)
            slot(0, 3)
            for g in range(HG):
                slot(1, g)
            with dve.Fori(2, PAIRS - 1) as i:
                for g in range(HG):
                    slot(i, g)
            def mat_low(n):
                dve.wait_ge(mat_ready, QUARTERS * n)
                dve.wait_ge(mat_hi_done, QUARTERS * (n + 1))
                dve.tensor_tensor(mat_part(n, 1, 0, QUARTERS), mat_staged(n, 0, QUARTERS), mat_part(n, 0, 0, QUARTERS),
                                  ALU.subtract).then_inc(mat_ready, QUARTERS)

            for g in range(HG):
                slot(PAIRS - 1, g)
            slot(PAIRS, 0)
            mat_low(PAIRS - 1)
            for g in range(1, HG):
                slot(PAIRS, g)

            def table_step(number, ins):
                ins.then_inc(table_math, 1)
                dve.wait_ge(table_math, number)

            earlier, all_real, place_if_not, extra, spare, at = (order[:, k:k + 1] for k in range(6))
            dve.wait_ge(routing, ROUTE_STEPS * PAIRS)
            table_step(1, dve.tensor_copy(pick_wide[:, :, :], wide(picked_sum[:, :], [P, EXPERTS, LIST_TILES], 2)))
            dve.wait_ge(table_mm, 1)
            table_step(2, dve.tensor_tensor(is_real[:, :], table_bank[0:ALL_TILES, 0:1], start_col[:, :], ALU.is_gt))
            dve.wait_ge(table_mm, 2)
            table_step(3, dve.tensor_copy(order[:, 0:2], table_bank[0:ALL_TILES, 0:2]))
            table_step(4, dve.scalar_tensor_tensor(out=place_if_not, in0=earlier, scalar=-2.0, in1=all_real,
                                                   op0=ALU.mult, op1=ALU.add))
            table_step(5, dve.tensor_tensor(extra, place_if_not, tile_col[:, :], ALU.add))
            table_step(6, dve.scalar_tensor_tensor(out=spare, in0=is_real[:, :], scalar=0.0, in1=extra,
                                                   op0=ALU.is_equal, op1=ALU.mult))
            dve.tensor_tensor(at, spare, earlier, ALU.add).then_inc(inv_done, 1)
            dve.wait_ge(inv_done, STEPS + 1)
            table_step(7, dve.tensor_scalar(one_hot[:, :], tile_row[:, :], at, None, ALU.is_equal))
            dve.wait_ge(table_mm, 3)
            table_step(TABLE_STEPS, dve.tensor_copy(table[:, :], table_bank[0:1, 0:ALL_TILES]))

            for n in range(PAIRS, EARLY):
                mat_low(n)

            def gelu_low(t, q):
                dve.wait_ge(gelu_done, 4 * t + (q + 1))
                dve.tensor_tensor(act_lo[:, q, :, :], act_f[:, q % 2, :, :], act_hi[:, q, :, :],
                                  ALU.subtract).then_inc(act_ready, 1)

            def xt_low(t):
                dve.wait_ge(xt_hi_done, t + 1)
                side = bass.ds((t % 2) * (DC * TOK), DC * TOK)
                dve.tensor_tensor(xt_lo[:, side], xt_bank[:, :], xt_hi[:, side], ALU.subtract).then_inc(xt_ready, 1)

            def gated(t):
                dve.wait_ge(down_used, 4 * t + 4)
                dve.wait_ge(add_ids_in, 16 * (t + 1))
                if not isinstance(t, int) or t >= 1:
                    dve.wait_ge(add_done, 32 * t)
                for sub in range(2):
                    dve.tensor_scalar(y_out[:, sub, :], down_bank[sub][:, 0:D], add_ids[:, sub, 1:2].bitcast(F32),
                                      1.0 / W_SCALE, ALU.mult, ALU.mult).then_inc(y_ready, 1)

            xt_low(0)
            for q in range(4):
                gelu_low(0, q)
            xt_low(1)
            with dve.Fori(1, TILES - 1) as t:
                gelu_low(t, 0)
                gelu_low(t, 1)
                gated(t - 1)
                xt_low(t + 1)
                gelu_low(t, 2)
                gelu_low(t, 3)
            gelu_low(TILES - 1, 0)
            gelu_low(TILES - 1, 1)
            gated(TILES - 2)
            gelu_low(TILES - 1, 2)
            gelu_low(TILES - 1, 3)
            gated(TILES - 1)

        @block.gpsimd
        def _(pool):
            def rstd(mv, ve, rs, mv_done, ve_done, rs_done, count):
                pool.wait_ge(mv_done, 2 * count + 2)
                apart(pool)
                pool.tensor_scalar(ve[:, :], mv[:, :, 1], EPS, None, ALU.add).then_inc(ve_done, 1)
                pool.wait_ge(ve_done, count + 1)
                pool.tensor_tensor(rs[:, :], ve[:, :], minus_half[:, :], ALU.pow).then_inc(rs_done, 1)

            def mask_penalty(pair):
                pool.wait_ge(mask_loaded, 16 * (pair + 1))
                if not isinstance(pair, int) or pair > 0:
                    pool.wait_ge(scored, 8 * HG * pair)
                apart(pool)
                pool.tensor_scalar(penalty[:, :, :], mask_in[:, :, :], 0.0, MASKED,
                                   ALU.is_equal, ALU.mult).then_inc(penalty_ready, 1)

            def proj_low(n_step, gg, kind):
                pool.wait_ge(proj_hi_done, 3 * n_step + (kind + 1))
                cols = slice(2 * gg, 2 * gg + 2)
                hi, lo = (qt_hi, kt_hi)[kind][:, cols, :], (qt_lo, kt_lo)[kind][:, cols, :]
                pool.tensor_tensor(lo, proj_f[:, kind, :].rearrange("p (a n) -> p a n", a=2), hi,
                                   ALU.subtract).then_inc(qk_ready, 1)

            def ctx_low(pair):
                pool.wait_ge(ctx_hi_done, pair + 1)
                pool.tensor_tensor(ctxt_lo[:, :, :], ctxt[:, :, :], ctxt_hi[:, :, :],
                                   ALU.subtract).then_inc(ctx_ready, 1)

            def mat_low(n, first=0, count=QUARTERS):
                pool.wait_ge(mat_hi_done, QUARTERS * n + (first + count))
                apart(pool)
                pool.tensor_tensor(mat_part(n, 1, first, count), mat_staged(n, first, count), mat_part(n, 0, first, count),
                                   ALU.subtract).then_inc(mat_ready, count)

            def scatter(use, part, done):
                pool.wait_ge(t_lo_done, use + 1)
                apart(pool)
                for n in part:
                    b, e = n % 2, n // 2
                    pool.indirect_dma_start(out=lists, out_offset=bass.IndirectOffsetOnAxis(ap=slot_of[:, b, e:e + 1], axis=0),
                                            in_=entry[:, b, e, :], in_offset=None).then_inc(done, 16)

            def next_ids(i):
                if isinstance(i, int) and i == 1:
                    pool.wait_ge(const_ready, 1)
                    pool.engine_nop().then_inc(ids_next, 1)
                    return
                pool.wait_ge(scattered, 16 * 2 * EXPERTS * (i - 1))
                pool.wait_ge(routing, ROUTE_STEPS * (i - 1))
                apart(pool)
                pool.tensor_scalar(from_end[:, :], from_end[:, :], -float(TOK), None, ALU.add)
                pool.tensor_scalar(entry[:, :, :, 0], entry[:, :, :, 0], float(TOK), None, ALU.add).then_inc(ids_next, 1)

            def slot(i, g):
                if "xn" in bank_uses(i, g):
                    rstd(mv1, ve1, rs1, mv1_done, ve1_done, rs1_done, i + 1)
                if g == 0 and real_pair(i, -1) and real_pair(i, 0):
                    mat_low(i - 1, 2, 2)
                if real(i, g + 3):
                    proj_low(HG * i + g + 3, (g + 3) % HG, 0)
                if g == HG - 1 and real_pair(i, -1):
                    next_ids(i)
                if g == HG - 1 and real_pair(i, 1):
                    mask_penalty(i + 1)
                if g == HG - 1 and real_pair(i, 1):
                    mat_low(i, 0, 2)
                if real(i, g + 3):
                    proj_low(HG * i + g + 3, (g + 3) % HG, 1)
                if "xn" in bank_uses(i, g):
                    ctx_low(i + 1)
                if g == 1 and real_pair(i, -1):
                    rstd(mv2, ve2, rs2, mv2_done, ve2_done, rs2_done, i - 1)
                if g < 3 and real_pair(i, -2):
                    ranked = t_use(i, 0, "ranks") if not ranks_at_once(i - 1) else t_use(i - 1, 3, "ranks")
                    shares = (range(0, 5), range(5, 10), range(10, 16))
                    if isinstance(i, int) and i == PAIRS:
                        shares = (range(0, 13), range(13, 16), range(0))
                    if shares[g]:
                        scatter(ranked, shares[g], scattered)

            pool.memset(ident[:, :], 0.0).then_inc(ident_zero, 1)
            pool.wait_ge(ident_zero, 1)
            pool.affine_select(out=ident[:, :], in_=ident[:, :], compare_op=ALU.not_equal, fill=1.0, base=0,
                               pattern=[[-1, P]], channel_multiplier=1).then_inc(ident_ready, 1)
            for ap, pattern, base, per_partition in (
                    (list_base[:, :, :], [[0, 2], [TOKENS, EXPERTS]], 0, 0),
                    (from_end[:, :], [[-SEQ, 2]], TOKENS - 1, -1),
                    (entry[:, :, :, 0], [[SEQ, 2], [0, EXPERTS]], 0, 1),
                    (tile_col[:, :], [[0, 1]], 0, 1),
                    (start_col[:, :], [[0, 1]], 0, TOK),
                    (tile_row[:, :], [[1, ALL_TILES]], 0, 0),
                    (lead[0:1, 0, :, :], [[TOKENS, EXPERTS], [0, LIST_TILES]], 0, 0)):
                pool.iota(ap, pattern=pattern, base=base, channel_multiplier=per_partition,
                          allow_small_or_imprecise_dtypes=True)
            pool.memset(tie[:, :, :, :], 1.0)
            pool.memset(before[:, :], 1.0).then_inc(const_raw, 1)
            pool.wait_ge(const_raw, 1)
            pool.memset(start_col[0:1, :], -1.0)
            pool.affine_select(out=tie[:, :, :, :], in_=tie[:, :, :, :], compare_op=ALU.is_gt, fill=0.0, base=0,
                               pattern=[[0, 2], [1, EXPERTS], [-1, EXPERTS]], channel_multiplier=0)
            pool.affine_select(out=before[:, :], in_=before[:, :], compare_op=ALU.is_gt, fill=0.0, base=0,
                               pattern=[[1, P]], channel_multiplier=-1).then_inc(const_ready, 1)
            pool.wait_ge(minus_half_set, 1)
            rstd(mv1, ve1, rs1, mv1_done, ve1_done, rs1_done, 0)
            ctx_low(0)
            for s in range(3):
                for kind in range(2):
                    proj_low(s, s, kind)
            mask_penalty(0)
            for i in range(2):
                for g in range(HG):
                    slot(i, g)
            with pool.Fori(2, PAIRS - 1) as i:
                for g in range(HG):
                    slot(i, g)
            for i in range(PAIRS - 1, PAIRS + 1):
                for g in range(HG):
                    slot(i, g)

            def gather(t, part):
                pool.wait_ge(gather_ids_in, 16 * (t + 1))
                if not isinstance(t, int) or t > 1:
                    pool.wait_ge(xt_full, t - 1)
                if not isinstance(t, int) or t > 0:
                    pool.wait_ge(gather_done, 32 * t)
                apart(pool)
                for sub in range(2):
                    pool.indirect_dma_start(out=gathered[:, part, sub, :], out_offset=None, in_=normed,
                                            in_offset=bass.IndirectOffsetOnAxis(ap=gather_ids[:, part, sub, 0:1], axis=0)
                                            ).then_inc(gather_done, 16)

            def add(t):
                pool.wait_ge(y_ready, 2 * t + 2)
                if not isinstance(t, int) or t > 0:
                    pool.wait_ge(add_done, 32 * t)
                apart(pool)
                for sub in range(2):
                    pool.indirect_dma_start(out=out_flat, out_offset=bass.IndirectOffsetOnAxis(ap=add_ids[:, sub, 0:1], axis=0),
                                            in_=y_out[:, sub, :], in_offset=None, compute_op=ALU.add).then_inc(add_done, 16)

            ranked = t_use(PAIRS, 3, "ranks")
            scatter(ranked, range(0, 2), first_scattered)
            scatter(ranked, range(2, 6), scattered)
            pool.wait_ge(normed_stored, 16 * PAIRS)
            pool.wait_ge(x2_stored, 16 * PAIRS)
            gather(0, 0)
            scatter(ranked, range(6, 16), scattered)
            gather(1, 1)
            gather(2, 0)
            pool.wait_ge(mat_ready, QUARTERS * EARLY)
            with pool.Fori(0, LATE_MATS) as m:
                gather(2 * m + 3, 1)
                add(2 * m)
                gather(2 * m + 4, 0)
                mat_low(m + EARLY)
                add(2 * m + 1)
            with pool.Fori(LATE_MATS, (TILES - 3) // 2) as two:
                for side in range(2):
                    t = 2 * two + (1 + side)
                    gather(t + 2, 1 - side)
                    add(t - 1)
            for t in range(TILES - 2, TILES + 1):
                if t + 2 < TILES:
                    gather(t + 2, t % 2)
                add(t - 1)


ROUTE_SHIFTED, ROUTE_PICKED = 3, 8
ROUTE_STEPS = 15
W_PIECES = [(m, gg) for gg in range(HG) for m in range(3)] + [(3, 0)]
QUARTERS = 4
TABLE_STEPS = 8


_ORDER = ["x", "ctx_t", "mask", "attn_w", "bq_t", "bk_t", "bv_t", "bo", "router", "expert_w"]


def kernel(x, ctx_1024, mask_BxSxS2_ik1, L0_xattn_WQ_w, L0_xattn_WQ_b, L0_xattn_WK_w, L0_xattn_WK_b,
           L0_xattn_WV_w, L0_xattn_WV_b, L0_xattn_WO_w, L0_xattn_WO_b, L0_ffn_router_w, L0_ffn_up_w, L0_ffn_down_w):
    import numpy as np
    import concourse.bacc as bacc
    from concourse.bass_utils import run_bass_kernel_spmd

    def t(a):
        return np.ascontiguousarray(np.asarray(a).T)

    def by_partition(w):
        w = np.asarray(w)
        return np.ascontiguousarray(w.reshape(-1, P, w.shape[1]).transpose(1, 0, 2)).reshape(P, -1)

    up, down = np.asarray(L0_ffn_up_w), np.asarray(L0_ffn_down_w)
    laid = {
        "x": np.asarray(x),
        "ctx_t": t(np.asarray(ctx_1024).reshape(BATCH * SEQ, D)),
        "mask": np.asarray(mask_BxSxS2_ik1),
        "attn_w": np.stack([by_partition(t(w)) for w in (L0_xattn_WQ_w, L0_xattn_WK_w, L0_xattn_WV_w, L0_xattn_WO_w)]),
        "bq_t": t(np.asarray(L0_xattn_WQ_b).reshape(CHUNKS, P)),
        "bk_t": t(np.asarray(L0_xattn_WK_b).reshape(CHUNKS, P)),
        "bv_t": t(np.asarray(L0_xattn_WV_b).reshape(CHUNKS, P)),
        "bo": np.asarray(L0_xattn_WO_b).reshape(1, D),
        "router": np.asarray(L0_ffn_router_w),
        "expert_w": np.stack([by_partition(w[e]) for e in range(EXPERTS) for w in (up, down)]),
    }
    nc = bacc.Bacc("TRN2", target_bir_lowering=False, num_devices=1)
    arrays, args = {}, []
    for name in _ORDER:
        a = np.ascontiguousarray(laid[name])
        arrays[f"in_{name}"] = a
        args.append(nc.dram_tensor(f"in_{name}", a.shape, mybir.dt.from_np(a.dtype), kind="ExternalInput").ap())
    out = nc.dram_tensor("out", (BATCH, SEQ, D), F32, kind="ExternalOutput").ap()
    xattn_ffn(nc, *args, out)
    r = run_bass_kernel_spmd(nc, [arrays], core_ids=[0])
    return r.results[0]["out"]
```
